# Optimizing a Trainium2 kernel written in Bass

```python
import numpy as np
import jax
import jax.numpy as jnp

def _softmax(x, axis=-1):
    return jax.nn.softmax(x, axis=axis)

def _gelu(x):
    return jax.nn.gelu(x, approximate=True)

def _silu(x):
    return jax.nn.silu(x)

def _sigmoid(x):
    return jax.nn.sigmoid(x)

def _layernorm(x, axis=-1, eps=1e-05):
    m = jnp.mean(x, axis=axis, keepdims=True)
    v = jnp.var(x, axis=axis, keepdims=True)
    return (x - m) / jnp.sqrt(v + eps)

def _scatter_add(tgt, idx, src, axis=0):
    return tgt.at[idx].add(src)

def _segment_sum(src, seg, n):
    return jax.ops.segment_sum(src, seg, n)
kernel_name = 'mk_adaln_attn_ffn_d1_seqx_r8_79da38'

def setup_inputs(seed: int=0):
    np.random.seed(seed)
    _w = jnp.asarray

    def _rec_inputs():
        import jax
        import jax.numpy as jnp
        _rk = jax.random.key(seed)
        x = -0.0005207 + 1.001 * jax.random.normal(jax.random.fold_in(_rk, 1), (8, 128, 512), jnp.float32)
        _lenS = 128 - jax.random.randint(jax.random.fold_in(_rk, 7), (8,), 0, max(1, 128 // 4) + 1, jnp.int32)
        _lenS2 = 128 - jax.random.randint(jax.random.fold_in(_rk, 8), (8,), 0, max(1, 128 // 4) + 1, jnp.int32)
        itok_Bx16_0_63 = jax.random.randint(jax.random.fold_in(_rk, 11), (8, 16), 0, 64, jnp.int32)
        itok_B_207_1644 = jax.random.randint(jax.random.fold_in(_rk, 12), (8,), 207, 1645, jnp.int32)
        itok_B_1_14 = jax.random.randint(jax.random.fold_in(_rk, 13), (8,), 1, 15, jnp.int32)
        return (x, itok_Bx16_0_63, itok_B_207_1644, itok_B_1_14)
    x, itok_Bx16_0_63, itok_B_207_1644, itok_B_1_14 = _rec_inputs()

    def _L0_cond_setup():
        import jax, jax.numpy as jnp
        import numpy as np
        B, S, HID = (4, 128, 512)
        D, HQ, HK = (128, 32, 8)
        PAGES, PSIZE, NPP = (64, 32, 16)
        THETA = 10000.0
        EPS = 1e-06
        SCALE = 1.0 / float(np.sqrt(D))

        def _rmsnorm(t, w):
            var = jnp.mean(t * t, axis=-1, keepdims=True)
            return t * jax.lax.rsqrt(var + EPS) * w

        def _rope(t, pos):
            inv_freq = 1.0 / THETA ** (jnp.arange(0, D, 2, dtype=jnp.float32) / D)
            freqs = pos[..., None].astype(jnp.float32) * inv_freq
            cos = jnp.cos(freqs)[:, :, None, :]
            sin = jnp.sin(freqs)[:, :, None, :]
            t1, t2 = (t[..., :D // 2], t[..., D // 2:])
            return jnp.concatenate([t1 * cos - t2 * sin, t2 * cos + t1 * sin], axis=-1)
        key = jax.random.key(seed)
        ks = jax.random.split(key, 10)
        x = jax.random.normal(ks[0], (B, S, HID), jnp.float32)
        Wq = jax.random.normal(ks[1], (HQ * D, HID), jnp.float32) * 0.02
        Wk = jax.random.normal(ks[2], (HK * D, HID), jnp.float32) * 0.02
        Wv = jax.random.normal(ks[3], (HK * D, HID), jnp.float32) * 0.02
        Wo = jax.random.normal(ks[4], (HID, HQ * D), jnp.float32) * 0.02
        q_norm_w = jax.random.uniform(ks[5], (D,), jnp.float32)
        k_norm_w = jax.random.uniform(ks[6], (D,), jnp.float32)
        k_cache = jax.random.normal(ks[7], (PAGES, PSIZE, HK, D), jnp.float32)
        v_cache = jax.random.normal(ks[8], (PAGES, PSIZE, HK, D), jnp.float32)
        block_table = jnp.arange(B * NPP, dtype=jnp.int32).reshape(B, NPP)
        cache_seqlens = jax.random.randint(ks[9], (B,), 0, 475).astype(jnp.int32)
        return dict(x=x, Wq=Wq, Wk=Wk, Wv=Wv, Wo=Wo, q_norm_w=q_norm_w, k_norm_w=k_norm_w, k_cache=k_cache, v_cache=v_cache, block_table=block_table, cache_seqlens=cache_seqlens)
    _L0_cond_all = _L0_cond_setup()
    _L0_cond_in = {k: v for k, v in _L0_cond_all.items() if k in ('Wq', 'Wk', 'Wv', 'Wo', 'q_norm_w', 'k_norm_w', 'k_cache', 'v_cache')}
    del _L0_cond_all

    def _L0_attn_setup():
        import jax, jax.numpy as jnp
        import numpy as np
        K_FACTOR = 0.5
        key = jax.random.key(seed)
        k1, k2, k3, k4 = jax.random.split(key, 4)
        B, S, H, I = (1, 256, 512, 1376)
        x = jax.random.normal(k1, (B, S, H), dtype=jnp.float32)
        w_gate = jax.random.normal(k2, (I, H), dtype=jnp.float32) * 0.02
        w_up = jax.random.normal(k3, (I, H), dtype=jnp.float32) * 0.02
        w_down = jax.random.normal(k4, (H, I), dtype=jnp.float32) * 0.02
        return {'x': x, 'w_gate': w_gate, 'w_up': w_up, 'w_down': w_down}
    _L0_attn_all = _L0_attn_setup()
    _L0_attn_in = {k: v for k, v in _L0_attn_all.items() if k in ('w_gate', 'w_up', 'w_down')}
    del _L0_attn_all

    def _L0_cond2_setup():
        import jax, jax.numpy as jnp
        import numpy as np
        B, S, D_IN = (8, 256, 512)
        A, D_OUT = (16, 512)
        key = jax.random.key(seed)
        k1, k2, k3 = jax.random.split(key, 3)
        x = jax.random.normal(k1, (B, S, D_IN), dtype=jnp.float32)
        weight = jax.random.normal(k2, (A, D_OUT, D_IN), dtype=jnp.float32) * 0.02
        adapter_ids = jax.random.randint(k3, (B,), 0, A, dtype=jnp.int64)
        return {'x': x, 'weight': weight, 'adapter_ids': adapter_ids}
    _L0_cond2_all = _L0_cond2_setup()
    _L0_cond2_in = {k: v for k, v in _L0_cond2_all.items() if k in ('weight',)}
    del _L0_cond2_all

    def _L0_ffn_setup():
        import jax, jax.numpy as jnp
        import numpy as np
        OUT_FEATURES = 512
        IN_FEATURES = 512

        def _unpack_int4_symmetric(packed, n_values):
            high = packed >> 4 & 15
            low = packed & 15
            interleaved = jnp.stack([high, low], axis=-1).reshape(-1)[:n_values]
            return interleaved.astype(jnp.float32) - 8.0
        key = jax.random.key(seed)
        k1, k2, k3, k4, k5 = jax.random.split(key, 5)
        x = jax.random.normal(k1, (4, 256, IN_FEATURES), dtype=jnp.float32)
        packed_w = jax.random.randint(k2, (OUT_FEATURES * IN_FEATURES // 2,), 0, 32, dtype=jnp.int32)
        packed_b = jax.random.randint(k3, (OUT_FEATURES // 2,), 0, 32, dtype=jnp.int32)
        scale_w = jax.random.uniform(k4, (), dtype=jnp.float32) * 0.01 + 0.0001
        scale_b = jax.random.uniform(k5, (), dtype=jnp.float32) * 0.01 + 0.0001
        return {'x': x, 'packed_w': packed_w, 'packed_b': packed_b, 'scale_w': scale_w, 'scale_b': scale_b}
    _L0_ffn_all = _L0_ffn_setup()
    _L0_ffn_in = {k: v for k, v in _L0_ffn_all.items() if k in ('packed_w', 'packed_b', 'scale_w', 'scale_b')}
    del _L0_ffn_all
    return {'x': x, 'itok_Bx16_0_63': itok_Bx16_0_63, 'itok_B_207_1644': itok_B_207_1644, 'itok_B_1_14': itok_B_1_14, 'L0_cond_Wq': _L0_cond_in['Wq'], 'L0_cond_Wk': _L0_cond_in['Wk'], 'L0_cond_Wv': _L0_cond_in['Wv'], 'L0_cond_Wo': _L0_cond_in['Wo'], 'L0_cond_q_norm_w': _L0_cond_in['q_norm_w'], 'L0_cond_k_norm_w': _L0_cond_in['k_norm_w'], 'L0_cond_k_cache': _L0_cond_in['k_cache'], 'L0_cond_v_cache': _L0_cond_in['v_cache'], 'L0_attn_w_gate': _L0_attn_in['w_gate'], 'L0_attn_w_up': _L0_attn_in['w_up'], 'L0_attn_w_down': _L0_attn_in['w_down'], 'L0_cond2_weight': _L0_cond2_in['weight'], 'L0_ffn_packed_w': _L0_ffn_in['packed_w'], 'L0_ffn_packed_b': _L0_ffn_in['packed_b'], 'L0_ffn_scale_w': _L0_ffn_in['scale_w'], 'L0_ffn_scale_b': _L0_ffn_in['scale_b']}

def reference(x, itok_Bx16_0_63, itok_B_207_1644, itok_B_1_14, L0_cond_Wq, L0_cond_Wk, L0_cond_Wv, L0_cond_Wo, L0_cond_q_norm_w, L0_cond_k_norm_w, L0_cond_k_cache, L0_cond_v_cache, L0_attn_w_gate, L0_attn_w_up, L0_attn_w_down, L0_cond2_weight, L0_ffn_packed_w, L0_ffn_packed_b, L0_ffn_scale_w, L0_ffn_scale_b):
    import jax
    import jax.numpy as jnp

    def _L0_cond_ref(x, Wq, Wk, Wv, Wo, q_norm_w, k_norm_w, k_cache, v_cache, block_table, cache_seqlens):
        import jax, jax.numpy as jnp
        import numpy as np
        B, S, HID = (4, 128, 512)
        D, HQ, HK = (128, 32, 8)
        PAGES, PSIZE, NPP = (64, 32, 16)
        THETA = 10000.0
        EPS = 1e-06
        SCALE = 1.0 / float(np.sqrt(D))

        def _rmsnorm(t, w):
            var = jnp.mean(t * t, axis=-1, keepdims=True)
            return t * jax.lax.rsqrt(var + EPS) * w

        def _rope(t, pos):
            inv_freq = 1.0 / THETA ** (jnp.arange(0, D, 2, dtype=jnp.float32) / D)
            freqs = pos[..., None].astype(jnp.float32) * inv_freq
            cos = jnp.cos(freqs)[:, :, None, :]
            sin = jnp.sin(freqs)[:, :, None, :]
            t1, t2 = (t[..., :D // 2], t[..., D // 2:])
            return jnp.concatenate([t1 * cos - t2 * sin, t2 * cos + t1 * sin], axis=-1)
        bsz, seqlen, _ = x.shape
        q = jnp.einsum('bsd,ed->bse', x, Wq).reshape(bsz, seqlen, HQ, D)
        k = jnp.einsum('bsd,ed->bse', x, Wk).reshape(bsz, seqlen, HK, D)
        v = jnp.einsum('bsd,ed->bse', x, Wv).reshape(bsz, seqlen, HK, D)
        q = _rmsnorm(q, q_norm_w)
        k = _rmsnorm(k, k_norm_w)
        pos = cache_seqlens[:, None] + jnp.arange(seqlen)[None, :]
        q = _rope(q, pos)
        k = _rope(k, pos)
        L = NPP * PSIZE
        kc = k_cache[block_table].reshape(bsz, L, HK, D)
        vc = v_cache[block_table].reshape(bsz, L, HK, D)
        k_all = jnp.concatenate([kc, k], axis=1)
        v_all = jnp.concatenate([vc, v], axis=1)
        valid_c = jnp.arange(L)[None, :] < cache_seqlens[:, None]
        valid = jnp.concatenate([valid_c, jnp.ones((bsz, seqlen), dtype=bool)], axis=1)
        rep = HQ // HK
        k_all = jnp.repeat(k_all, rep, axis=2)
        v_all = jnp.repeat(v_all, rep, axis=2)
        scores = jnp.einsum('bqhd,bkhd->bhqk', q, k_all) * SCALE
        scores = jnp.where(valid[:, None, None, :], scores, -1e+30)
        probs = jax.nn.softmax(scores, axis=-1)
        o = jnp.einsum('bhqk,bkhd->bqhd', probs, v_all)
        o = o.reshape(bsz, seqlen, HQ * D)
        return jnp.einsum('bse,de->bsd', o, Wo)

    def _L0_attn_ref(x, w_gate, w_up, w_down):
        import jax, jax.numpy as jnp
        import numpy as np
        K_FACTOR = 0.5
        s = jax.nn.silu(jnp.einsum('bsh,ih->bsi', x, w_gate))
        B, S, I = s.shape
        k = int(K_FACTOR * I)
        _, idx = jax.lax.top_k(-jnp.abs(s), k)
        flat = s.reshape(B * S, I)
        rows = jnp.arange(B * S)[:, None]
        flat = flat.at[rows, idx.reshape(B * S, k)].set(0.0)
        s = flat.reshape(B, S, I)
        s = s * jnp.einsum('bsh,ih->bsi', x, w_up)
        return jnp.einsum('bsi,hi->bsh', s, w_down)

    def _L0_cond2_ref(x, weight, adapter_ids):
        import jax, jax.numpy as jnp
        import numpy as np
        B, S, D_IN = (8, 256, 512)
        A, D_OUT = (16, 512)
        w = weight[adapter_ids]
        return jnp.einsum('bij,bkj->bik', x, w)

    def _L0_ffn_ref(x, packed_w, packed_b, scale_w, scale_b):
        import jax, jax.numpy as jnp
        import numpy as np
        OUT_FEATURES = 512
        IN_FEATURES = 512

        def _unpack_int4_symmetric(packed, n_values):
            high = packed >> 4 & 15
            low = packed & 15
            interleaved = jnp.stack([high, low], axis=-1).reshape(-1)[:n_values]
            return interleaved.astype(jnp.float32) - 8.0
        qw = _unpack_int4_symmetric(packed_w, OUT_FEATURES * IN_FEATURES)
        W = (scale_w * qw).reshape(OUT_FEATURES, IN_FEATURES)
        qb = _unpack_int4_symmetric(packed_b, OUT_FEATURES)
        b = scale_b * qb
        return jnp.einsum('bsi,oi->bso', x, W) + b
    x = x + _L0_attn_ref(_L0_cond_ref(x, L0_cond_Wq, L0_cond_Wk, L0_cond_Wv, L0_cond_Wo, L0_cond_q_norm_w, L0_cond_k_norm_w, L0_cond_k_cache, L0_cond_v_cache, itok_Bx16_0_63, itok_B_207_1644), L0_attn_w_gate, L0_attn_w_up, L0_attn_w_down)
    x = x + _L0_ffn_ref(_L0_cond2_ref(x, L0_cond2_weight, itok_B_1_14), L0_ffn_packed_w, L0_ffn_packed_b, L0_ffn_scale_w, L0_ffn_scale_b)
    return x

_drawn_inputs = setup_inputs


def setup_inputs(seed=0):
    import zlib

    import numpy as np

    out = dict(_drawn_inputs(seed))
    spreads = {}
    factors = {}
    for name, (base, spread) in spreads.items():
        noise = np.random.default_rng([zlib.crc32(name.encode()), seed]).standard_normal(out[name].shape)
        drawn = base * np.exp(spread * noise) if base else spread * noise
        out[name] = jnp.asarray(drawn.astype(out[name].dtype))
    for name, factor in factors.items():
        out[name] = (out[name] * factor).astype(out[name].dtype)
    return out
```

```python
from contextlib import ExitStack

import concourse.bass as bass
from concourse import mybir

F32 = mybir.dt.float32
F32R = mybir.dt.float32r
BF16 = mybir.dt.bfloat16
I32 = mybir.dt.int32
U32 = mybir.dt.uint32
U16 = mybir.dt.uint16
ALU = mybir.AluOpType
ACT = mybir.ActivationFunctionType

P = 128
B, S, DM = 8, 128, 512
D, HQ, HK = 128, 32, 8
REP = HQ // HK
PAGES, PSIZE, NPP = 64, 32, 16
L = NPP * PSIZE
KEYS = L + S
HALF = KEYS // 2
NK = DM // P
NC = L // P
NJ = KEYS // P
GQ = REP * D
GW = GQ + 2 * D
STEPS = HK * B
EPS = 1e-6
SOFTMAX_SCALE = float(D) ** -0.5
NEG = -1e30
FI = 1376
DROP = FI // 2
FCH = [(i * P, min(P, FI - i * P)) for i in range((FI + P - 1) // P)]
BANKS3 = [(0, 512), (512, 512), (1024, FI - 1024)]
ROUND = 1.5 * 2.0 ** 23
TWO_PI = (6.28125, 0.0019350051879882812, 3.0199157663446503e-07)
PI = 3.141592653589793
UNPACKED = 7
LINKS = 1 + (1 + 3 * 15) + 4 + (1 + 3 * 16) + 4 + 5
SINES_READY = 3 + 2 * 7
MASK_READY = SINES_READY + 1
PI_IN = 3.1415925
C_ID, C_INV, C_PART, C_LANE, C_KEY, C_ALL = 0, 128, 192, 193, 194, 194 + L


def live(s):
    return not isinstance(s, int) or 0 <= s < STEPS


def wait(eng, sem, n):
    if not isinstance(n, int) or n > 0:
        eng.wait_ge(sem, n)


def at_most(n):
    return min(n, STEPS) if isinstance(n, int) else n


def product3(pe, out, left, right, start, stop):
    pe.matmul(out, left[0], right[0], start=start, stop=False)
    pe.matmul(out, left[0], right[1], start=False, stop=False)
    return pe.matmul(out, left[1], right[0], start=False, stop=stop)


def adaln_attn_ffn(nc, xt, xn, lens, pages, ids, wqkv, wo, qw, kw, kc, vc, wg, wu, wd, wa, pw, pb, scales,
                   consts, out):
    with ExitStack() as whole:
        def semaphore(name):
            return whole.enter_context(nc.semaphore(name))

        def tensors(stack):
            return lambda name, shape, dt=F32: stack.enter_context(nc.sbuf_tensor(name, shape, dt))

        sb = tensors(whole)
        acc = sb("acc", [P, B, DM])
        cst = sb("cst", [P, C_KEY])
        ident = cst[:, C_ID:C_ID + P]

        const_in = semaphore("const_in")
        xt_in = semaphore("xt_in")
        w_in = semaphore("w_in")
        wo_in = semaphore("wo_in")
        k_in = [semaphore(f"k_in{n}") for n in range(2)]
        v_in = [semaphore(f"v_in{n}") for n in range(4)]
        xt_hi_done = semaphore("xt_hi_done")
        w_hi_done = semaphore("w_hi_done")
        w_lo_done = semaphore("w_lo_done")
        wo_hi_done = semaphore("wo_hi_done")
        wo_lo_done = semaphore("wo_lo_done")
        setup_dve = semaphore("setup_dve")
        setup_pool = semaphore("setup_pool")
        sines_done = semaphore("sines_done")
        held = semaphore("held")
        idx_ready = semaphore("idx_ready")
        q_projected = semaphore("q_projected")
        kv_projected = semaphore("kv_projected")
        q_copied = semaphore("q_copied")
        kv_copied = semaphore("kv_copied")
        squares_done = semaphore("squares_done")
        eps_added = semaphore("eps_added")
        rstd_done = semaphore("rstd_done")
        rope_parts = semaphore("rope_parts")
        rope_done = semaphore("rope_done")
        kc_turned = semaphore("kc_turned")
        q_turned = semaphore("q_turned")
        kn_turned = semaphore("kn_turned")
        kc_hi_done = semaphore("kc_hi_done")
        q_hi_done = semaphore("q_hi_done")
        kn_hi_done = semaphore("kn_hi_done")
        kc_lo_done = semaphore("kc_lo_done")
        q_lo_done = semaphore("q_lo_done")
        kn_lo_done = semaphore("kn_lo_done")
        scored = [semaphore(f"scored{h}") for h in range(REP)]
        max_done = [semaphore(f"max_done{h}") for h in range(REP)]
        shift_done = [semaphore(f"shift_done{h}") for h in range(REP)]
        exp_done = [semaphore(f"exp_done{h}") for h in range(REP)]
        recip_done = semaphore("recip_done")
        probs_done = semaphore("probs_done")
        p_turned = [semaphore(f"p_turned{j}") for j in range(NJ)]
        p_copied = [semaphore(f"p_copied{j}") for j in range(NJ)]
        valued = semaphore("valued")
        o_hi_done = semaphore("o_hi_done")
        o_lo_done = semaphore("o_lo_done")
        o_projected = semaphore("o_projected")
        acc_added = semaphore("acc_added")

        with ExitStack() as phase1:
            sb = tensors(phase1)
            ps = lambda name, n: phase1.enter_context(nc.psum_tensor(name, [P, n], F32))
            proj_ps = ps("proj_ps", 512)
            turn_ps = [ps("turn_ps0", 512), ps("turn_ps1", 512)]
            score_ps = [ps("score_ps0", 1024), ps("score_ps1", 1024)]
            value_ps = ps("value_ps", 512)

            xt_hi = sb("xt_hi", [P, B, NK, S], F32R)
            xt_lo = sb("xt_lo", [P, B, NK, S], F32R)
            w_raw = sb("w_raw", [P, NK, GW])
            w_hi = sb("w_hi", [P, NK, GW], F32R)
            w_lo = sb("w_lo", [P, NK, GW], F32R)
            wo_raw = sb("wo_raw", [P, REP, DM])
            wo_hi = sb("wo_hi", [P, REP, DM], F32R)
            wo_lo = sb("wo_lo", [P, REP, DM], F32R)
            mask = sb("mask", [P, B, KEYS], BF16)
            qa = sb("qa", [P, B, D])
            qb = sb("qb", [P, B, D])
            ka = sb("ka", [P, B, D])
            kb = sb("kb", [P, B, D])
            kg = sb("kg", [P, 2, NC, D])
            vt = sb("vt", [P, 4, NJ, D])
            qk = sb("qk", [P, REP + 1, D])
            rot = sb("rot", [P, REP + 1, D])
            rot_b = sb("rot_b", [P, REP + 1, D])
            kt_hi = sb("kt_hi", [P, KEYS], F32R)
            kt_lo = sb("kt_lo", [P, KEYS], F32R)
            qt_hi = sb("qt_hi", [P, GQ], F32R)
            qt_lo = sb("qt_lo", [P, GQ], F32R)
            probs = sb("probs", [P, 2, REP, KEYS])
            pt = sb("pt", [P, NJ, GQ])
            ot_hi = sb("ot_hi", [P, GQ], F32R)
            ot_lo = sb("ot_lo", [P, GQ], F32R)
            ss = sb("ss", [P, REP + 1])
            ss_eps = sb("ss_eps", [P, REP + 1])
            power = sb("power", [P, REP + 1])
            eps = sb("eps", [P, REP + 1])
            rstd = sb("rstd", [P, 2, REP + 1])
            row_max = sb("row_max", [P, REP])
            shift = sb("shift", [P, REP])
            sums = sb("sums", [P, REP])
            recips = sb("recips", [P, REP])
            lens_i = sb("lens_i", [P, B], I32)
            pages_i = sb("pages_i", [P, B * NC], I32)
            idx = sb("idx", [P, B * NC], U32)
            x_raw = probs[:, :, :, :].rearrange("p a h k -> p (a h k)")[:, 0:B * NK * S]
            angle, turns, sines, cosines = (pt[:, i, :].rearrange("p (b f) -> p b f", b=B) for i in range(4))
            squared = sb("squared", [P, REP + 1, D])
            pos = sb("pos", [P, B])
            lens_f = sb("lens_f", [P, B])
            qkw = rot_b[:, 0:2, :]
            key_no = rot[:, 0:NC, :].rearrange("p c d -> p (c d)")

            with nc.Block() as block:
                @block.sync
                def _(sp):
                    sp.dma_start(cst[:, :], consts[:, 0:C_KEY]).then_inc(const_in, 16)
                    sp.dma_start(key_no, consts[:, C_KEY:C_ALL]).then_inc(const_in, 16)
                    sp.dma_start(lens_i[:, :], lens).then_inc(const_in, 16)
                    sp.dma_start(pages_i[:, :], pages).then_inc(const_in, 16)
                    sp.dma_start(qkw[:, 0, :], qw).then_inc(const_in, 16)
                    sp.dma_start(qkw[:, 1, :], kw).then_inc(const_in, 16)
                    sp.dma_start(x_raw, xt).then_inc(xt_in, 16)
                    sp.dma_start(w_raw[:, :, :], wqkv[0]).then_inc(w_in, 16)
                    sp.dma_start(wo_raw[:, :, :], wo[0]).then_inc(wo_in, 16)
                    with sp.Fori(1, HK) as g:
                        sp.wait_ge(w_hi_done, g)
                        sp.wait_ge(w_lo_done, g)
                        sp.dma_start(w_raw[:, :, :], wqkv[bass.ds(g, 1)].rearrange("o p k n -> p (o k) n"))\
                            .then_inc(w_in, 16)
                        sp.wait_ge(wo_hi_done, g)
                        sp.wait_ge(wo_lo_done, g)
                        sp.dma_start(wo_raw[:, :, :], wo[bass.ds(g, 1)].rearrange("o p h n -> p (o h) n"))\
                            .then_inc(wo_in, 16)

                @block.gpsimd
                def _(pool):
                    pool.memset(power[:, :], -0.5).then_inc(setup_pool, 1)
                    pool.memset(eps[:, :], D * EPS).then_inc(setup_pool, 1)
                    pool.wait_ge(const_in, 6 * 16)
                    pool.tensor_scalar(idx[:, :], pages_i[:, :], float(PSIZE * HK), cst[:, C_LANE:C_LANE + 1],
                                       ALU.mult, ALU.add).then_inc(idx_ready, 1)

                    def hold(waits):
                        for sem, n in waits:
                            wait(pool, sem, n)
                        pool.sem_inc(held, 1)

                    def gather(s, b, g):
                        if b == 0 and not (isinstance(g, int) and g == 0):
                            waits = [(place, s // 2 * (NC * 16)) for place in k_in]
                            waits += [(place, s // 4 * (NC * 16)) for place in v_in]
                            hold(waits)
                            pool.tensor_scalar(idx[:, :], idx[:, :], 1.0, None, ALU.add).then_inc(idx_ready, 1)
                        hold([(idx_ready, g + 1), (kc_turned, s - 1)])
                        for c in range(NC):
                            pool.indirect_dma_start(
                                kg[:, b % 2, c, :], None, kc,
                                bass.IndirectOffsetOnAxis(ap=idx[:, b * NC + c:b * NC + c + 1], axis=0))\
                                .then_inc(k_in[b % 2], 16)
                        for c in range(NC):
                            pool.indirect_dma_start(
                                vt[:, b % 4, c, :], None, vc,
                                bass.IndirectOffsetOnAxis(ap=idx[:, b * NC + c:b * NC + c + 1], axis=0))\
                                .then_inc(v_in[b % 4], 16)

                    def norms(s, b):
                        wait(pool, squares_done, s + 1)
                        pool.tensor_tensor(ss_eps[:, :], ss[:, :], eps[:, :], ALU.add).then_inc(eps_added, 1)
                        wait(pool, eps_added, s + 1)
                        wait(pool, exp_done[REP - 1], s - 1)
                        pool.tensor_tensor(rstd[:, b % 2, :], ss_eps[:, :], power[:, :], ALU.pow)\
                            .then_inc(rstd_done, 1)

                    def step(s, b, g):
                        ahead, b3 = s + 3, (b + 3) % B
                        if live(ahead):
                            gather(ahead, b3, g + (b + 3) // B)
                            norms(ahead, b3)

                    pool.wait_ge(setup_pool, 2)
                    for s in range(-3, 0):
                        step(s, s % B, -1)
                    with pool.Fori(0, STEPS - B, B) as s0:
                        g = pool.snap(s0 // B)
                        for b in range(B):
                            step(s0 + b, b, g)
                    for b in range(B):
                        step(STEPS - B + b, b, HK - 1)

                @block.tensor
                def _(pe):
                    def pair(hi, lo, at):
                        return hi[at], lo[at]

                    def project_q(s, b, g):
                        if b == 0:
                            wait(pe, w_hi_done, g + 1)
                            wait(pe, w_lo_done, g + 1)
                        wait(pe, kv_copied, s)
                        wait(pe, acc_added, s - 2)
                        for k in range(NK):
                            last = product3(pe, proj_ps[:, :], (xt_hi[:, b, k, :], xt_lo[:, b, k, :]),
                                            (w_hi[:, k, 0:GQ], w_lo[:, k, 0:GQ]), k == 0, k == NK - 1)
                        last.then_inc(q_projected, 1)

                    def project_kv(s, b):
                        wait(pe, q_copied, s + 1)
                        for k in range(NK):
                            last = product3(pe, proj_ps[:, 0:2 * D], (xt_hi[:, b, k, :], xt_lo[:, b, k, :]),
                                            (w_hi[:, k, GQ:GW], w_lo[:, k, GQ:GW]), k == 0, k == NK - 1)
                        last.then_inc(kv_projected, 1)

                    def turn_cached_k(s, b):
                        wait(pe, p_copied[3], s - 1)
                        wait(pe, k_in[b % 2], (s // 2 + 1) * (NC * 16))
                        for c in range(NC):
                            last = pe.transpose(turn_ps[0][:, c * P:(c + 1) * P], kg[:, b % 2, c, :], ident)
                        last.then_inc(kc_turned, 1)

                    def turn_q(s):
                        wait(pe, p_copied[4], s - 1)
                        wait(pe, rope_done, s + 1)
                        for h in range(REP):
                            last = pe.transpose(turn_ps[1][:, h * P:(h + 1) * P], rot[:, h, :], ident)
                        last.then_inc(q_turned, 1)

                    def turn_new_k(s):
                        wait(pe, kc_lo_done, s + 1)
                        pe.transpose(turn_ps[0][:, 0:P], rot[:, REP, :], ident).then_inc(kn_turned, 1)

                    def scores(s):
                        wait(pe, q_lo_done, s + 1)
                        wait(pe, kn_lo_done, s + 1)
                        for h in range(REP):
                            wait(pe, max_done[(h + 2) % REP], s if h < 2 else s + 1)
                            for a in range(2):
                                last = product3(pe, score_ps[h % 2][:, 512 * a:512 * a + HALF],
                                                (qt_hi[:, h * P:(h + 1) * P], qt_lo[:, h * P:(h + 1) * P]),
                                                (kt_hi[:, a * HALF:(a + 1) * HALF], kt_lo[:, a * HALF:(a + 1) * HALF]),
                                                True, True)
                            last.then_inc(scored[h], 1)

                    def turn_probs(s, b, j):
                        if j == 0:
                            wait(pe, probs_done, s + 1)
                            wait(pe, q_lo_done, at_most(s + 2))
                        elif j == 1:
                            wait(pe, kn_lo_done, at_most(s + 2))
                        else:
                            wait(pe, p_copied[j - 2], s + 1)
                        for h in range(REP):
                            last = pe.transpose(turn_ps[1 - j % 2][:, h * P:(h + 1) * P],
                                                probs[:, b % 2, h, j * P:(j + 1) * P], ident)
                        last.then_inc(p_turned[j], 1)

                    def values(s, b, j):
                        if j == 0:
                            wait(pe, v_in[b % 4], (s // 4 + 1) * (NC * 16))
                            wait(pe, kv_copied, s + 1)
                        wait(pe, p_copied[j], s + 1)
                        last = pe.matmul(value_ps[:, :], vt[:, b % 4, j, :], pt[:, j, :],
                                         start=(j == 0), stop=(j == NJ - 1))
                        if j == NJ - 1:
                            last.then_inc(valued, 1)

                    def project_o(s, b, g):
                        if b == 0:
                            wait(pe, wo_hi_done, g + 1)
                            wait(pe, wo_lo_done, g + 1)
                        wait(pe, kv_copied, at_most(s + 4))
                        wait(pe, o_lo_done, s + 1)
                        for h in range(REP):
                            at = slice(h * P, (h + 1) * P)
                            last = product3(pe, proj_ps[:, :], (ot_hi[:, at], ot_lo[:, at]),
                                            (wo_hi[:, h, :], wo_lo[:, h, :]), h == 0, h == REP - 1)
                        last.then_inc(o_projected, 1)

                    def step(s, b, g):
                        b2, b3 = (b + 2) % B, (b + 3) % B
                        if live(s):
                            turn_probs(s, b, 0)
                            turn_probs(s, b, 1)
                        if live(s + 3):
                            project_q(s + 3, b3, g + (b + 3) // B)
                        if live(s):
                            for j in range(NJ):
                                values(s, b, j)
                                if j + 2 < NJ:
                                    turn_probs(s, b, j + 2)
                        if live(s + 2):
                            turn_cached_k(s + 2, b2)
                            turn_q(s + 2)
                        if live(s + 3):
                            project_kv(s + 3, b3)
                        if live(s + 2):
                            turn_new_k(s + 2)
                        if live(s):
                            project_o(s, b, g)
                        if live(s + 2):
                            scores(s + 2)

                    pe.wait_ge(const_in, 6 * 16)
                    pe.wait_ge(xt_hi_done, 1)
                    pe.wait_ge(setup_dve, MASK_READY + 2)
                    for s in range(-3, 0):
                        step(s, s % B, -1)
                    with pe.Fori(0, STEPS - B, B) as s0:
                        g = pe.snap(s0 // B)
                        for b in range(B):
                            step(s0 + b, b, g)
                    for b in range(B):
                        step(STEPS - B + b, b, HK - 1)

                @block.scalar
                def _(act):
                    def split_w(g):
                        wait(act, w_in, (g + 1) * 16)
                        wait(act, kv_projected, g * B)
                        act.activation(w_hi[:, :, :], w_raw[:, :, :], ACT.Copy).then_inc(w_hi_done, 1)

                    def split_wo(g):
                        wait(act, wo_in, (g + 1) * 16)
                        wait(act, o_projected, g * B)
                        act.activation(wo_hi[:, :, :], wo_raw[:, :, :], ACT.Copy).then_inc(wo_hi_done, 1)

                    def copy_q(s):
                        wait(act, q_projected, s + 1)
                        wait(act, rope_done, s)
                        act.activation(qk[:, 0:REP, :].rearrange("p h d -> p (h d)"), proj_ps[:, :], ACT.Copy)\
                            .then_inc(q_copied, 1)

                    def copy_kv(s, b):
                        wait(act, kv_projected, s + 1)
                        act.activation(qk[:, REP, :], proj_ps[:, 0:D], ACT.Copy)
                        act.activation(vt[:, b % 4, NC, :], proj_ps[:, D:2 * D], ACT.Copy).then_inc(kv_copied, 1)

                    def squares(s):
                        wait(act, eps_added, s)
                        wait(act, q_copied, s + 1)
                        wait(act, kv_copied, s + 1)
                        for h in range(REP + 1):
                            last = act.activation(squared[:, h, :], qk[:, h, :], ACT.Square, accum_out=ss[:, h:h + 1])
                        last.then_inc(squares_done, 1)

                    def split_cached_k(s):
                        wait(act, kc_turned, s + 1)
                        act.activation(kt_hi[:, 0:L], turn_ps[0][:, :], ACT.Copy).then_inc(kc_hi_done, 1)

                    def split_q(s):
                        wait(act, q_turned, s + 1)
                        act.activation(qt_hi[:, :], turn_ps[1][:, :], ACT.Copy).then_inc(q_hi_done, 1)

                    def split_new_k(s):
                        wait(act, kn_turned, s + 1)
                        act.activation(kt_hi[:, L:KEYS], turn_ps[0][:, 0:P], ACT.Copy).then_inc(kn_hi_done, 1)

                    def exps(s, b):
                        wait(act, recip_done, s)
                        for h in range(REP):
                            wait(act, shift_done[h], s + 1)
                            row = probs[:, b % 2, h, :]
                            act.activation(row, row, ACT.Exp, bias=shift[:, h:h + 1],
                                           scale=rstd[:, b % 2, h:h + 1], accum_out=sums[:, h:h + 1])\
                                .then_inc(exp_done[h], 1)

                    def copy_probs(s, j):
                        wait(act, p_turned[j], s + 1)
                        act.activation(pt[:, j, :], turn_ps[1][:, :], ACT.Copy).then_inc(p_copied[j], 1)

                    def split_o(s):
                        wait(act, valued, s + 1)
                        act.activation(ot_hi[:, :], value_ps[:, :], ACT.Copy).then_inc(o_hi_done, 1)

                    def step(s, b, g):
                        b2, b3 = (b + 2) % B, (b + 3) % B
                        if live(s):
                            copy_probs(s, 0)
                        if live(s + 3):
                            copy_q(s + 3)
                        if live(s):
                            copy_probs(s, 2)
                            copy_probs(s, 4)
                        if live(s + 2):
                            split_cached_k(s + 2)
                            split_q(s + 2)
                        if live(s):
                            split_o(s)
                        if live(s + 3):
                            copy_kv(s + 3, b3)
                        if live(s + 2):
                            split_new_k(s + 2)
                        if live(s + 3):
                            squares(s + 3)
                        if live(s + 2):
                            exps(s + 2, b2)
                        if b == B - 4 and live(s + 4):
                            split_w(g + 1)
                        if b == B - 1 and live(s + 1):
                            split_wo(g + 1)

                    act.wait_ge(setup_dve, SINES_READY)
                    act.activation(sines, sines, ACT.Sin)
                    act.activation(cosines, cosines, ACT.Sin).then_inc(sines_done, 1)
                    act.wait_ge(xt_in, 16)
                    act.activation(xt_hi[:, :, :, :].rearrange("p b k t -> p (b k t)"), x_raw, ACT.Copy)\
                        .then_inc(xt_hi_done, 1)
                    split_w(0)
                    for s in range(-3, 0):
                        step(s, s % B, -1)
                    with act.Fori(0, STEPS - B, B) as s0:
                        g = act.snap(s0 // B)
                        for b in range(B):
                            step(s0 + b, b, g)
                    for b in range(B):
                        step(STEPS - B + b, b, HK - 1)

                @block.vector
                def _(dve):
                    links = [0]

                    def link(instruction):
                        links[0] += 1
                        instruction.then_inc(setup_dve, 1)
                        dve.wait_ge(setup_dve, links[0])

                    def reduced(to, quarter):
                        link(dve.tensor_scalar(turns, angle, 1 / (2 * PI), 0.25 * quarter, ALU.mult, ALU.add))
                        link(dve.tensor_scalar(turns, turns, ROUND, ROUND, ALU.add, ALU.subtract))
                        link(dve.scalar_tensor_tensor(to, turns, -TWO_PI[0], angle, ALU.mult, ALU.add))
                        link(dve.scalar_tensor_tensor(to, turns, -TWO_PI[1], to, ALU.mult, ALU.add))
                        link(dve.scalar_tensor_tensor(to, turns, -TWO_PI[2], to, ALU.mult, ALU.add))
                        link(dve.tensor_scalar(to, to, 0.5 * PI * quarter, PI_IN, ALU.add, ALU.min))
                        link(dve.tensor_scalar(to, to, -PI_IN, None, ALU.max))

                    def split_w(g):
                        wait(dve, w_hi_done, g + 1)
                        dve.tensor_tensor(w_lo[:, :, :], w_raw[:, :, :], w_hi[:, :, :].bitcast(F32), ALU.subtract)\
                            .then_inc(w_lo_done, 1)

                    def split_wo(g):
                        wait(dve, wo_hi_done, g + 1)
                        dve.tensor_tensor(wo_lo[:, :, :], wo_raw[:, :, :], wo_hi[:, :, :].bitcast(F32), ALU.subtract)\
                            .then_inc(wo_lo_done, 1)

                    def over_heads(table):
                        return table.unsqueeze(1).broadcast_to((P, REP, table.shape[-1]))

                    def rotate(s, b):
                        wait(dve, kv_copied, s + 1)
                        wait(dve, q_turned, s)
                        wait(dve, kn_turned, s)
                        q, k, lo, hi = qk[:, 0:REP, :], qk[:, REP, :], slice(0, D // 2), slice(D // 2, D)
                        dve.tensor_tensor(rot[:, 0:REP, :], q, over_heads(qa[:, b, :]), ALU.mult)
                        dve.tensor_tensor(rot_b[:, 0:REP, lo], q[:, :, hi], over_heads(qb[:, b, lo]), ALU.mult)
                        dve.tensor_tensor(rot_b[:, 0:REP, hi], q[:, :, lo], over_heads(qb[:, b, hi]), ALU.mult)
                        wait(dve, rstd_done, s + 1)
                        norm = rstd[:, b % 2, REP:REP + 1]
                        dve.scalar_tensor_tensor(rot[:, REP, :], k, norm, ka[:, b, :], ALU.mult, ALU.mult)
                        dve.scalar_tensor_tensor(rot_b[:, REP, lo], k[:, hi], norm, kb[:, b, lo], ALU.mult, ALU.mult)
                        dve.scalar_tensor_tensor(rot_b[:, REP, hi], k[:, lo], norm, kb[:, b, hi], ALU.mult, ALU.mult)\
                            .then_inc(rope_parts, 1)
                        wait(dve, rope_parts, s + 1)
                        dve.tensor_tensor(rot[:, :, :], rot[:, :, :], rot_b[:, :, :], ALU.add).then_inc(rope_done, 1)

                    def split_cached_k(s):
                        wait(dve, kc_hi_done, s + 1)
                        dve.tensor_tensor(kt_lo[:, 0:L], turn_ps[0][:, :], kt_hi[:, 0:L].bitcast(F32), ALU.subtract)\
                            .then_inc(kc_lo_done, 1)

                    def split_q(s):
                        wait(dve, q_hi_done, s + 1)
                        dve.tensor_tensor(qt_lo[:, :], turn_ps[1][:, :], qt_hi[:, :].bitcast(F32), ALU.subtract)\
                            .then_inc(q_lo_done, 1)

                    def split_new_k(s):
                        wait(dve, kn_hi_done, s + 1)
                        dve.tensor_tensor(kt_lo[:, L:KEYS], turn_ps[0][:, 0:P], kt_hi[:, L:KEYS].bitcast(F32),
                                          ALU.subtract).then_inc(kn_lo_done, 1)

                    def maxima(s, b):
                        for h in range(REP):
                            dve.wait_ge(setup_dve, MASK_READY)
                            if h == 0:
                                wait(dve, p_turned[NJ - 1], s - 1)
                            wait(dve, scored[h], s + 1)
                            dve.tensor_tensor_reduce(
                                probs[:, b % 2, h, :].rearrange("p (a k) -> p a k", a=2),
                                score_ps[h % 2][:, :].rearrange("p (a k) -> p a k", a=2)[:, :, 0:HALF],
                                mask[:, b, :].rearrange("p (a k) -> p a k", a=2),
                                1.0, -3e38, ALU.add, ALU.max, row_max[:, h:h + 1]).then_inc(max_done[h], 1)
                            wait(dve, max_done[h], s + 1)
                            dve.scalar_tensor_tensor(shift[:, h:h + 1], row_max[:, h:h + 1], -1.0,
                                                     rstd[:, b % 2, h:h + 1], ALU.mult, ALU.mult)\
                                .then_inc(shift_done[h], 1)

                    def normalise(s, b):
                        wait(dve, exp_done[REP - 1], s + 1)
                        dve.reciprocal(recips[:, :], sums[:, :]).then_inc(recip_done, 1)
                        wait(dve, recip_done, s + 1)
                        for h in range(REP):
                            row = probs[:, b % 2, h, :]
                            last = dve.tensor_scalar(row, row, recips[:, h:h + 1], None, ALU.mult)
                        last.then_inc(probs_done, 1)

                    def copy_probs(s, j):
                        wait(dve, p_turned[j], s + 1)
                        dve.tensor_copy(pt[:, j, :], turn_ps[0][:, :]).then_inc(p_copied[j], 1)

                    def split_o(s):
                        wait(dve, o_hi_done, s + 1)
                        dve.tensor_tensor(ot_lo[:, :], value_ps[:, :], ot_hi[:, :].bitcast(F32), ALU.subtract)\
                            .then_inc(o_lo_done, 1)

                    def add_up(s, b):
                        wait(dve, o_projected, s + 1)
                        dve.tensor_tensor(acc[:, b, :], acc[:, b, :], proj_ps[:, :], ALU.add).then_inc(acc_added, 1)

                    def step(s, b, g):
                        b1, b2 = (b + 1) % B, (b + 2) % B
                        if live(s):
                            copy_probs(s, 1)
                        if live(s + 2):
                            rotate(s + 2, b2)
                        if live(s):
                            copy_probs(s, 3)
                        if live(s + 1):
                            normalise(s + 1, b1)
                        if live(s + 2):
                            split_cached_k(s + 2)
                            split_q(s + 2)
                        if live(s):
                            split_o(s)
                        if live(s + 2):
                            split_new_k(s + 2)
                        if live(s):
                            add_up(s, b)
                        if live(s + 2):
                            maxima(s + 2, b2)
                        if b == B - 4 and live(s + 4):
                            split_w(g + 1)
                        if b == B - 1 and live(s + 1):
                            split_wo(g + 1)

                    dve.memset(mask[:, :, L:KEYS], 0.0)
                    dve.memset(acc[:, :, :], 0.0).then_inc(acc_added, 1)
                    dve.wait_ge(const_in, 6 * 16)
                    link(dve.tensor_copy(lens_f[:, :], lens_i[:, :]))
                    link(dve.tensor_scalar(pos[:, :], lens_f[:, :], cst[:, C_PART:C_PART + 1], None, ALU.add))
                    shape = (P, B, D // 2)
                    link(dve.tensor_tensor(angle, pos[:, :].unsqueeze(2).broadcast_to(shape),
                                           cst[:, C_INV:C_INV + D // 2].unsqueeze(1).broadcast_to(shape), ALU.mult))
                    reduced(sines, 0)
                    reduced(cosines, 1)
                    assert links[0] == SINES_READY
                    for b in range(B):
                        last = dve.tensor_scalar(mask[:, b, 0:L], key_no, lens_f[:, b:b + 1], NEG, ALU.is_ge,
                                                 ALU.mult)
                    link(last)
                    dve.wait_ge(sines_done, 1)
                    lo, hi = slice(0, D // 2), slice(D // 2, D)
                    for n, (ta, tb, factor) in enumerate(((qa, qb, 1.0), (ka, kb, float(D) ** 0.5))):
                        w_of = lambda half: qkw[:, n, half].unsqueeze(1).broadcast_to(shape)
                        dve.scalar_tensor_tensor(ta[:, :, lo], cosines, factor, w_of(lo), ALU.mult, ALU.mult)
                        dve.scalar_tensor_tensor(ta[:, :, hi], cosines, factor, w_of(hi), ALU.mult, ALU.mult)
                        dve.scalar_tensor_tensor(tb[:, :, lo], sines, -factor, w_of(hi), ALU.mult, ALU.mult)
                        last = dve.scalar_tensor_tensor(tb[:, :, hi], sines, factor, w_of(lo), ALU.mult, ALU.mult)
                    link(last)
                    dve.wait_ge(xt_hi_done, 1)
                    link(dve.tensor_tensor(xt_lo[:, :, :, :].rearrange("p b k t -> p (b k t)"), x_raw,
                                      xt_hi[:, :, :, :].rearrange("p b k t -> p (b k t)").bitcast(F32),
                                      ALU.subtract))
                    split_w(0)
                    for s in range(-3, 0):
                        step(s, s % B, -1)
                    with dve.Fori(0, STEPS - B, B) as s0:
                        g = dve.snap(s0 // B)
                        for b in range(B):
                            step(s0 + b, b, g)
                    for b in range(B):
                        step(STEPS - B + b, b, HK - 1)

        small_in = semaphore("small_in")
        w2_in = [semaphore(f"w2_in{n}") for n in range(2)]
        wd_in = semaphore("wd_in")
        wa_in = semaphore("wa_in")
        xn_in = semaphore("xn_in")
        out_done = semaphore("out_done")
        w2_hi_done = semaphore("w2_hi_done")
        w2_lo_done = semaphore("w2_lo_done")
        unpacked = semaphore("unpacked")
        c_copied = semaphore("c_copied")
        c_turned = semaphore("c_turned")
        ct_copied = semaphore("ct_copied")
        ct_hi_done = semaphore("ct_hi_done")
        ct_lo_done = semaphore("ct_lo_done")
        gated = semaphore("gated")
        upped = semaphore("upped")
        silu_done = semaphore("silu_done")
        abs_done = semaphore("abs_done")
        search = semaphore("search")
        h_done = semaphore("h_done")
        h_turned = [semaphore(f"h_turned{n}") for n in range(3)]
        h_copied = [semaphore(f"h_copied{n}") for n in range(3)]
        downed = semaphore("downed")
        down_copied = semaphore("down_copied")
        x1_done = semaphore("x1_done")
        x1_turned = semaphore("x1_turned")
        x1_copied = semaphore("x1_copied")
        adapted = semaphore("adapted")
        y_copied = semaphore("y_copied")
        y_turned = semaphore("y_turned")
        yt_copied = semaphore("yt_copied")
        yt_hi_done = semaphore("yt_hi_done")
        yt_lo_done = semaphore("yt_lo_done")
        int4_done = semaphore("int4_done")
        int4_scaled = semaphore("int4_scaled")
        x1b_done = semaphore("x1b_done")
        res_done = semaphore("res_done")

        with ExitStack() as phase2:
            sb = tensors(phase2)
            ps = lambda name, n: phase2.enter_context(nc.psum_tensor(name, [P, n], F32))
            gate_ps, up_ps = ps("gate_ps", 1536), ps("up_ps", 1536)
            turn2_ps, out_ps = ps("turn2_ps", 512), ps("out_ps", 512)
            NF = len(FCH)
            wg_hi, wg_lo = sb("wg_hi", [P, NK, FI], F32R), sb("wg_lo", [P, NK, FI], F32R)
            wu_hi, wu_lo = sb("wu_hi", [P, NK, FI], F32R), sb("wu_lo", [P, NK, FI], F32R)
            wd_sb = sb("wd_sb", [P, NF, DM])
            wf = sb("wf", [P, 2, 2, DM], F32R)
            pb_sb = sb("pb_sb", [P, DM // 2], I32)
            bias = sb("bias", [P, DM])
            scl = sb("scl", [P, 2])
            ids_sb = sb("ids_sb", [1, B], I32)
            wa_sb = sb("wa_sb", [P, NK, DM])
            s_sb, m_sb, h_sb = (sb(n, [P, FI]) for n in ("s_sb", "m_sb", "h_sb"))
            key, key2, junk = (sb(n, [P, FI], U16) for n in ("key", "key2", "junk"))
            c_sb = sb("c_sb", [P, DM])
            ct = sb("ct", [P, DM])
            ct_hi, ct_lo = sb("ct_hi", [P, DM], F32R), sb("ct_lo", [P, DM], F32R)
            ht = sb("ht", [P, NF, S])
            xn_sb, dn, x1, x1t, x1b = (sb(n, [P, DM]) for n in ("xn_sb", "dn", "x1", "x1t", "x1b"))
            y, yt, fo = (sb(n, [P, DM]) for n in ("y", "yt", "fo"))
            yt_hi, yt_lo = sb("yt_hi", [P, DM], F32R), sb("yt_lo", [P, DM], F32R)
            tried = sb("tried", [P, 1])
            count = sb("count", [P, 1])
            taken = sb("taken", [P, 1])
            high, low = sb("high", [P, 1]), sb("low", [P, 1])
            room = sb("room", [P, 1])
            edge = sb("edge", [P, 2], U16)
            HT_JOBS = [FCH[0:4], FCH[4:8], FCH[8:]]
            pw_sb = ht[:, 0:2 * NK, :].rearrange("p (a k) t -> p a (k t)", a=2).bitcast(I32)
            nibble = h_sb[:, 0:2 * DM].rearrange("p (a n) -> p a n", a=2).bitcast(I32)
            bias_i = dn[:, :].rearrange("p (n t) -> p n t", t=2).bitcast(I32)
            stage = [s_sb, m_sb]

            with nc.Block() as block:
                @block.sync
                def _(sp):
                    sp.dma_start(ids_sb[:, :], ids).then_inc(small_in, 16)
                    sp.dma_start(pw_sb[:, :, :], pw).then_inc(small_in, 16)
                    sp.dma_start(pb_sb[:, :], pb).then_inc(small_in, 16)
                    sp.dma_start(scl[:, :], scales).then_inc(small_in, 16)
                    for n in range(2 * NK):
                        if n >= 2:
                            sp.wait_ge(w2_lo_done, n - 1)
                        sp.dma_start(stage[n % 2][:, :], (wg if n < NK else wu)[:, n % NK, :])\
                            .then_inc(w2_in[n % 2], 16)
                    last = FCH[-1][1]
                    sp.dma_start(wd_sb[:, 0:NF - 1, :], wd[0:(NF - 1) * P, :].rearrange("(c p) n -> p c n", p=P))\
                        .then_inc(wd_in, 16)
                    sp.dma_start(wd_sb[0:last, NF - 1, :], wd[(NF - 1) * P:FI, :]).then_inc(wd_in, 16)
                    sp.wait_ge(small_in, 4 * 16)
                    for b in range(B):
                        adapter = sp.value_load(ids_sb[0:1, b:b + 1], min_val=0, max_val=wa.shape[0] - 1)
                        wait(sp, adapted, b)
                        sp.dma_start(wa_sb[:, :, :], wa[bass.ds(adapter, 1)].rearrange("o p k n -> p (o k) n"))\
                            .then_inc(wa_in, 16)
                        wait(sp, x1_done, b)
                        sp.dma_start(xn_sb[:, :], xn[b * S:(b + 1) * S, :]).then_inc(xn_in, 16)
                        if b:
                            sp.wait_ge(res_done, b)
                            sp.dma_start(out[(b - 1) * S:b * S, :], acc[:, b - 1, :]).then_inc(out_done, 16)
                    sp.wait_ge(res_done, B)
                    sp.dma_start(out[(B - 1) * S:B * S, :], acc[:, B - 1, :]).then_inc(out_done, 16)
                    sp.wait_ge(out_done, B * 16)

                @block.tensor
                def _(pe):
                    def gate_and_up(i):
                        wait(pe, c_copied, i + 1)
                        for k in range(NK):
                            last = pe.transpose(turn2_ps[:, k * P:(k + 1) * P], c_sb[:, k * P:(k + 1) * P], ident)
                        last.then_inc(c_turned, 1)
                        wait(pe, ct_lo_done, i + 1)
                        for to, w, before, done in ((gate_ps, (wg_hi, wg_lo), silu_done, gated),
                                                    (up_ps, (wu_hi, wu_lo), h_done, upped)):
                            wait(pe, before, i)
                            for at, n in BANKS3:
                                for k in range(NK):
                                    turn = slice(k * P, (k + 1) * P)
                                    last = product3(pe, to[:, at:at + n], (ct_hi[:, turn], ct_lo[:, turn]),
                                                    (w[0][:, k, at:at + n], w[1][:, k, at:at + n]),
                                                    k == 0, k == NK - 1)
                            last.then_inc(done, 1)

                    def tail(i):
                        wait(pe, h_done, i + 1)
                        c = 0
                        for n, job in enumerate(HT_JOBS):
                            if n:
                                wait(pe, h_copied[n - 1], i + 1)
                            for m, (at, width) in enumerate(job):
                                last = pe.transpose(turn2_ps[0:width, m * P:(m + 1) * P], h_sb[:, at:at + width],
                                                    ident)
                            last.then_inc(h_turned[n], 1)
                        wait(pe, h_copied[2], i + 1)
                        for c, (at, width) in enumerate(FCH):
                            last = pe.matmul(out_ps[:, :], ht[0:width, c, :], wd_sb[0:width, c, :],
                                             start=(c == 0), stop=(c == NF - 1))
                        last.then_inc(downed, 1)
                        wait(pe, x1_done, i + 1)
                        for k in range(NK):
                            last = pe.transpose(turn2_ps[:, k * P:(k + 1) * P], x1[:, k * P:(k + 1) * P], ident)
                        last.then_inc(x1_turned, 1)
                        wait(pe, x1_copied, i + 1)
                        wait(pe, wa_in, (i + 1) * 16)
                        for k in range(NK):
                            last = pe.matmul(out_ps[:, :], x1t[:, k * P:(k + 1) * P], wa_sb[:, k, :],
                                             start=(k == 0), stop=(k == NK - 1))
                        last.then_inc(adapted, 1)
                        wait(pe, y_copied, i + 1)
                        split = y[:, :].rearrange("p (a q r) -> p a r q", a=2, r=2)
                        for c in range(NK):
                            last = pe.transpose(turn2_ps[:, c * P:(c + 1) * P], split[:, c // 2, c % 2, :], ident)
                        last.then_inc(y_turned, 1)
                        wait(pe, yt_lo_done, i + 1)
                        for c in range(NK):
                            w = wf[:, c // 2, c % 2, :]
                            pe.matmul(out_ps[:, :], yt_hi[:, c * P:(c + 1) * P], w, start=(c == 0), stop=False)
                            last = pe.matmul(out_ps[:, :], yt_lo[:, c * P:(c + 1) * P], w, start=False,
                                             stop=(c == NK - 1))
                        last.then_inc(int4_done, 1)

                    pe.wait_ge(w2_lo_done, 2 * NK)
                    pe.wait_ge(wd_in, 2 * 16)
                    pe.wait_ge(unpacked, UNPACKED)
                    gate_and_up(0)
                    with pe.Fori(0, B - 1) as i:
                        gate_and_up(i + 1)
                        tail(i)
                    tail(B - 1)

                @block.scalar
                def _(act):
                    def front(i):
                        act.activation(c_sb[:, :], acc[:, i, :] if isinstance(i, int) else
                                       acc[:, bass.ds(i, 1), :].rearrange("p o n -> p (o n)"), ACT.Copy)\
                            .then_inc(c_copied, 1)
                        wait(act, c_turned, i + 1)
                        act.activation(ct[:, :], turn2_ps[:, :], ACT.Copy).then_inc(ct_copied, 1)
                        wait(act, ct_copied, i + 1)
                        act.activation(ct_hi[:, :], ct[:, :], ACT.Copy).then_inc(ct_hi_done, 1)
                        wait(act, gated, i + 1)
                        wait(act, h_done, i)
                        act.activation(s_sb[:, :], gate_ps[:, 0:FI], ACT.Silu).then_inc(silu_done, 1)
                        wait(act, silu_done, i + 1)
                        act.activation(m_sb[:, :], s_sb[:, :], ACT.Abs).then_inc(abs_done, 1)

                    def tail(i):
                        c = 0
                        for n, job in enumerate(HT_JOBS):
                            wait(act, h_turned[n], i + 1)
                            full = sum(width == P for _, width in job)
                            last = act.activation(ht[:, c:c + full, :].rearrange("p c t -> p (c t)"),
                                                  turn2_ps[:, 0:full * P], ACT.Copy)
                            for m in range(full, len(job)):
                                width = job[m][1]
                                last = act.activation(ht[0:width, c + m, :], turn2_ps[0:width, m * P:(m + 1) * P],
                                                      ACT.Copy)
                            last.then_inc(h_copied[n], 1)
                            c += len(job)
                        wait(act, downed, i + 1)
                        act.activation(dn[:, :], out_ps[:, :], ACT.Copy).then_inc(down_copied, 1)
                        wait(act, x1_turned, i + 1)
                        act.activation(x1t[:, :], turn2_ps[:, :], ACT.Copy).then_inc(x1_copied, 1)
                        wait(act, adapted, i + 1)
                        act.activation(y[:, :], out_ps[:, :], ACT.Copy).then_inc(y_copied, 1)
                        wait(act, y_turned, i + 1)
                        act.activation(yt[:, :], turn2_ps[:, :], ACT.Copy).then_inc(yt_copied, 1)
                        wait(act, yt_copied, i + 1)
                        act.activation(yt_hi[:, :], yt[:, :], ACT.Copy).then_inc(yt_hi_done, 1)
                        wait(act, int4_done, i + 1)
                        act.activation(fo[:, :], out_ps[:, :], ACT.Copy, scale=scl[:, 0:1]).then_inc(int4_scaled, 1)

                    for n in range(2 * NK):
                        act.wait_ge(w2_in[n % 2], (n // 2 + 1) * 16)
                        act.activation((wg_hi if n < NK else wu_hi)[:, n % NK, :], stage[n % 2][:, :], ACT.Copy)\
                            .then_inc(w2_hi_done, 1)
                    act.wait_ge(w2_lo_done, 2 * NK)
                    act.wait_ge(small_in, 4 * 16)
                    front(0)
                    with act.Fori(0, B - 1) as i:
                        front(i + 1)
                        tail(i)
                    tail(B - 1)

                @block.gpsimd
                def _(pool):
                    def front(i):
                        wait(pool, ct_hi_done, i + 1)
                        pool.tensor_tensor(ct_lo[:, :], ct[:, :], ct_hi[:, :].bitcast(F32), ALU.subtract)\
                            .then_inc(ct_lo_done, 1)

                    def tail(i):
                        wait(pool, down_copied, i + 1)
                        wait(pool, xn_in, (i + 1) * 16)
                        pool.tensor_tensor(x1[:, :], dn[:, :], xn_sb[:, :], ALU.add).then_inc(x1_done, 1)
                        wait(pool, x1_done, i + 1)
                        pool.tensor_tensor(x1b[:, :], x1[:, :], bias[:, :], ALU.add).then_inc(x1b_done, 1)
                        wait(pool, yt_hi_done, i + 1)
                        pool.tensor_tensor(yt_lo[:, :], yt[:, :], yt_hi[:, :].bitcast(F32), ALU.subtract)\
                            .then_inc(yt_lo_done, 1)
                        wait(pool, int4_scaled, i + 1)
                        wait(pool, x1b_done, i + 1)
                        to = acc[:, i, :] if isinstance(i, int) else \
                            acc[:, bass.ds(i, 1), :].rearrange("p o n -> p (o n)")
                        pool.tensor_tensor(to, fo[:, :], x1b[:, :], ALU.add).then_inc(res_done, 1)

                    pool.wait_ge(unpacked, UNPACKED)
                    front(0)
                    with pool.Fori(0, B - 1) as i:
                        front(i + 1)
                        tail(i)
                    tail(B - 1)

                @block.vector
                def _(dve):
                    links = [0]

                    def link(instruction):
                        links[0] += 1
                        instruction.then_inc(unpacked, 1)
                        dve.wait_ge(unpacked, links[0])

                    def threshold(i, n):
                        return i * LINKS + n

                    def drop_lower_half(i):
                        n = [0]

                        def chain(instruction):
                            n[0] += 1
                            instruction.then_inc(search, 1)
                            dve.wait_ge(search, threshold(i, n[0]))

                        def descend(keys, bits, below, result):
                            chain(dve.memset(tried[:, :], 2.0 ** (bits - 1)))
                            for bit in range(bits - 1, -1, -1):
                                chain(dve.tensor_scalar(junk[:, :], keys, tried[:, :], None, ALU.is_lt, ALU.add,
                                                        accum_out=count[:, :]))
                                chain(dve.tensor_scalar(taken[:, :], count[:, :], below, 2.0 ** bit,
                                                        ALU.is_lt, ALU.mult))
                                chain(dve.scalar_tensor_tensor(tried[:, :] if bit else result, taken[:, :],
                                                               -(2.0 ** (bit - 1)) if bit else -1.0, tried[:, :],
                                                               ALU.add, ALU.add))

                        wait(dve, abs_done, i + 1)
                        halves = m_sb[:, :].bitcast(U16).rearrange("p (n t) -> p n t", t=2)
                        chain(dve.tensor_copy(key[:, :], halves[:, :, 1]))
                        descend(key[:, :], 15, DROP - 0.5, high[:, :])
                        chain(dve.tensor_scalar(junk[:, :], key[:, :], high[:, :], None, ALU.is_lt, ALU.add,
                                                accum_out=count[:, :]))
                        chain(dve.tensor_scalar(room[:, :], count[:, :], -1.0, DROP - 0.5, ALU.mult, ALU.add))
                        chain(dve.tensor_scalar(junk[:, :], key[:, :], high[:, :], 65535.0, ALU.not_equal, ALU.mult))
                        chain(dve.tensor_tensor(key2[:, :], junk[:, :], halves[:, :, 0], ALU.max))
                        descend(key2[:, :], 16, room[:, :], low[:, :])
                        chain(dve.tensor_scalar(junk[:, :], key2[:, :], low[:, :], None, ALU.is_lt, ALU.add,
                                                accum_out=count[:, :]))
                        chain(dve.scalar_tensor_tensor(room[:, :], count[:, :], -1.0, room[:, :], ALU.mult, ALU.add))
                        chain(dve.tensor_copy(edge[:, 0:1], low[:, :]))
                        chain(dve.tensor_copy(edge[:, 1:2], high[:, :]))
                        at = edge[:, :].bitcast(F32)
                        above, equal, rank = key, key2, junk
                        dve.tensor_scalar(above[:, :].bitcast(BF16), m_sb[:, :], at, None, ALU.is_gt)
                        chain(dve.tensor_scalar(equal[:, :].bitcast(BF16), m_sb[:, :], at, None, ALU.is_equal))
                        chain(dve.tensor_tensor_scan(rank[:, :], equal[:, :].bitcast(BF16), equal[:, :].bitcast(BF16),
                                                     0.0, ALU.add, ALU.bypass))
                        chain(dve.scalar_tensor_tensor(equal[:, :].bitcast(BF16), rank[:, :], room[:, :],
                                                       equal[:, :].bitcast(BF16), ALU.is_gt, ALU.mult))
                        chain(dve.tensor_tensor(above[:, :].bitcast(BF16), above[:, :].bitcast(BF16),
                                                equal[:, :].bitcast(BF16), ALU.add))
                        wait(dve, h_turned[2], i)
                        chain(dve.tensor_tensor(h_sb[:, :], above[:, :].bitcast(BF16), s_sb[:, :], ALU.mult))
                        wait(dve, upped, i + 1)
                        dve.tensor_tensor(h_sb[:, :], h_sb[:, :], up_ps[:, 0:FI], ALU.mult).then_inc(h_done, 1)
                        assert n[0] == LINKS

                    for n in range(2 * NK):
                        dve.wait_ge(w2_hi_done, n + 1)
                        hi, lo = (wg_hi, wg_lo) if n < NK else (wu_hi, wu_lo)
                        dve.tensor_tensor(lo[:, n % NK, :], stage[n % 2][:, :], hi[:, n % NK, :].bitcast(F32),
                                          ALU.subtract).then_inc(w2_lo_done, 1)
                    dve.wait_ge(small_in, 4 * 16)
                    for parity in range(2):
                        shift4 = (4, ALU.arith_shift_right) if parity == 0 else (0, ALU.arith_shift_right)
                        link(dve.tensor_scalar(nibble[:, :, :], pw_sb[:, :, :], shift4[0], 15, shift4[1],
                                               ALU.bitwise_and))
                        link(dve.tensor_scalar(wf[:, :, parity, :], nibble[:, :, :], -8.0, None, ALU.add))
                        link(dve.tensor_scalar(bias_i[:, :, parity], pb_sb[:, :], shift4[0], 15, shift4[1],
                                               ALU.bitwise_and))
                    link(dve.tensor_scalar(bias[:, :], bias_i[:, :, :].rearrange("p n t -> p (n t)"), -8.0,
                                           scl[:, 1:2], ALU.add, ALU.mult))
                    assert links[0] == UNPACKED
                    drop_lower_half(0)
                    with dve.Fori(1, B) as i:
                        drop_lower_half(i)


_INS = ["xt", "xn", "lens", "pages", "ids", "wqkv", "wo", "qw", "kw", "kc", "vc", "wg", "wu", "wd", "wa", "pw", "pb",
        "scales", "consts"]


def kernel(x, itok_Bx16_0_63, itok_B_207_1644, itok_B_1_14, L0_cond_Wq, L0_cond_Wk, L0_cond_Wv, L0_cond_Wo,
           L0_cond_q_norm_w, L0_cond_k_norm_w, L0_cond_k_cache, L0_cond_v_cache, L0_attn_w_gate, L0_attn_w_up,
           L0_attn_w_down, L0_cond2_weight, L0_ffn_packed_w, L0_ffn_packed_b, L0_ffn_scale_w, L0_ffn_scale_b):
    import numpy as np
    import concourse.bacc as bacc
    from concourse.bass_utils import run_bass_kernel_spmd

    x, pages, lens, ids = (np.asarray(a) for a in (x, itok_Bx16_0_63, itok_B_207_1644, itok_B_1_14))
    wq, wk, wv, wo = (np.asarray(a) for a in (L0_cond_Wq, L0_cond_Wk, L0_cond_Wv, L0_cond_Wo))
    by_head = [w.reshape(HK, -1, NK, P).transpose(0, 3, 2, 1) for w in (wq, wk, wv)]
    chunked = lambda w: np.asarray(w).T.reshape(NK, P, -1).transpose(1, 0, 2)
    consts = np.zeros((P, C_ALL), np.float32)
    consts[:, C_ID:C_ID + P] = np.eye(P)
    consts[:, C_INV:C_INV + D // 2] = 1.0 / 10000.0 ** (np.arange(0, D, 2) / D)
    consts[:, C_PART] = np.arange(P)
    consts[:, C_LANE] = np.arange(P) % PSIZE * HK
    consts[:, C_KEY:] = np.arange(L)
    arrays = dict(
        xt=x.reshape(B, S, NK, P).transpose(3, 0, 2, 1).reshape(P, -1),
        xn=x.reshape(B * S, DM),
        lens=np.broadcast_to(lens, (P, B)),
        pages=np.repeat(pages.reshape(B, NC, P // PSIZE).transpose(2, 0, 1).reshape(P // PSIZE, -1), PSIZE, axis=0),
        ids=ids.reshape(1, B),
        wqkv=np.concatenate(by_head, axis=3),
        wo=wo.reshape(DM, HK, REP, D).transpose(1, 3, 2, 0),
        qw=np.broadcast_to(np.asarray(L0_cond_q_norm_w), (P, D)),
        kw=np.broadcast_to(np.asarray(L0_cond_k_norm_w), (P, D)),
        kc=np.asarray(L0_cond_k_cache).reshape(-1, D),
        vc=np.asarray(L0_cond_v_cache).reshape(-1, D),
        wg=chunked(L0_attn_w_gate),
        wu=chunked(L0_attn_w_up),
        wd=np.asarray(L0_attn_w_down).T,
        wa=np.asarray(L0_cond2_weight).transpose(0, 2, 1).reshape(-1, NK, P, DM).transpose(0, 2, 1, 3),
        pw=np.asarray(L0_ffn_packed_w).reshape(DM, 2, P).transpose(2, 1, 0),
        pb=np.broadcast_to(np.asarray(L0_ffn_packed_b), (P, DM // 2)),
        scales=np.broadcast_to(np.stack([np.asarray(L0_ffn_scale_w), np.asarray(L0_ffn_scale_b)]), (P, 2)),
        consts=consts,
    )
    nc = bacc.Bacc("TRN2", target_bir_lowering=False, num_devices=1)
    arrays = {n: np.ascontiguousarray(arrays[n]) for n in _INS}
    args = [nc.dram_tensor(n, a.shape, mybir.dt.from_np(a.dtype), kind="ExternalInput").ap() for n, a in arrays.items()]
    out = nc.dram_tensor("out", (B * S, DM), F32, kind="ExternalOutput").ap()
    adaln_attn_ffn(nc, *args, out)
    r = run_bass_kernel_spmd(nc, [arrays], core_ids=[0])
    return r.results[0]["out"].reshape(B, S, DM)
```

```python
from contextlib import ExitStack

import concourse.bass as bass
from concourse import mybir

F32 = mybir.dt.float32
F32R = mybir.dt.float32r
BF16 = mybir.dt.bfloat16
I32 = mybir.dt.int32
U32 = mybir.dt.uint32
U16 = mybir.dt.uint16
ALU = mybir.AluOpType
ACT = mybir.ActivationFunctionType

P = 128
B, S, DM = 8, 128, 512
D, HQ, HK = 128, 32, 8
REP = HQ // HK
PAGES, PSIZE, NPP = 64, 32, 16
L = NPP * PSIZE
KEYS = L + S
HALF = KEYS // 2
NK = DM // P
NC = L // P
NJ = KEYS // P
GQ = REP * D
GW = GQ + 2 * D
STEPS = HK * B
EPS = 1e-6
SOFTMAX_SCALE = float(D) ** -0.5
NEG = -1e30
FI = 1376
DROP = FI // 2
FCH = [(i * P, min(P, FI - i * P)) for i in range((FI + P - 1) // P)]
BANKS3 = [(0, 512), (512, 512), (1024, FI - 1024)]
ROUND = 1.5 * 2.0 ** 23
TWO_PI = (6.28125, 0.0019350051879882812, 3.0199157663446503e-07)
PI = 3.141592653589793
Q_CALLS = 3
W_PIECES = [(slice(0, 2), slice(0, GQ)), (slice(2, NK), slice(0, GQ)), (slice(0, NK), slice(GQ, GW))]
WO_HALVES = [slice(0, REP // 2), slice(REP // 2, REP)]
UNPACKED = 7
LINKS = (1 + 1 + 3 * 15) + 3 + (1 + 3 * 16) + 2 + 3
SINES_READY = 3 + 2 * 7
MASK_READY = SINES_READY + 1
TABLES_READY = MASK_READY + 1
PI_IN = 3.1415925
C_ID, C_INV, C_PART, C_LANE, C_KEY, C_ALL = 0, 128, 192, 193, 194, 194 + L


WG_AT = {STEPS - 3: (0, 1), STEPS - 2: (2,), STEPS - 1: (3,)}


def live(s):
    return not isinstance(s, int) or 0 <= s < STEPS


def wait(eng, sem, n):
    if not isinstance(n, int) or n > 0:
        eng.wait_ge(sem, n)


def at_most(n):
    return min(n, STEPS) if isinstance(n, int) else n


def aligned(at):
    return -(-at // 32) * 32


def product3(pe, out, left, right, start, stop):
    pe.matmul(out, left[0], right[0], start=start, stop=False)
    pe.matmul(out, left[0], right[1], start=False, stop=False)
    return pe.matmul(out, left[1], right[0], start=False, stop=stop)


def adaln_attn_ffn(nc, xt, xn, lens, pages, ids, wqkv, wo, qw, kw, kc, vc, wg, wu, wd, wa, pw, pb, scales,
                   consts, out):
    with ExitStack() as whole:
        def semaphore(name):
            return whole.enter_context(nc.semaphore(name))

        def tensors(stack):
            return lambda name, shape, dt=F32: stack.enter_context(nc.sbuf_tensor(name, shape, dt))

        sb = tensors(whole)
        acc = sb("acc", [P, B, DM])
        cst = sb("cst", [P, C_KEY])
        ident = cst[:, C_ID:C_ID + P]

        const_in = semaphore("const_in")
        xt_in = semaphore("xt_in")
        w_in = semaphore("w_in")
        wo_in = semaphore("wo_in")
        k_in = [semaphore(f"k_in{n}") for n in range(2)]
        v_in = [semaphore(f"v_in{n}") for n in range(2)]
        xt_hi_done = semaphore("xt_hi_done")
        w_hi_done = [semaphore(f"w_hi_done{n}") for n in range(3)]
        w_lo_done = [semaphore(f"w_lo_done{n}") for n in range(3)]
        wo_hi_done = semaphore("wo_hi_done")
        wo_lo_done = [semaphore(f"wo_lo_done{n}") for n in range(2)]
        setup_dve = semaphore("setup_dve")
        setup_pool = semaphore("setup_pool")
        sines_done = semaphore("sines_done")
        held = semaphore("held")
        idx_ready = semaphore("idx_ready")
        q_chunks = semaphore("q_chunks")
        kv_projected = semaphore("kv_projected")
        q_copied = semaphore("q_copied")
        kv_copied = semaphore("kv_copied")
        squares_done = semaphore("squares_done")
        eps_added = semaphore("eps_added")
        rstd_done = semaphore("rstd_done")
        ropeq_parts = semaphore("ropeq_parts")
        ropek_parts = semaphore("ropek_parts")
        ropeq_done = semaphore("ropeq_done")
        ropek_done = semaphore("ropek_done")
        kc_turned = semaphore("kc_turned")
        q_turned = semaphore("q_turned")
        kn_turned = semaphore("kn_turned")
        kc_hi_done = semaphore("kc_hi_done")
        q_hi_done = semaphore("q_hi_done")
        kn_hi_done = semaphore("kn_hi_done")
        kc_lo_done = semaphore("kc_lo_done")
        q_lo_done = semaphore("q_lo_done")
        kn_lo_done = semaphore("kn_lo_done")
        scored = [semaphore(f"scored{h}") for h in range(REP)]
        max_done = [semaphore(f"max_done{h}") for h in range(REP)]
        shift_done = [semaphore(f"shift_done{h}") for h in range(REP)]
        exp_done = [semaphore(f"exp_done{h}") for h in range(REP)]
        recip_done = semaphore("recip_done")
        probs_done = semaphore("probs_done")
        p_turned = [semaphore(f"p_turned{j}") for j in range(NJ)]
        p_hi_done = [semaphore(f"p_hi_done{j}") for j in range(NJ)]
        p_lo_done = [semaphore(f"p_lo_done{j}") for j in range(NJ)]
        v_hi_done = semaphore("v_hi_done")
        v_lo_done = semaphore("v_lo_done")
        valued = semaphore("valued")
        o_hi_done = semaphore("o_hi_done")
        o_lo_done = semaphore("o_lo_done")
        o_projected = semaphore("o_projected")
        acc_added = semaphore("acc_added")

        wg_in = semaphore("wg_in")
        wg_hi_done = semaphore("wg_hi_done")
        wg_lo_done = semaphore("wg_lo_done")
        early = aligned(nc.sbuf_base)
        wg_hi, wg_lo, wu_hi = (nc.alloc_sbuf_tensor_at(name, [P, NK, FI], F32R, offset=early + n * NK * FI * 4)
                               for n, name in enumerate(("wg_hi", "wg_lo", "wu_hi")))
        wg_raw = nc.alloc_sbuf_tensor_at("wg_raw", [P, NK, FI], F32, offset=early + 2 * NK * FI * 4)

        with ExitStack() as phase1:
            sb = tensors(phase1)
            ps = lambda name, n: phase1.enter_context(nc.psum_tensor(name, [P, n], F32))
            proj_ps = ps("proj_ps", 512)
            turn_ps = [ps("turn_ps0", 512), ps("turn_ps1", 512)]
            score_ps = [ps("score_ps0", 1024), ps("score_ps1", 1024)]
            value_ps = ps("value_ps", 512)

            xt_hi = sb("xt_hi", [P, B, NK, S], F32R)
            xt_lo = sb("xt_lo", [P, B, NK, S], F32R)
            w_raw = sb("w_raw", [P, NK, GW])
            w_hi = sb("w_hi", [P, NK, GW], F32R)
            w_lo = sb("w_lo", [P, NK, GW], F32R)
            wo_raw = sb("wo_raw", [P, REP, DM])
            wo_hi = sb("wo_hi", [P, REP, DM], F32R)
            wo_lo = sb("wo_lo", [P, REP, DM], F32R)
            mask = sb("mask", [P, B, KEYS], BF16)
            qa = sb("qa", [P, B, D])
            qb = sb("qb", [P, B, D])
            ka = sb("ka", [P, B, D])
            kb = sb("kb", [P, B, D])
            kg = sb("kg", [P, 2, NC, D])
            vg = sb("vg", [P, 2, NC, D])
            vn = sb("vn", [P, 4, D])
            v_hi = sb("v_hi", [P, 2, NJ, D], F32R)
            v_lo = sb("v_lo", [P, 2, NJ, D], F32R)
            qk = sb("qk", [P, REP + 1, D])
            rot_q = sb("rot_q", [P, 2, REP, D])
            rot_k = sb("rot_k", [P, D])
            rot_b = sb("rot_b", [P, REP + 1, D])
            kt_hi = sb("kt_hi", [P, KEYS], F32R)
            kt_lo = sb("kt_lo", [P, KEYS], F32R)
            qt_hi = sb("qt_hi", [P, GQ], F32R)
            qt_lo = sb("qt_lo", [P, GQ], F32R)
            probs = sb("probs", [P, 2, REP, KEYS])
            pt_hi = sb("pt_hi", [P, 2, GQ], F32R)
            pt_lo = sb("pt_lo", [P, 2, GQ], F32R)
            ot_hi = sb("ot_hi", [P, GQ], F32R)
            ot_lo = sb("ot_lo", [P, GQ], F32R)
            ss = sb("ss", [P, REP + 1])
            ss_eps = sb("ss_eps", [P, REP + 1])
            power = sb("power", [P, REP + 1])
            eps = sb("eps", [P, REP + 1])
            rstd = sb("rstd", [P, 2, REP + 1])
            row_max = sb("row_max", [P, REP])
            shift = sb("shift", [P, REP])
            sums = sb("sums", [P, REP])
            recips = sb("recips", [P, REP])
            lens_i = sb("lens_i", [P, B], I32)
            pages_i = sb("pages_i", [P, B * NC], I32)
            idx = sb("idx", [P, B * NC], U32)
            x_raw = probs[:, :, :, :].rearrange("p a h k -> p (a h k)")[:, 0:B * NK * S]
            angle, turns, sines, cosines = (wo_raw[:, i, :].rearrange("p (b f) -> p b f", b=B) for i in range(4))
            squared = sb("squared", [P, REP + 1, D], BF16)
            pos = sb("pos", [P, B])
            lens_f = sb("lens_f", [P, B])
            qkw = rot_b[:, 0:2, :]
            key_no = rot_q[:, 0, 0:NC, :].rearrange("p c d -> p (c d)")

            with nc.Block() as block:
                @block.sync
                def _(sp):
                    sp.dma_start(cst[:, :], consts[:, 0:C_KEY]).then_inc(const_in, 16)
                    sp.dma_start(key_no, consts[:, C_KEY:C_ALL]).then_inc(const_in, 16)
                    sp.dma_start(lens_i[:, :], lens).then_inc(const_in, 16)
                    sp.dma_start(pages_i[:, :], pages).then_inc(const_in, 16)
                    sp.dma_start(qkw[:, 0, :], qw).then_inc(const_in, 16)
                    sp.dma_start(qkw[:, 1, :], kw).then_inc(const_in, 16)
                    sp.dma_start(x_raw, xt).then_inc(xt_in, 16)
                    sp.dma_start(w_raw[:, :, :], wqkv[0]).then_inc(w_in, 16)
                    sp.wait_ge(setup_dve, TABLES_READY)
                    sp.dma_start(wo_raw[:, :, :], wo[0]).then_inc(wo_in, 16)
                    with sp.Fori(1, HK) as g:
                        for n in range(len(W_PIECES)):
                            sp.wait_ge(w_lo_done[n], g)
                        sp.dma_start(w_raw[:, :, :], wqkv[bass.ds(g, 1)].rearrange("o p k n -> p (o k) n"))\
                            .then_inc(w_in, 16)
                        for n in range(len(WO_HALVES)):
                            sp.wait_ge(wo_lo_done[n], g)
                        sp.dma_start(wo_raw[:, :, :], wo[bass.ds(g, 1)].rearrange("o p h n -> p (o h) n"))\
                            .then_inc(wo_in, 16)
                    sp.wait_ge(kv_projected, STEPS)
                    sp.dma_start(wg_raw[:, :, :], wg).then_inc(wg_in, 16)

                @block.gpsimd
                def _(pool):
                    pool.memset(power[:, :], -0.5).then_inc(setup_pool, 1)
                    pool.memset(eps[:, :], D * EPS).then_inc(setup_pool, 1)
                    pool.wait_ge(const_in, 6 * 16)
                    pool.tensor_scalar(idx[:, :], pages_i[:, :], float(PSIZE * HK), cst[:, C_LANE:C_LANE + 1],
                                       ALU.mult, ALU.add).then_inc(idx_ready, 1)

                    def hold(waits):
                        for sem, n in waits:
                            wait(pool, sem, n)
                        pool.sem_inc(held, 1)

                    def gather_k(s, b, g):
                        if b == 0 and not (isinstance(g, int) and g == 0):
                            hold([(place, s // 2 * (NC * 16)) for place in k_in + v_in])
                            pool.tensor_scalar(idx[:, :], idx[:, :], 1.0, None, ALU.add).then_inc(idx_ready, 1)
                        hold([(idx_ready, g + 1), (kc_turned, s - 1)])
                        for c in range(NC):
                            pool.indirect_dma_start(
                                kg[:, b % 2, c, :], None, kc,
                                bass.IndirectOffsetOnAxis(ap=idx[:, b * NC + c:b * NC + c + 1], axis=0))\
                                .then_inc(k_in[b % 2], 16)

                    def gather_v(s, b):
                        hold([(v_lo_done, s - 1)])
                        for c in range(NC):
                            pool.indirect_dma_start(
                                vg[:, b % 2, c, :], None, vc,
                                bass.IndirectOffsetOnAxis(ap=idx[:, b * NC + c:b * NC + c + 1], axis=0))\
                                .then_inc(v_in[b % 2], 16)

                    def split_v(s, b):
                        wait(pool, v_hi_done, s + 1)
                        pool.tensor_tensor(v_lo[:, b % 2, 0:NC, :], vg[:, b % 2, :, :],
                                           v_hi[:, b % 2, 0:NC, :].bitcast(F32), ALU.subtract)
                        pool.tensor_tensor(v_lo[:, b % 2, NC, :], vn[:, b % 4, :],
                                           v_hi[:, b % 2, NC, :].bitcast(F32), ALU.subtract).then_inc(v_lo_done, 1)

                    def norms(s, b):
                        wait(pool, squares_done, s + 1)
                        pool.tensor_tensor(ss_eps[:, :], ss[:, :], eps[:, :], ALU.add).then_inc(eps_added, 1)
                        wait(pool, eps_added, s + 1)
                        wait(pool, exp_done[REP - 1], s - 1)
                        pool.tensor_tensor(rstd[:, b % 2, :], ss_eps[:, :], power[:, :], ALU.pow)\
                            .then_inc(rstd_done, 1)

                    def step(s, b, g):
                        b1, b2, b3 = (b + 1) % B, (b + 2) % B, (b + 3) % B
                        if live(s + 2):
                            gather_v(s + 2, b2)
                        if live(s + 3):
                            gather_k(s + 3, b3, g + (b + 3) // B)
                            norms(s + 3, b3)
                        if live(s + 1):
                            split_v(s + 1, b1)

                    pool.wait_ge(setup_pool, 2)
                    for s in range(-3, 0):
                        step(s, s % B, -1)
                    with pool.Fori(0, STEPS - B, B) as s0:
                        g = pool.snap(s0 // B)
                        for b in range(B):
                            step(s0 + b, b, g)
                    for b in range(B):
                        step(STEPS - B + b, b, HK - 1)

                @block.tensor
                def _(pe):
                    def pair(hi, lo, at):
                        return hi[at], lo[at]

                    def project_q(s, b, g, ks):
                        if b == 0 and ks[0] in (0, 2):
                            wait(pe, w_lo_done[ks[0] // 2], g + 1)
                        if ks[0] == 0:
                            wait(pe, kv_copied, s)
                            wait(pe, acc_added, s - 2)
                        for k in ks:
                            last = product3(pe, proj_ps[:, :], (xt_hi[:, b, k, :], xt_lo[:, b, k, :]),
                                            (w_hi[:, k, 0:GQ], w_lo[:, k, 0:GQ]), k == 0, k == NK - 1)
                        last.then_inc(q_chunks, 1)

                    def project_kv(s, b, g):
                        if b == 0:
                            wait(pe, w_lo_done[2], g + 1)
                        wait(pe, q_copied, s + 1)
                        for k in range(NK):
                            last = product3(pe, proj_ps[:, 0:2 * D], (xt_hi[:, b, k, :], xt_lo[:, b, k, :]),
                                            (w_hi[:, k, GQ:GW], w_lo[:, k, GQ:GW]), k == 0, k == NK - 1)
                        last.then_inc(kv_projected, 1)

                    def turn_cached_k(s, b):
                        wait(pe, p_lo_done[3], s - 1)
                        wait(pe, k_in[b % 2], (s // 2 + 1) * (NC * 16))
                        for c in range(NC):
                            last = pe.transpose(turn_ps[0][:, c * P:(c + 1) * P], kg[:, b % 2, c, :], ident)
                        last.then_inc(kc_turned, 1)

                    def turn_q(s, b):
                        wait(pe, p_lo_done[4], s - 1)
                        wait(pe, ropeq_done, s + 1)
                        for h in range(REP):
                            last = pe.transpose(turn_ps[1][:, h * P:(h + 1) * P], rot_q[:, b % 2, h, :], ident)
                        last.then_inc(q_turned, 1)

                    def turn_new_k(s):
                        wait(pe, kc_lo_done, s + 1)
                        wait(pe, ropek_done, s + 1)
                        pe.transpose(turn_ps[0][:, 0:P], rot_k[:, :], ident).then_inc(kn_turned, 1)

                    def scores(s, heads):
                        if heads[0] == 0:
                            wait(pe, q_lo_done, s + 1)
                            wait(pe, kn_lo_done, s + 1)
                        for h in heads:
                            wait(pe, max_done[(h + 2) % REP], s if h < 2 else s + 1)
                            for a in range(2):
                                last = product3(pe, score_ps[h % 2][:, 512 * a:512 * a + HALF],
                                                (qt_hi[:, h * P:(h + 1) * P], qt_lo[:, h * P:(h + 1) * P]),
                                                (kt_hi[:, a * HALF:(a + 1) * HALF], kt_lo[:, a * HALF:(a + 1) * HALF]),
                                                True, True)
                            last.then_inc(scored[h], 1)

                    def turn_probs(s, b, j):
                        if j == 0:
                            wait(pe, probs_done, s + 1)
                            wait(pe, q_lo_done, at_most(s + 2))
                        elif j == 1:
                            wait(pe, kn_lo_done, at_most(s + 2))
                        else:
                            wait(pe, p_lo_done[j - 2], s + 1)
                        for h in range(REP):
                            last = pe.transpose(turn_ps[1 - j % 2][:, h * P:(h + 1) * P],
                                                probs[:, b % 2, h, j * P:(j + 1) * P], ident)
                        last.then_inc(p_turned[j], 1)

                    def values(s, b, j):
                        if j == 0:
                            wait(pe, v_lo_done, s + 1)
                        wait(pe, p_lo_done[j], s + 1)
                        at = (b + j) % 2
                        last = product3(pe, value_ps[:, :], (v_hi[:, b % 2, j, :], v_lo[:, b % 2, j, :]),
                                        (pt_hi[:, at, :], pt_lo[:, at, :]), j == 0, j == NJ - 1)
                        if j == NJ - 1:
                            last.then_inc(valued, 1)

                    def project_o(s, b, g):
                        wait(pe, kv_copied, at_most(s + 4))
                        wait(pe, o_lo_done, s + 1)
                        for h in range(REP):
                            if b == 0 and h % 2 == 0:
                                wait(pe, wo_lo_done[h // 2], g + 1)
                            at = slice(h * P, (h + 1) * P)
                            last = product3(pe, proj_ps[:, :], (ot_hi[:, at], ot_lo[:, at]),
                                            (wo_hi[:, h, :], wo_lo[:, h, :]), h == 0, h == REP - 1)
                        last.then_inc(o_projected, 1)

                    def step(s, b, g):
                        b1, b2, b3 = (b + 1) % B, (b + 2) % B, (b + 3) % B
                        g3 = g + (b + 3) // B
                        if live(s):
                            turn_probs(s, b, 1)
                        if live(s + 3):
                            project_q(s + 3, b3, g3, (0, 1))
                        if live(s):
                            values(s, b, 0)
                            turn_probs(s, b, 2)
                            values(s, b, 1)
                            turn_probs(s, b, 3)
                        if live(s + 3):
                            project_q(s + 3, b3, g3, (2,))
                        if live(s):
                            values(s, b, 2)
                            turn_probs(s, b, 4)
                            values(s, b, 3)
                        if live(s + 3):
                            project_q(s + 3, b3, g3, (3,))
                        if live(s + 2):
                            turn_cached_k(s + 2, b2)
                        if live(s):
                            values(s, b, 4)
                        if live(s + 3):
                            project_kv(s + 3, b3, g3)
                        if live(s + 2):
                            turn_q(s + 2, b2)
                            turn_new_k(s + 2)
                        if live(s):
                            project_o(s, b, g)
                        if live(s + 2):
                            scores(s + 2, (0, 1))
                        if live(s + 1):
                            turn_probs(s + 1, b1, 0)
                        if live(s + 2):
                            scores(s + 2, (2, 3))

                    pe.wait_ge(const_in, 6 * 16)
                    pe.wait_ge(xt_hi_done, 1)
                    pe.wait_ge(setup_dve, MASK_READY + 2)
                    for s in range(-3, 0):
                        step(s, s % B, -1)
                    with pe.Fori(0, STEPS - B, B) as s0:
                        g = pe.snap(s0 // B)
                        for b in range(B):
                            step(s0 + b, b, g)
                    for b in range(B):
                        step(STEPS - B + b, b, HK - 1)

                @block.scalar
                def _(act):
                    def split_w(g, n):
                        ks, cols = W_PIECES[n]
                        wait(act, w_in, (g + 1) * 16)
                        if n < 2:
                            wait(act, q_chunks, g * (B * Q_CALLS) - (0 if n else Q_CALLS - 1))
                        else:
                            wait(act, kv_projected, g * B)
                        act.activation(w_hi[:, ks, cols], w_raw[:, ks, cols], ACT.Copy).then_inc(w_hi_done[n], 1)

                    def split_wo(g):
                        wait(act, wo_in, (g + 1) * 16)
                        wait(act, o_projected, g * B)
                        act.activation(wo_hi[:, :, :], wo_raw[:, :, :], ACT.Copy).then_inc(wo_hi_done, 1)

                    def copy_q(s):
                        wait(act, q_chunks, (s + 1) * Q_CALLS)
                        wait(act, ropeq_done, s)
                        wait(act, squares_done, s)
                        act.activation(qk[:, 0:REP, :].rearrange("p h d -> p (h d)"), proj_ps[:, :], ACT.Copy)\
                            .then_inc(q_copied, 1)

                    def copy_kv(s, b):
                        wait(act, kv_projected, s + 1)
                        wait(act, ropek_done, s)
                        act.activation(qk[:, REP, :], proj_ps[:, 0:D], ACT.Copy)
                        act.activation(vn[:, b % 4, :], proj_ps[:, D:2 * D], ACT.Copy).then_inc(kv_copied, 1)

                    def split_v(s, b):
                        wait(act, v_in[b % 2], (s // 2 + 1) * (NC * 16))
                        wait(act, kv_copied, s + 1)
                        act.activation(v_hi[:, b % 2, 0:NC, :], vg[:, b % 2, :, :], ACT.Copy)
                        act.activation(v_hi[:, b % 2, NC, :], vn[:, b % 4, :], ACT.Copy).then_inc(v_hi_done, 1)

                    def squares(s):
                        wait(act, eps_added, s)
                        wait(act, q_copied, s + 1)
                        wait(act, kv_copied, s + 1)
                        for h in range(REP + 1):
                            last = act.activation(squared[:, h, :], qk[:, h, :], ACT.Square, accum_out=ss[:, h:h + 1])
                        last.then_inc(squares_done, 1)

                    def split_cached_k(s):
                        wait(act, kc_turned, s + 1)
                        act.activation(kt_hi[:, 0:L], turn_ps[0][:, :], ACT.Copy).then_inc(kc_hi_done, 1)

                    def split_q(s):
                        wait(act, q_turned, s + 1)
                        act.activation(qt_hi[:, :], turn_ps[1][:, :], ACT.Copy).then_inc(q_hi_done, 1)

                    def split_new_k(s):
                        wait(act, kn_turned, s + 1)
                        act.activation(kt_hi[:, L:KEYS], turn_ps[0][:, 0:P], ACT.Copy).then_inc(kn_hi_done, 1)

                    def exps(s, b, heads):
                        if heads[0] == 0:
                            wait(act, recip_done, s)
                        for h in heads:
                            wait(act, shift_done[h], s + 1)
                            row = probs[:, b % 2, h, :]
                            act.activation(row, row, ACT.Exp, bias=shift[:, h:h + 1],
                                           scale=rstd[:, b % 2, h:h + 1], accum_out=sums[:, h:h + 1])\
                                .then_inc(exp_done[h], 1)

                    def split_probs(s, b, j):
                        wait(act, p_turned[j], s + 1)
                        act.activation(pt_hi[:, (b + j) % 2, :], turn_ps[1 - j % 2][:, :], ACT.Copy)\
                            .then_inc(p_hi_done[j], 1)

                    def split_o(s):
                        wait(act, valued, s + 1)
                        act.activation(ot_hi[:, :], value_ps[:, :], ACT.Copy).then_inc(o_hi_done, 1)

                    def step(s, b, g):
                        b1, b2, b3 = (b + 1) % B, (b + 2) % B, (b + 3) % B
                        next_w = b == B - 4 and live(s + 4)
                        if live(s):
                            split_probs(s, b, 1)
                        if live(s + 1):
                            exps(s + 1, b1, (1, 2))
                        if live(s):
                            split_probs(s, b, 2)
                        if live(s + 1):
                            exps(s + 1, b1, (3,))
                        if live(s):
                            split_probs(s, b, 3)
                        if next_w:
                            split_w(g + 1, 0)
                        if live(s):
                            split_probs(s, b, 4)
                        if live(s + 3):
                            copy_q(s + 3)
                        if live(s + 2):
                            split_cached_k(s + 2)
                        if live(s):
                            split_o(s)
                        if live(s + 3):
                            copy_kv(s + 3, b3)
                        if live(s + 2):
                            split_q(s + 2)
                            split_new_k(s + 2)
                        if live(s + 3):
                            squares(s + 3)
                        if next_w:
                            split_w(g + 1, 1)
                        if live(s + 1):
                            split_v(s + 1, b1)
                        if next_w:
                            split_w(g + 1, 2)
                        if b == B - 1 and live(s + 1):
                            split_wo(g + 1)
                        if live(s + 1):
                            split_probs(s + 1, b1, 0)
                        if live(s + 2):
                            exps(s + 2, b2, (0,))

                    def split_wg(s):
                        for k in WG_AT.get(s, ()):
                            act.wait_ge(wg_in, 16)
                            act.activation(wg_hi[:, k, :], wg_raw[:, k, :], ACT.Copy).then_inc(wg_hi_done, 1)

                    act.wait_ge(setup_dve, SINES_READY)
                    act.activation(sines, sines, ACT.Sin)
                    act.activation(cosines, cosines, ACT.Sin).then_inc(sines_done, 1)
                    act.wait_ge(xt_in, 16)
                    act.activation(xt_hi[:, :, :, :].rearrange("p b k t -> p (b k t)"), x_raw, ACT.Copy)\
                        .then_inc(xt_hi_done, 1)
                    for n in range(len(W_PIECES)):
                        split_w(0, n)
                    for s in range(-3, 0):
                        step(s, s % B, -1)
                    with act.Fori(0, STEPS - B, B) as s0:
                        g = act.snap(s0 // B)
                        for b in range(B):
                            step(s0 + b, b, g)
                    for b in range(B):
                        step(STEPS - B + b, b, HK - 1)
                        split_wg(STEPS - B + b)

                @block.vector
                def _(dve):
                    links = [0]

                    def link(instruction):
                        links[0] += 1
                        instruction.then_inc(setup_dve, 1)
                        dve.wait_ge(setup_dve, links[0])

                    def reduced(to, quarter):
                        link(dve.tensor_scalar(turns, angle, 1 / (2 * PI), 0.25 * quarter, ALU.mult, ALU.add))
                        link(dve.tensor_scalar(turns, turns, ROUND, ROUND, ALU.add, ALU.subtract))
                        link(dve.scalar_tensor_tensor(to, turns, -TWO_PI[0], angle, ALU.mult, ALU.add))
                        link(dve.scalar_tensor_tensor(to, turns, -TWO_PI[1], to, ALU.mult, ALU.add))
                        link(dve.scalar_tensor_tensor(to, turns, -TWO_PI[2], to, ALU.mult, ALU.add))
                        link(dve.tensor_scalar(to, to, 0.5 * PI * quarter, PI_IN, ALU.add, ALU.min))
                        link(dve.tensor_scalar(to, to, -PI_IN, None, ALU.max))

                    def split_w(g, n):
                        ks, cols = W_PIECES[n]
                        wait(dve, w_hi_done[n], g + 1)
                        dve.tensor_tensor(w_lo[:, ks, cols], w_raw[:, ks, cols], w_hi[:, ks, cols].bitcast(F32),
                                          ALU.subtract).then_inc(w_lo_done[n], 1)

                    def split_wo(g, n):
                        hs = WO_HALVES[n]
                        wait(dve, wo_hi_done, g + 1)
                        dve.tensor_tensor(wo_lo[:, hs, :], wo_raw[:, hs, :], wo_hi[:, hs, :].bitcast(F32), ALU.subtract)\
                            .then_inc(wo_lo_done[n], 1)

                    def over_heads(table):
                        return table.unsqueeze(1).broadcast_to((P, REP, table.shape[-1]))

                    lo, hi = slice(0, D // 2), slice(D // 2, D)

                    def rotate_q(s, b):
                        wait(dve, q_copied, s + 1)
                        wait(dve, ropeq_done, s)
                        wait(dve, q_turned, s - 1)
                        q = qk[:, 0:REP, :]
                        dve.tensor_tensor(rot_q[:, b % 2, :, :], q, over_heads(qa[:, b, :]), ALU.mult)
                        dve.tensor_tensor(rot_b[:, 0:REP, lo], q[:, :, hi], over_heads(qb[:, b, lo]), ALU.mult)
                        dve.tensor_tensor(rot_b[:, 0:REP, hi], q[:, :, lo], over_heads(qb[:, b, hi]), ALU.mult)\
                            .then_inc(ropeq_parts, 1)

                    def add_q(s, b):
                        wait(dve, ropeq_parts, s + 1)
                        dve.tensor_tensor(rot_q[:, b % 2, :, :], rot_q[:, b % 2, :, :], rot_b[:, 0:REP, :], ALU.add)\
                            .then_inc(ropeq_done, 1)

                    def rotate_k(s, b):
                        wait(dve, kn_turned, s)
                        wait(dve, kv_copied, s + 1)
                        wait(dve, rstd_done, s + 1)
                        k, norm = qk[:, REP, :], rstd[:, b % 2, REP:REP + 1]
                        dve.scalar_tensor_tensor(rot_k[:, :], k, norm, ka[:, b, :], ALU.mult, ALU.mult)
                        dve.scalar_tensor_tensor(rot_b[:, REP, lo], k[:, hi], norm, kb[:, b, lo], ALU.mult, ALU.mult)
                        dve.scalar_tensor_tensor(rot_b[:, REP, hi], k[:, lo], norm, kb[:, b, hi], ALU.mult, ALU.mult)\
                            .then_inc(ropek_parts, 1)
                        wait(dve, ropek_parts, s + 1)
                        dve.tensor_tensor(rot_k[:, :], rot_k[:, :], rot_b[:, REP, :], ALU.add)\
                            .then_inc(ropek_done, 1)

                    def split_cached_k(s):
                        wait(dve, kc_hi_done, s + 1)
                        dve.tensor_tensor(kt_lo[:, 0:L], turn_ps[0][:, :], kt_hi[:, 0:L].bitcast(F32), ALU.subtract)\
                            .then_inc(kc_lo_done, 1)

                    def split_q(s):
                        wait(dve, q_hi_done, s + 1)
                        dve.tensor_tensor(qt_lo[:, :], turn_ps[1][:, :], qt_hi[:, :].bitcast(F32), ALU.subtract)\
                            .then_inc(q_lo_done, 1)

                    def split_new_k(s):
                        wait(dve, kn_hi_done, s + 1)
                        dve.tensor_tensor(kt_lo[:, L:KEYS], turn_ps[0][:, 0:P], kt_hi[:, L:KEYS].bitcast(F32),
                                          ALU.subtract).then_inc(kn_lo_done, 1)

                    def maxima(s, b, heads):
                        def bias(h):
                            wait(dve, max_done[h], s + 1)
                            dve.scalar_tensor_tensor(shift[:, h:h + 1], row_max[:, h:h + 1], -1.0,
                                                     rstd[:, b % 2, h:h + 1], ALU.mult, ALU.mult)\
                                .then_inc(shift_done[h], 1)

                        for h in heads:
                            dve.wait_ge(setup_dve, MASK_READY)
                            if h == 0:
                                wait(dve, p_turned[NJ - 1], s - 1)
                            wait(dve, scored[h], s + 1)
                            dve.tensor_tensor_reduce(
                                probs[:, b % 2, h, :].rearrange("p (a k) -> p a k", a=2),
                                score_ps[h % 2][:, :].rearrange("p (a k) -> p a k", a=2)[:, :, 0:HALF],
                                mask[:, b, :].rearrange("p (a k) -> p a k", a=2),
                                1.0, -3e38, ALU.add, ALU.max, row_max[:, h:h + 1]).then_inc(max_done[h], 1)
                            if h:
                                bias(h - 1)
                        if h == REP - 1:
                            bias(h)

                    def normalise(s, b, heads):
                        if heads[0] == 0:
                            wait(dve, exp_done[REP - 1], s + 1)
                            dve.reciprocal(recips[:, :], sums[:, :]).then_inc(recip_done, 1)
                            wait(dve, recip_done, s + 1)
                        for h in heads:
                            row = probs[:, b % 2, h, :]
                            last = dve.tensor_scalar(row, row, recips[:, h:h + 1], None, ALU.mult)
                        if h == REP - 1:
                            last.then_inc(probs_done, 1)

                    def split_probs(s, b, j):
                        wait(dve, p_hi_done[j], s + 1)
                        at = (b + j) % 2
                        dve.tensor_tensor(pt_lo[:, at, :], turn_ps[1 - j % 2][:, :], pt_hi[:, at, :].bitcast(F32),
                                          ALU.subtract).then_inc(p_lo_done[j], 1)

                    def split_o(s):
                        wait(dve, o_hi_done, s + 1)
                        dve.tensor_tensor(ot_lo[:, :], value_ps[:, :], ot_hi[:, :].bitcast(F32), ALU.subtract)\
                            .then_inc(o_lo_done, 1)

                    def add_up(s, b):
                        wait(dve, o_projected, s + 1)
                        dve.tensor_tensor(acc[:, b, :], acc[:, b, :], proj_ps[:, :], ALU.add).then_inc(acc_added, 1)

                    def step(s, b, g):
                        b1, b2 = (b + 1) % B, (b + 2) % B
                        if live(s):
                            split_probs(s, b, 1)
                        if b == B - 3 and live(s + 3):
                            split_w(g + 1, 1)
                        if live(s + 2):
                            rotate_k(s + 2, b2)
                        if live(s):
                            split_probs(s, b, 2)
                            split_probs(s, b, 3)
                        if b == B - 3 and live(s + 3):
                            split_w(g + 1, 2)
                        if live(s + 1):
                            normalise(s + 1, b1, (0, 1))
                        if live(s):
                            split_probs(s, b, 4)
                        if b == 0:
                            split_wo(g, 0)
                        if live(s + 1):
                            normalise(s + 1, b1, (2, 3))
                        if live(s + 2):
                            split_cached_k(s + 2)
                        if live(s):
                            split_o(s)
                        if b == 0:
                            split_wo(g, 1)
                        if live(s + 3):
                            rotate_q(s + 3, (b + 3) % B)
                        if b == B - 4 and live(s + 4):
                            split_w(g + 1, 0)
                        if live(s + 2):
                            split_q(s + 2)
                            split_new_k(s + 2)
                        if live(s + 3):
                            add_q(s + 3, (b + 3) % B)
                        if live(s):
                            add_up(s, b)
                        if live(s + 2):
                            maxima(s + 2, b2, (0, 1))
                        if live(s + 1):
                            split_probs(s + 1, b1, 0)
                        if live(s + 2):
                            maxima(s + 2, b2, (2, 3))

                    def split_wg(s):
                        for k in WG_AT.get(s, ()):
                            dve.wait_ge(wg_hi_done, k + 1)
                            dve.tensor_tensor(wg_lo[:, k, :], wg_raw[:, k, :], wg_hi[:, k, :].bitcast(F32),
                                              ALU.subtract).then_inc(wg_lo_done, 1)

                    dve.memset(mask[:, :, L:KEYS], 0.0)
                    dve.memset(acc[:, :, :], 0.0).then_inc(acc_added, 1)
                    dve.wait_ge(const_in, 6 * 16)
                    link(dve.tensor_copy(lens_f[:, :], lens_i[:, :]))
                    link(dve.tensor_scalar(pos[:, :], lens_f[:, :], cst[:, C_PART:C_PART + 1], None, ALU.add))
                    shape = (P, B, D // 2)
                    link(dve.tensor_tensor(angle, pos[:, :].unsqueeze(2).broadcast_to(shape),
                                           cst[:, C_INV:C_INV + D // 2].unsqueeze(1).broadcast_to(shape), ALU.mult))
                    reduced(sines, 0)
                    reduced(cosines, 1)
                    assert links[0] == SINES_READY
                    for b in range(B):
                        last = dve.tensor_scalar(mask[:, b, 0:L], key_no, lens_f[:, b:b + 1], NEG, ALU.is_ge,
                                                 ALU.mult)
                    link(last)
                    dve.wait_ge(sines_done, 1)
                    for n, (ta, tb, factor) in enumerate(((qa, qb, 1.0), (ka, kb, float(D) ** 0.5))):
                        w_of = lambda half: qkw[:, n, half].unsqueeze(1).broadcast_to(shape)
                        dve.scalar_tensor_tensor(ta[:, :, lo], cosines, factor, w_of(lo), ALU.mult, ALU.mult)
                        dve.scalar_tensor_tensor(ta[:, :, hi], cosines, factor, w_of(hi), ALU.mult, ALU.mult)
                        dve.scalar_tensor_tensor(tb[:, :, lo], sines, -factor, w_of(hi), ALU.mult, ALU.mult)
                        last = dve.scalar_tensor_tensor(tb[:, :, hi], sines, factor, w_of(lo), ALU.mult, ALU.mult)
                    link(last)
                    dve.wait_ge(xt_hi_done, 1)
                    link(dve.tensor_tensor(xt_lo[:, :, :, :].rearrange("p b k t -> p (b k t)"), x_raw,
                                      xt_hi[:, :, :, :].rearrange("p b k t -> p (b k t)").bitcast(F32),
                                      ALU.subtract))
                    split_w(0, 0)
                    for s in range(-3, 0):
                        step(s, s % B, -1)
                    with dve.Fori(0, STEPS - B, B) as s0:
                        g = dve.snap(s0 // B)
                        for b in range(B):
                            step(s0 + b, b, g)
                    for b in range(B):
                        step(STEPS - B + b, b, HK - 1)
                        split_wg(STEPS - B + b)

        small_in = semaphore("small_in")
        wu_in = semaphore("wu_in")
        wd_in = semaphore("wd_in")
        wa_in = semaphore("wa_in")
        xn_in = semaphore("xn_in")
        out_done = semaphore("out_done")
        wu_hi_done = semaphore("wu_hi_done")
        wu_lo_done = semaphore("wu_lo_done")
        unpacked = semaphore("unpacked")
        c_copied = semaphore("c_copied")
        c_turned = semaphore("c_turned")
        ct_copied = semaphore("ct_copied")
        ct_hi_done = semaphore("ct_hi_done")
        ct_lo_done = semaphore("ct_lo_done")
        gated = semaphore("gated")
        upped = semaphore("upped")
        silu_done = semaphore("silu_done")
        abs_done = semaphore("abs_done")
        search = [semaphore(f"search{j}") for j in range(2)]
        key2_done = semaphore("key2_done")
        edges_done = semaphore("edges_done")
        sides_done = semaphore("sides_done")
        su_done = semaphore("su_done")
        h_done = semaphore("h_done")
        h_turned = [semaphore(f"h_turned{n}") for n in range(3)]
        h_copied = [semaphore(f"h_copied{n}") for n in range(3)]
        downed = semaphore("downed")
        down_copied = semaphore("down_copied")
        x1_done = semaphore("x1_done")
        x1_turned = semaphore("x1_turned")
        x1_copied = semaphore("x1_copied")
        adapted = semaphore("adapted")
        y_copied = semaphore("y_copied")
        y_turned = semaphore("y_turned")
        yt_copied = semaphore("yt_copied")
        yt_hi_done = semaphore("yt_hi_done")
        yt_lo_done = semaphore("yt_lo_done")
        int4_done = semaphore("int4_done")
        int4_scaled = semaphore("int4_scaled")
        x1b_done = semaphore("x1b_done")
        res_done = semaphore("res_done")

        with ExitStack() as phase2:
            sb = tensors(phase2)
            ps = lambda name, n: phase2.enter_context(nc.psum_tensor(name, [P, n], F32))
            gu_ps = [ps(f"gu_ps{j}", 1536) for j in range(2)]
            turn2_ps, out_ps = ps("turn2_ps", 512), ps("out_ps", 512)
            NF = len(FCH)
            sb("placed_by_hand", [P, 3, NK, FI])
            wu_lo = sb("wu_lo", [P, NK, FI], F32R)
            wu_raw = nc.alloc_sbuf_tensor_at("wu_raw", [P, NK, FI], F32, offset=aligned(nc.sbuf_base))
            wd_sb = sb("wd_sb", [P, NF, DM])
            wf = sb("wf", [P, 2, 2, DM], F32R)
            bias = sb("bias", [P, DM])
            scl = sb("scl", [P, 2])
            ids_sb = sb("ids_sb", [1, B], I32)
            wa_sb = sb("wa_sb", [P, NK, DM])
            pair = lambda name, shape, dt=F32: [sb(f"{name}{j}", shape, dt) for j in range(2)]
            s_sb = pair("s_sb", [P, FI])
            m_sb = pair("m_sb", [P, FI])
            key, key2, junk = (pair(n, [P, FI], U16) for n in ("key", "key2", "junk"))
            ct_hi, ct_lo = (pair(n, [P, DM], F32R) for n in ("ct_hi", "ct_lo"))
            tried, count, taken, high, low, room = (pair(n, [P, 1]) for n in
                                                    ("tried", "count", "taken", "high", "low", "room"))
            edge = pair("edge", [P, 2], U16)
            c_sb = sb("c_sb", [P, DM])
            ht = sb("ht", [P, NF, S])
            xn_sb = sb("xn_sb", [P, DM])
            x1 = sb("x1", [P, DM])
            y = sb("y", [P, DM])
            yt_hi, yt_lo = sb("yt_hi", [P, DM], F32R), sb("yt_lo", [P, DM], F32R)
            HT_JOBS = [FCH[0:4], FCH[4:8], FCH[8:]]
            pw_sb = ht[:, 0:2 * NK, :].rearrange("p (a k) t -> p a (k t)", a=2).bitcast(I32)
            nibble = m_sb[1][:, 0:2 * DM].rearrange("p (a n) -> p a n", a=2).bitcast(I32)
            bias_i = x1[:, :].rearrange("p (n t) -> p n t", t=2).bitcast(I32)
            pb_sb = y[:, 0:DM // 2].bitcast(I32)

            with nc.Block() as block:
                @block.sync
                def _(sp):
                    sp.dma_start(pw_sb[:, :, :], pw).then_inc(small_in, 16)
                    sp.dma_start(pb_sb[:, :], pb).then_inc(small_in, 16)
                    sp.dma_start(scl[:, :], scales).then_inc(small_in, 16)
                    sp.dma_start(ids_sb[:, :], ids).then_inc(small_in, 16)
                    sp.dma_start(wu_raw[:, :, :], wu).then_inc(wu_in, 16)
                    sp.wait_ge(small_in, 4 * 16)
                    for b in range(B):
                        adapter = sp.value_load(ids_sb[0:1, b:b + 1], min_val=0, max_val=wa.shape[0] - 1)
                        wait(sp, adapted, b)
                        sp.dma_start(wa_sb[:, :, :], wa[bass.ds(adapter, 1)].rearrange("o p k n -> p (o k) n"))\
                            .then_inc(wa_in, 16)
                        wait(sp, res_done, b)
                        sp.dma_start(xn_sb[:, :], xn[b * S:(b + 1) * S, :]).then_inc(xn_in, 16)
                        if b == 0:
                            last = FCH[-1][1]
                            sp.wait_ge(wu_lo_done, NK)
                            sp.dma_start(wd_sb[:, 0:NF - 1, :],
                                         wd[0:(NF - 1) * P, :].rearrange("(c p) n -> p c n", p=P)).then_inc(wd_in, 16)
                            sp.dma_start(wd_sb[0:last, NF - 1, :], wd[(NF - 1) * P:FI, :]).then_inc(wd_in, 16)
                        else:
                            sp.dma_start(out[(b - 1) * S:b * S, :], acc[:, b - 1, :]).then_inc(out_done, 16)
                    sp.wait_ge(res_done, B)
                    sp.dma_start(out[(B - 1) * S:B * S, :], acc[:, B - 1, :]).then_inc(out_done, 16)
                    sp.wait_ge(out_done, B * 16)

                @block.tensor
                def _(pe):
                    def front(i):
                        wait(pe, c_copied, i + 1)
                        for k in range(NK):
                            last = pe.transpose(turn2_ps[:, k * P:(k + 1) * P], c_sb[:, k * P:(k + 1) * P], ident)
                        last.then_inc(c_turned, 1)
                        wait(pe, ct_lo_done, i + 1)

                    def products(j, w, banks):
                        for at, n in banks:
                            for k in range(NK):
                                turn = slice(k * P, (k + 1) * P)
                                last = product3(pe, gu_ps[j][:, at:at + n], (ct_hi[j][:, turn], ct_lo[j][:, turn]),
                                                (w[0][:, k, at:at + n], w[1][:, k, at:at + n]), k == 0, k == NK - 1)
                        return last

                    def gate(i, j):
                        wait(pe, su_done, i - 1)
                        products(j, (wg_hi, wg_lo), BANKS3).then_inc(gated, 1)

                    def up(i, j, bank):
                        if bank == 0:
                            wait(pe, silu_done, i + 1)
                        last = products(j, (wu_hi, wu_lo), BANKS3[bank:bank + 1])
                        if bank == len(BANKS3) - 1:
                            last.then_inc(upped, 1)

                    def tail(i, j, more):
                        wait(pe, h_done, i + 1)
                        c = 0
                        for n, job in enumerate(HT_JOBS):
                            if n:
                                wait(pe, h_copied[n - 1], i + 1)
                            for m, (at, width) in enumerate(job):
                                last = pe.transpose(turn2_ps[0:width, m * P:(m + 1) * P], m_sb[j][:, at:at + width],
                                                    ident)
                            last.then_inc(h_turned[n], 1)
                            if more:
                                up(i + 2, j, n)
                        wait(pe, h_copied[2], i + 1)
                        for c, (at, width) in enumerate(FCH):
                            last = pe.matmul(out_ps[:, :], ht[0:width, c, :], wd_sb[0:width, c, :],
                                             start=(c == 0), stop=(c == NF - 1))
                        last.then_inc(downed, 1)
                        wait(pe, x1_done, i + 1)
                        for k in range(NK):
                            last = pe.transpose(turn2_ps[:, k * P:(k + 1) * P], x1[:, k * P:(k + 1) * P], ident)
                        last.then_inc(x1_turned, 1)
                        wait(pe, x1_copied, i + 1)
                        wait(pe, wa_in, (i + 1) * 16)
                        for k in range(NK):
                            last = pe.matmul(out_ps[:, :], x1[:, k * P:(k + 1) * P], wa_sb[:, k, :],
                                             start=(k == 0), stop=(k == NK - 1))
                        last.then_inc(adapted, 1)
                        wait(pe, y_copied, i + 1)
                        split = y[:, :].rearrange("p (a q r) -> p a r q", a=2, r=2)
                        for c in range(NK):
                            last = pe.transpose(turn2_ps[:, c * P:(c + 1) * P], split[:, c // 2, c % 2, :], ident)
                        last.then_inc(y_turned, 1)
                        wait(pe, yt_lo_done, i + 1)
                        for c in range(NK):
                            w = wf[:, c // 2, c % 2, :]
                            pe.matmul(out_ps[:, :], yt_hi[:, c * P:(c + 1) * P], w, start=(c == 0), stop=False)
                            last = pe.matmul(out_ps[:, :], yt_lo[:, c * P:(c + 1) * P], w, start=False,
                                             stop=(c == NK - 1))
                        last.then_inc(int4_done, 1)

                    def body(i0, more):
                        if more:
                            for j in range(2):
                                front(i0 + 2 + j)
                            for j in range(2):
                                gate(i0 + 2 + j, j)
                        for j in range(2):
                            tail(i0 + j, j, more)

                    for j in range(2):
                        front(j)
                        gate(j, j)
                    pe.wait_ge(wu_lo_done, NK)
                    for j in range(2):
                        for bank in range(len(BANKS3)):
                            up(j, j, bank)
                    pe.wait_ge(unpacked, UNPACKED)
                    pe.wait_ge(wd_in, 2 * 16)
                    with pe.Fori(0, B // 2 - 1) as p:
                        body(pe.snap(p * 2), True)
                    body(B - 2, False)

                @block.scalar
                def _(act):
                    def row(i):
                        return acc[:, i, :] if isinstance(i, int) else \
                            acc[:, bass.ds(i, 1), :].rearrange("p o n -> p (o n)")

                    def front(i, j):
                        wait(act, ct_lo_done, i)
                        act.activation(c_sb[:, :], row(i), ACT.Copy).then_inc(c_copied, 1)
                        wait(act, c_turned, i + 1)
                        act.activation(c_sb[:, :], turn2_ps[:, :], ACT.Copy).then_inc(ct_copied, 1)
                        wait(act, ct_copied, i + 1)
                        act.activation(ct_hi[j][:, :], c_sb[:, :], ACT.Copy).then_inc(ct_hi_done, 1)

                    def silu(i, j):
                        wait(act, gated, i + 1)
                        wait(act, h_done, i - 1)
                        act.activation(s_sb[j][:, :], gu_ps[j][:, 0:FI], ACT.Silu).then_inc(silu_done, 1)

                    def magnitudes(i, j):
                        wait(act, silu_done, i + 1)
                        act.activation(m_sb[j][:, :], s_sb[j][:, :], ACT.Abs).then_inc(abs_done, 1)

                    def sides(i, j):
                        wait(act, abs_done, i + 1)
                        wait(act, edges_done, i + 1)
                        act.activation(key[j][:, :].bitcast(BF16), m_sb[j][:, :], ACT.Sign,
                                       bias=edge[j][:, :].bitcast(F32), scale=-1.0).then_inc(sides_done, 1)

                    def copy_h(i):
                        c = 0
                        for n, job in enumerate(HT_JOBS):
                            wait(act, h_turned[n], i + 1)
                            full = sum(width == P for _, width in job)
                            last = act.activation(ht[:, c:c + full, :].rearrange("p c t -> p (c t)"),
                                                  turn2_ps[:, 0:full * P], ACT.Copy)
                            for m in range(full, len(job)):
                                width = job[m][1]
                                last = act.activation(ht[0:width, c + m, :], turn2_ps[0:width, m * P:(m + 1) * P],
                                                      ACT.Copy)
                            last.then_inc(h_copied[n], 1)
                            c += len(job)

                    def tail(i):
                        wait(act, downed, i + 1)
                        act.activation(x1[:, :], out_ps[:, :], ACT.Copy).then_inc(down_copied, 1)
                        wait(act, x1_turned, i + 1)
                        wait(act, x1b_done, i + 1)
                        act.activation(x1[:, :], turn2_ps[:, :], ACT.Copy).then_inc(x1_copied, 1)
                        wait(act, adapted, i + 1)
                        wait(act, res_done, i)
                        act.activation(y[:, :], out_ps[:, :], ACT.Copy).then_inc(y_copied, 1)
                        wait(act, y_turned, i + 1)
                        act.activation(y[:, :], turn2_ps[:, :], ACT.Copy).then_inc(yt_copied, 1)
                        wait(act, yt_copied, i + 1)
                        act.activation(yt_hi[:, :], y[:, :], ACT.Copy).then_inc(yt_hi_done, 1)
                        wait(act, int4_done, i + 1)
                        act.activation(y[:, :], out_ps[:, :], ACT.Copy, scale=scl[:, 0:1]).then_inc(int4_scaled, 1)

                    def body(i0, more):
                        if more:
                            for j in range(2):
                                front(i0 + 2 + j, j)
                        for j in range(2):
                            sides(i0 + j, j)
                        if more:
                            silu(i0 + 2, 0)
                        copy_h(i0)
                        if more:
                            magnitudes(i0 + 2, 0)
                            silu(i0 + 3, 1)
                        tail(i0)
                        copy_h(i0 + 1)
                        if more:
                            magnitudes(i0 + 3, 1)
                        tail(i0 + 1)

                    for j in range(2):
                        front(j, j)
                    silu(0, 0)
                    act.wait_ge(wu_in, 16)
                    for k in range(NK):
                        act.activation(wu_hi[:, k, :], wu_raw[:, k, :], ACT.Copy).then_inc(wu_hi_done, 1)
                    silu(1, 1)
                    act.wait_ge(small_in, 4 * 16)
                    act.wait_ge(unpacked, UNPACKED)
                    for j in range(2):
                        magnitudes(j, j)
                    with act.Fori(0, B // 2 - 1) as p:
                        body(act.snap(p * 2), True)
                    body(B - 2, False)

                @block.gpsimd
                def _(pool):
                    def front(i, j):
                        wait(pool, ct_hi_done, i + 1)
                        pool.tensor_tensor(ct_lo[j][:, :], c_sb[:, :], ct_hi[j][:, :].bitcast(F32), ALU.subtract)\
                            .then_inc(ct_lo_done, 1)

                    def tail(i):
                        wait(pool, down_copied, i + 1)
                        wait(pool, xn_in, (i + 1) * 16)
                        pool.tensor_tensor(x1[:, :], x1[:, :], xn_sb[:, :], ALU.add).then_inc(x1_done, 1)
                        wait(pool, x1_done, i + 1)
                        pool.tensor_tensor(xn_sb[:, :], x1[:, :], bias[:, :], ALU.add).then_inc(x1b_done, 1)
                        wait(pool, yt_hi_done, i + 1)
                        pool.tensor_tensor(yt_lo[:, :], y[:, :], yt_hi[:, :].bitcast(F32), ALU.subtract)\
                            .then_inc(yt_lo_done, 1)
                        wait(pool, int4_scaled, i + 1)
                        wait(pool, x1b_done, i + 1)
                        to = acc[:, i, :] if isinstance(i, int) else \
                            acc[:, bass.ds(i, 1), :].rearrange("p o n -> p (o n)")
                        pool.tensor_tensor(to, y[:, :], xn_sb[:, :], ALU.add).then_inc(res_done, 1)

                    def body(i0, more):
                        if more:
                            for j in range(2):
                                front(i0 + 2 + j, j)
                        for j in range(2):
                            tail(i0 + j)

                    for j in range(2):
                        front(j, j)
                    pool.wait_ge(unpacked, UNPACKED)
                    with pool.Fori(0, B // 2 - 1) as p:
                        body(pool.snap(p * 2), True)
                    body(B - 2, False)

                @block.vector
                def _(dve):
                    links = [0]

                    def link(instruction):
                        links[0] += 1
                        instruction.then_inc(unpacked, 1)
                        dve.wait_ge(unpacked, links[0])

                    def drop_lower_halves(i0, pair_no):
                        n = [0, 0]

                        def then(j, instruction):
                            n[j] += 1
                            instruction.then_inc(search[j], 1)

                        def after(j):
                            dve.wait_ge(search[j], pair_no * LINKS + (1 + n[j]))

                        def count_below(j, keys, threshold):
                            after(j)
                            then(j, dve.tensor_scalar(junk[j][:, :], keys[j][:, :], threshold[j][:, :], None, ALU.is_lt,
                                                      ALU.add, accum_out=count[j][:, :]))

                        def judge(j, below, bit):
                            after(j)
                            then(j, dve.tensor_scalar(taken[j][:, :], count[j][:, :], below[j], 2.0 ** bit,
                                                      ALU.is_lt, ALU.mult))

                        def try_next(j, bit, result):
                            after(j)
                            then(j, dve.scalar_tensor_tensor((tried if bit else result)[j][:, :], taken[j][:, :],
                                                             -(2.0 ** (bit - 1)) if bit else -1.0, tried[j][:, :],
                                                             ALU.add, ALU.add))

                        def descend(bits, keys, below, result):
                            for j in range(2):
                                after(j)
                                then(j, dve.memset(tried[j][:, :], 2.0 ** (bits - 1)))
                            for bit in range(bits - 1, -1, -1):
                                count_below(0, keys, tried)
                                if bit < bits - 1:
                                    try_next(1, bit + 1, result)
                                judge(0, below, bit)
                                count_below(1, keys, tried)
                                try_next(0, bit, result)
                                judge(1, below, bit)
                            try_next(1, 0, result)

                        halves = [s[:, :].bitcast(U16).rearrange("p (n t) -> p n t", t=2) for s in s_sb]
                        for j in range(2):
                            dve.wait_ge(silu_done, i0 + (j + 1))
                            after(j)
                            then(j, dve.tensor_scalar(key[j][:, :], halves[j][:, :, 1], 0x7FFF, None, ALU.bitwise_and))
                        descend(15, key, [DROP - 0.5] * 2, high)
                        for j in range(2):
                            count_below(j, key, high)
                        for j in range(2):
                            after(j)
                            then(j, dve.tensor_scalar(junk[j][:, :], key[j][:, :], high[j][:, :], 65535.0,
                                                      ALU.not_equal, ALU.mult))
                        for j in range(2):
                            after(j)
                            then(j, dve.tensor_scalar(room[j][:, :], count[j][:, :], -1.0, DROP - 0.5,
                                                      ALU.mult, ALU.add))
                            dve.tensor_tensor(key2[j][:, :], junk[j][:, :], halves[j][:, :, 0], ALU.max)\
                                .then_inc(key2_done, 1)
                        dve.wait_ge(key2_done, i0 + 2)
                        for j in range(2):
                            dve.wait_ge(abs_done, i0 + (j + 1))
                            dve.wait_ge(upped, i0 + (j + 1))
                            dve.tensor_tensor(s_sb[j][:, :], gu_ps[j][:, 0:FI], s_sb[j][:, :], ALU.mult)\
                                .then_inc(su_done, 1)
                        descend(16, key2, [r[:, :] for r in room], low)
                        for j in range(2):
                            count_below(j, key2, low)
                        for j in range(2):
                            after(j)
                            then(j, dve.scalar_tensor_tensor(room[j][:, :], count[j][:, :], -1.0, room[j][:, :],
                                                             ALU.mult, ALU.add))
                            dve.tensor_copy(edge[j][:, 0:1], low[j][:, :])
                            dve.tensor_copy(edge[j][:, 1:2], high[j][:, :]).then_inc(edges_done, 1)
                        for j in range(2):
                            side, equal, rank, kept = (t[j][:, :].bitcast(BF16) if t is not key2 else t[j][:, :]
                                                       for t in (key, junk, key2, junk))
                            dve.wait_ge(sides_done, i0 + (j + 1))
                            after(j)
                            then(j, dve.tensor_scalar(equal, side, 0.0, None, ALU.is_equal))
                            after(j)
                            then(j, dve.tensor_tensor_scan(rank, equal, equal, 0.0, ALU.add, ALU.bypass))
                            after(j)
                            then(j, dve.scalar_tensor_tensor(kept, rank, room[j][:, :], side, ALU.is_gt, ALU.subtract))
                            after(j)
                            dve.wait_ge(su_done, i0 + (j + 1))
                            dve.scalar_tensor_tensor(m_sb[j][:, :], kept, 0.0, s_sb[j][:, :], ALU.is_gt, ALU.mult)\
                                .then_inc(h_done, 1)
                        assert n == [LINKS, LINKS]

                    dve.wait_ge(small_in, 4 * 16)
                    for parity in range(2):
                        shift4 = 0 if parity else 4
                        link(dve.tensor_scalar(nibble[:, :, :], pw_sb[:, :, :], shift4, 15, ALU.arith_shift_right,
                                               ALU.bitwise_and))
                        link(dve.tensor_scalar(wf[:, :, parity, :], nibble[:, :, :], -8.0, None, ALU.add))
                        link(dve.tensor_scalar(bias_i[:, :, parity], pb_sb[:, :], shift4, 15, ALU.arith_shift_right,
                                               ALU.bitwise_and))
                    link(dve.tensor_scalar(bias[:, :], bias_i[:, :, :].rearrange("p n t -> p (n t)"), -8.0,
                                           scl[:, 1:2], ALU.add, ALU.mult))
                    assert links[0] == UNPACKED
                    for j in range(2):
                        dve.memset(taken[j][:, :], 0.0).then_inc(search[j], 1)
                    for k in range(NK):
                        dve.wait_ge(wu_hi_done, k + 1)
                        dve.tensor_tensor(wu_lo[:, k, :], wu_raw[:, k, :], wu_hi[:, k, :].bitcast(F32),
                                          ALU.subtract).then_inc(wu_lo_done, 1)
                    with dve.Fori(0, B // 2) as p:
                        drop_lower_halves(dve.snap(p * 2), p)


_INS = ["xt", "xn", "lens", "pages", "ids", "wqkv", "wo", "qw", "kw", "kc", "vc", "wg", "wu", "wd", "wa", "pw", "pb",
        "scales", "consts"]


def kernel(x, itok_Bx16_0_63, itok_B_207_1644, itok_B_1_14, L0_cond_Wq, L0_cond_Wk, L0_cond_Wv, L0_cond_Wo,
           L0_cond_q_norm_w, L0_cond_k_norm_w, L0_cond_k_cache, L0_cond_v_cache, L0_attn_w_gate, L0_attn_w_up,
           L0_attn_w_down, L0_cond2_weight, L0_ffn_packed_w, L0_ffn_packed_b, L0_ffn_scale_w, L0_ffn_scale_b):
    import numpy as np
    import concourse.bacc as bacc
    from concourse.bass_utils import run_bass_kernel_spmd

    x, pages, lens, ids = (np.asarray(a) for a in (x, itok_Bx16_0_63, itok_B_207_1644, itok_B_1_14))
    wq, wk, wv, wo = (np.asarray(a) for a in (L0_cond_Wq, L0_cond_Wk, L0_cond_Wv, L0_cond_Wo))
    by_head = [w.reshape(HK, -1, NK, P).transpose(0, 3, 2, 1) for w in (wq, wk, wv)]
    chunked = lambda w: np.asarray(w).T.reshape(NK, P, -1).transpose(1, 0, 2)
    consts = np.zeros((P, C_ALL), np.float32)
    consts[:, C_ID:C_ID + P] = np.eye(P)
    consts[:, C_INV:C_INV + D // 2] = 1.0 / 10000.0 ** (np.arange(0, D, 2) / D)
    consts[:, C_PART] = np.arange(P)
    consts[:, C_LANE] = np.arange(P) % PSIZE * HK
    consts[:, C_KEY:] = np.arange(L)
    arrays = dict(
        xt=x.reshape(B, S, NK, P).transpose(3, 0, 2, 1).reshape(P, -1),
        xn=x.reshape(B * S, DM),
        lens=np.broadcast_to(lens, (P, B)),
        pages=np.repeat(pages.reshape(B, NC, P // PSIZE).transpose(2, 0, 1).reshape(P // PSIZE, -1), PSIZE, axis=0),
        ids=ids.reshape(1, B),
        wqkv=np.concatenate(by_head, axis=3),
        wo=wo.reshape(DM, HK, REP, D).transpose(1, 3, 2, 0),
        qw=np.broadcast_to(np.asarray(L0_cond_q_norm_w), (P, D)),
        kw=np.broadcast_to(np.asarray(L0_cond_k_norm_w), (P, D)),
        kc=np.asarray(L0_cond_k_cache).reshape(-1, D),
        vc=np.asarray(L0_cond_v_cache).reshape(-1, D),
        wg=chunked(L0_attn_w_gate),
        wu=chunked(L0_attn_w_up),
        wd=np.asarray(L0_attn_w_down).T,
        wa=np.asarray(L0_cond2_weight).transpose(0, 2, 1).reshape(-1, NK, P, DM).transpose(0, 2, 1, 3),
        pw=np.asarray(L0_ffn_packed_w).reshape(DM, 2, P).transpose(2, 1, 0),
        pb=np.broadcast_to(np.asarray(L0_ffn_packed_b), (P, DM // 2)),
        scales=np.broadcast_to(np.stack([np.asarray(L0_ffn_scale_w), np.asarray(L0_ffn_scale_b)]), (P, 2)),
        consts=consts,
    )
    nc = bacc.Bacc("TRN2", target_bir_lowering=False, num_devices=1)
    arrays = {n: np.ascontiguousarray(arrays[n]) for n in _INS}
    args = [nc.dram_tensor(n, a.shape, mybir.dt.from_np(a.dtype), kind="ExternalInput").ap() for n, a in arrays.items()]
    out = nc.dram_tensor("out", (B * S, DM), F32, kind="ExternalOutput").ap()
    adaln_attn_ffn(nc, *args, out)
    r = run_bass_kernel_spmd(nc, [arrays], core_ids=[0])
    return r.results[0]["out"].reshape(B, S, DM)
```

```python
import math
from contextlib import ExitStack

import concourse.bass as bass
from concourse import mybir

F32 = mybir.dt.float32
F32R = mybir.dt.float32r
BF16 = mybir.dt.bfloat16
I32 = mybir.dt.int32
U32 = mybir.dt.uint32
U16 = mybir.dt.uint16
ALU = mybir.AluOpType
ACT = mybir.ActivationFunctionType

P = 128
B, S, DM = 8, 128, 512
D, HQ, HK = 128, 32, 8
REP = HQ // HK
PAGES, PSIZE, NPP = 64, 32, 16
L = NPP * PSIZE
KEYS = L + S
HALF = KEYS // 2
NK = DM // P
NC = L // P
NJ = KEYS // P
GQ = REP * D
GW = GQ + 2 * D
STEPS = HK * B
EPS = 1e-6
SOFTMAX_SCALE = float(D) ** -0.5
NEG = -1e30
FI = 1376
DROP = FI // 2
FCH = [(i * P, min(P, FI - i * P)) for i in range((FI + P - 1) // P)]
BANKS3 = [(0, 512), (512, 512), (1024, FI - 1024)]
ROUND = 1.5 * 2.0 ** 23
TWO_PI = (6.28125, 0.0019350051879882812, 3.0199157663446503e-07)
PI = 3.141592653589793
Q_CALLS = 3
W_PIECES = [(slice(0, 2), slice(0, GQ)), (slice(2, NK), slice(0, GQ)), (slice(0, NK), slice(GQ, GW))]
WO_HALVES = [slice(0, REP // 2), slice(REP // 2, REP)]
ALL_BANKS = range(len(BANKS3))
LAST_BANK = len(BANKS3) - 1
UNPACKED = 7
TOP = 16
SORT_LINKS, DESCENT_LINKS = 7, 2 + (1 + 3 * 16) + 1
TIE_LINKS = 4
LINKS = (1 + 1 + 3 * 15) + 4 + DESCENT_LINKS + 2 + TIE_LINKS
FLAGS = 3 + 5
WU_ON_DVE = (2, 3)
EARLY = 8
WG_AT = {STEPS - 3: (0, 1), STEPS - 2: (2, 3)}
FIRST = 3
SINES_READY = 10
TABLES_READY = SINES_READY + 1
MASK_READY = TABLES_READY + 1
PI_IN = 3.1415925
C_ID, C_INV, C_PART, C_LANE, C_RANK = 0, 128, 192, 193, 194
C_KEY = C_RANK + TOP
C_ALL = C_KEY + L


def live(s):
    return not isinstance(s, int) or 0 <= s < STEPS


def wait(eng, sem, n):
    if not isinstance(n, int) or n > 0:
        eng.wait_ge(sem, n)


def at_most(n):
    return min(n, STEPS) if isinstance(n, int) else n


def aligned(at):
    return -(-at // 32) * 32


def product3(pe, out, left, right, start, stop):
    pe.matmul(out, left[0], right[0], start=start, stop=False)
    pe.matmul(out, left[0], right[1], start=False, stop=False)
    return pe.matmul(out, left[1], right[0], start=False, stop=stop)


def adaln_attn_ffn(nc, xt, xn, lens, pages, ids, wqkv, wo, qw, kw, kc, vc, wg, wu, wd, wa, pw, pb, scales,
                   consts, out):
    with ExitStack() as whole:
        def semaphore(name):
            return whole.enter_context(nc.semaphore(name))

        def tensors(stack):
            return lambda name, shape, dt=F32: stack.enter_context(nc.sbuf_tensor(name, shape, dt))

        sb = tensors(whole)
        acc = sb("acc", [P, B, DM])
        cst = sb("cst", [P, C_KEY])
        ident = cst[:, C_ID:C_ID + P]

        const_in = semaphore("const_in")
        table_in = semaphore("table_in")
        x0_in = semaphore("x0_in")
        xt_in = semaphore("xt_in")
        w0_in = [semaphore(f"w0_in{n}") for n in range(3)]
        w_in = semaphore("w_in")
        wo_in = semaphore("wo_in")
        k_in = [semaphore(f"k_in{n}") for n in range(2)]
        v_in = [semaphore(f"v_in{n}") for n in range(2)]
        xt_hi_done = semaphore("xt_hi_done")
        x0_lo_done = semaphore("x0_lo_done")
        xt_lo_done = semaphore("xt_lo_done")
        w_hi_done = [semaphore(f"w_hi_done{n}") for n in range(3)]
        w_lo_done = [semaphore(f"w_lo_done{n}") for n in range(3)]
        wo_hi_done = semaphore("wo_hi_done")
        wo_lo_done = [semaphore(f"wo_lo_done{n}") for n in range(2)]
        setup_dve = semaphore("setup_dve")
        setup_pool = semaphore("setup_pool")
        sines_done = semaphore("sines_done")
        held = semaphore("held")
        idx_ready = semaphore("idx_ready")
        q_chunks = semaphore("q_chunks")
        kv_projected = semaphore("kv_projected")
        q_copied = semaphore("q_copied")
        kv_copied = semaphore("kv_copied")
        squares_done = semaphore("squares_done")
        eps_added = semaphore("eps_added")
        rstd_done = semaphore("rstd_done")
        ropeq_parts = semaphore("ropeq_parts")
        ropek_parts = semaphore("ropek_parts")
        ropeq_done = semaphore("ropeq_done")
        ropek_done = semaphore("ropek_done")
        kc_turned = semaphore("kc_turned")
        q_turned = semaphore("q_turned")
        kn_turned = semaphore("kn_turned")
        kc_hi_done = semaphore("kc_hi_done")
        q_hi_done = semaphore("q_hi_done")
        kn_hi_done = semaphore("kn_hi_done")
        kc_lo_done = semaphore("kc_lo_done")
        q_lo_done = semaphore("q_lo_done")
        kn_lo_done = semaphore("kn_lo_done")
        scored = [semaphore(f"scored{h}") for h in range(REP)]
        max_done = [semaphore(f"max_done{h}") for h in range(REP)]
        shift_done = [semaphore(f"shift_done{h}") for h in range(REP)]
        exp_done = [semaphore(f"exp_done{h}") for h in range(REP)]
        recip_done = semaphore("recip_done")
        probs_done = semaphore("probs_done")
        p_turned = [semaphore(f"p_turned{j}") for j in range(NJ)]
        p_hi_done = [semaphore(f"p_hi_done{j}") for j in range(NJ)]
        p_lo_done = [semaphore(f"p_lo_done{j}") for j in range(NJ)]
        v_hi_done = semaphore("v_hi_done")
        v_lo_done = semaphore("v_lo_done")
        valued = semaphore("valued")
        o_hi_done = semaphore("o_hi_done")
        o_lo_done = semaphore("o_lo_done")
        o_projected = semaphore("o_projected")
        acc_added = semaphore("acc_added")

        wg_in = semaphore("wg_in")
        wg_hi_done = semaphore("wg_hi_done")
        wg_lo_done = semaphore("wg_lo_done")
        early = aligned(nc.sbuf_base)
        wg_hi, wg_lo, wu_hi = (nc.alloc_sbuf_tensor_at(name, [P, NK, FI], F32R, offset=early + n * NK * FI * 4)
                               for n, name in enumerate(("wg_hi", "wg_lo", "wu_hi")))
        wg_raw = nc.alloc_sbuf_tensor_at("wg_raw", [P, NK, FI], F32, offset=early + 2 * NK * FI * 4)

        with ExitStack() as phase1:
            sb = tensors(phase1)
            ps = lambda name, n: phase1.enter_context(nc.psum_tensor(name, [P, n], F32))
            proj_ps = ps("proj_ps", 512)
            turn_ps = [ps("turn_ps0", 512), ps("turn_ps1", 512)]
            score_ps = [ps("score_ps0", 1024), ps("score_ps1", 1024)]
            value_ps = ps("value_ps", 512)

            xt_hi = sb("xt_hi", [P, B, NK, S], F32R)
            xt_lo = sb("xt_lo", [P, B, NK, S], F32R)
            w_raw = sb("w_raw", [P, NK, GW])
            w_hi = sb("w_hi", [P, NK, GW], F32R)
            w_lo = sb("w_lo", [P, NK, GW], F32R)
            wo_raw = sb("wo_raw", [P, REP, DM])
            wo_hi = sb("wo_hi", [P, REP, DM], F32R)
            wo_lo = sb("wo_lo", [P, REP, DM], F32R)
            mask = sb("mask", [P, B, KEYS], BF16)
            qa = sb("qa", [P, B, D])
            qb = sb("qb", [P, B, D])
            ka = sb("ka", [P, B, D])
            kb = sb("kb", [P, B, D])
            kg = sb("kg", [P, 2, NC, D])
            vg = sb("vg", [P, 2, NC, D])
            vn = sb("vn", [P, 4, D])
            v_hi = sb("v_hi", [P, 2, NJ, D], F32R)
            v_lo = sb("v_lo", [P, 2, NJ, D], F32R)
            qk = sb("qk", [P, REP + 1, D])
            rot_q = sb("rot_q", [P, 2, REP, D])
            rot_k = sb("rot_k", [P, D])
            rot_b = sb("rot_b", [P, REP + 1, D])
            kt_hi = sb("kt_hi", [P, KEYS], F32R)
            kt_lo = sb("kt_lo", [P, KEYS], F32R)
            qt_hi = sb("qt_hi", [P, GQ], F32R)
            qt_lo = sb("qt_lo", [P, GQ], F32R)
            probs = sb("probs", [P, 2, REP, KEYS])
            pt_hi = sb("pt_hi", [P, 2, GQ], F32R)
            pt_lo = sb("pt_lo", [P, 2, GQ], F32R)
            ot_hi = sb("ot_hi", [P, GQ], F32R)
            ot_lo = sb("ot_lo", [P, GQ], F32R)
            ss = sb("ss", [P, REP + 1])
            ss_eps = sb("ss_eps", [P, REP + 1])
            power = sb("power", [P, REP + 1])
            eps = sb("eps", [P, REP + 1])
            rstd = sb("rstd", [P, 2, REP + 1])
            row_max = sb("row_max", [P, REP])
            shift = sb("shift", [P, REP])
            sums = sb("sums", [P, REP])
            recips = sb("recips", [P, REP])
            lens_i = sb("lens_i", [P, B], I32)
            pages_i = sb("pages_i", [P, B * NC], I32)
            idx = sb("idx", [P, B * NC], U32)
            x_raw = probs[:, :, :, :].rearrange("p a h k -> p (a h k)")[:, 0:B * NK * S]\
                .rearrange("p (b k t) -> p b k t", b=B, k=NK)
            angle = wo_raw[:, 0, :].rearrange("p (b f) -> p b f", b=B)
            trig = wo_raw[:, 2:4, :].rearrange("p t (b f) -> p t b f", b=B)
            sines, cosines = trig[:, 0, :, :], trig[:, 1, :, :]
            turns = vg[:, :, :, :].rearrange("p t c d -> p t (c d)").rearrange("p t (b f) -> p t b f", b=B)
            squared = sb("squared", [P, REP + 1, D], BF16)
            pos = sb("pos", [P, B])
            lens_f = sb("lens_f", [P, B])
            qkw = rot_b[:, 0:2, :]
            key_no = rot_q[:, 0, 0:NC, :].rearrange("p c d -> p (c d)")

            with nc.Block() as block:
                @block.sync
                def _(sp):
                    xt_b = xt.rearrange("p (b k t) -> p b k t", b=B, k=NK)
                    sp.dma_start(cst[:, :], consts[:, 0:C_KEY]).then_inc(const_in, 16)
                    sp.dma_start(lens_i[:, :], lens).then_inc(const_in, 16)
                    sp.dma_start(x_raw[:, 0, :, :], xt_b[:, 0, :, :]).then_inc(x0_in, 16)
                    for n, (ks, cols) in enumerate(W_PIECES):
                        sp.dma_start(w_raw[:, ks, cols], wqkv[0, :, ks, cols]).then_inc(w0_in[n], 16)
                    sp.dma_start(qkw[:, 0, :], qw).then_inc(table_in, 16)
                    sp.dma_start(qkw[:, 1, :], kw).then_inc(table_in, 16)
                    sp.dma_start(pages_i[:, :], pages).then_inc(table_in, 16)
                    sp.dma_start(key_no, consts[:, C_KEY:C_ALL]).then_inc(table_in, 16)
                    sp.dma_start(x_raw[:, 1:B, :, :], xt_b[:, 1:B, :, :]).then_inc(xt_in, 16)
                    sp.wait_ge(setup_dve, TABLES_READY)
                    sp.dma_start(wo_raw[:, :, :], wo[0]).then_inc(wo_in, 16)
                    with sp.Fori(1, HK) as g:
                        for n in range(len(W_PIECES)):
                            sp.wait_ge(w_lo_done[n], g)
                        sp.dma_start(w_raw[:, :, :], wqkv[bass.ds(g, 1)].rearrange("o p k n -> p (o k) n"))\
                            .then_inc(w_in, 16)
                        for n in range(len(WO_HALVES)):
                            sp.wait_ge(wo_lo_done[n], g)
                        sp.dma_start(wo_raw[:, :, :], wo[bass.ds(g, 1)].rearrange("o p h n -> p (o h) n"))\
                            .then_inc(wo_in, 16)
                    sp.wait_ge(kv_projected, STEPS)
                    sp.dma_start(wg_raw[:, :, :], wg).then_inc(wg_in, 16)

                @block.gpsimd
                def _(pool):
                    pool.memset(power[:, :], -0.5).then_inc(setup_pool, 1)
                    pool.memset(eps[:, :], D * EPS).then_inc(setup_pool, 1)
                    pool.wait_ge(xt_hi_done, 1)
                    pool.tensor_tensor(xt_lo[:, 0, :, :], x_raw[:, 0, :, :], xt_hi[:, 0, :, :].bitcast(F32),
                                       ALU.subtract).then_inc(x0_lo_done, 1)
                    for n, (ks, cols) in enumerate(W_PIECES):
                        pool.wait_ge(w_hi_done[n], 1)
                        pool.tensor_tensor(w_lo[:, ks, cols], w_raw[:, ks, cols], w_hi[:, ks, cols].bitcast(F32),
                                           ALU.subtract).then_inc(w_lo_done[n], 1)
                    pool.wait_ge(const_in, 2 * 16)
                    pool.wait_ge(table_in, 4 * 16)
                    pool.tensor_scalar(idx[:, :], pages_i[:, :], float(PSIZE * HK), cst[:, C_LANE:C_LANE + 1],
                                       ALU.mult, ALU.add).then_inc(idx_ready, 1)

                    def hold(waits):
                        for sem, n in waits:
                            wait(pool, sem, n)
                        pool.sem_inc(held, 1)

                    def gather_k(s, b, g):
                        if b == 0 and not (isinstance(g, int) and g == 0):
                            hold([(place, s // 2 * (NC * 16)) for place in k_in + v_in])
                            pool.tensor_scalar(idx[:, :], idx[:, :], 1.0, None, ALU.add).then_inc(idx_ready, 1)
                        hold([(idx_ready, g + 1), (kc_turned, s - 1)])
                        for c in range(NC):
                            pool.indirect_dma_start(
                                kg[:, b % 2, c, :], None, kc,
                                bass.IndirectOffsetOnAxis(ap=idx[:, b * NC + c:b * NC + c + 1], axis=0))\
                                .then_inc(k_in[b % 2], 16)

                    def gather_v(s, b):
                        hold([(v_lo_done, s - 1)])
                        for c in range(NC):
                            pool.indirect_dma_start(
                                vg[:, b % 2, c, :], None, vc,
                                bass.IndirectOffsetOnAxis(ap=idx[:, b * NC + c:b * NC + c + 1], axis=0))\
                                .then_inc(v_in[b % 2], 16)

                    def split_v(s, b):
                        wait(pool, v_hi_done, s + 1)
                        pool.tensor_tensor(v_lo[:, b % 2, 0:NC, :], vg[:, b % 2, :, :],
                                           v_hi[:, b % 2, 0:NC, :].bitcast(F32), ALU.subtract)
                        pool.tensor_tensor(v_lo[:, b % 2, NC, :], vn[:, b % 4, :],
                                           v_hi[:, b % 2, NC, :].bitcast(F32), ALU.subtract).then_inc(v_lo_done, 1)

                    def norms(s, b):
                        wait(pool, squares_done, s + 1)
                        pool.tensor_tensor(ss_eps[:, :], ss[:, :], eps[:, :], ALU.add).then_inc(eps_added, 1)
                        wait(pool, eps_added, s + 1)
                        wait(pool, exp_done[REP - 1], s - 1)
                        pool.tensor_tensor(rstd[:, b % 2, :], ss_eps[:, :], power[:, :], ALU.pow)\
                            .then_inc(rstd_done, 1)

                    def step(s, b, g):
                        b1, b2, b3 = (b + 1) % B, (b + 2) % B, (b + 3) % B
                        if live(s + 2):
                            gather_v(s + 2, b2)
                        if live(s + 3):
                            gather_k(s + 3, b3, g + (b + 3) // B)
                            norms(s + 3, b3)
                        if live(s + 1):
                            split_v(s + 1, b1)

                    pool.wait_ge(setup_pool, 2)
                    for s in range(-3, 0):
                        if s == -2:
                            pool.wait_ge(setup_dve, SINES_READY)
                        step(s, s % B, -1)
                    with pool.Fori(0, STEPS - B, B) as s0:
                        g = pool.snap(s0 // B)
                        for b in range(B):
                            step(s0 + b, b, g)
                    for b in range(B):
                        step(STEPS - B + b, b, HK - 1)

                @block.tensor
                def _(pe):
                    def pair(hi, lo, at):
                        return hi[at], lo[at]

                    def project_q(s, b, g, ks):
                        if b == 0 and ks[0] in (0, 2):
                            wait(pe, w_lo_done[ks[0] // 2], g + 1)
                        if ks[0] == 0:
                            wait(pe, kv_copied, s)
                            wait(pe, acc_added, s - 2)
                            if isinstance(s, int) and s < FIRST:
                                wait(pe, xt_lo_done, s)
                                wait(pe, x0_lo_done, 1)
                        for k in ks:
                            last = product3(pe, proj_ps[:, :], (xt_hi[:, b, k, :], xt_lo[:, b, k, :]),
                                            (w_hi[:, k, 0:GQ], w_lo[:, k, 0:GQ]), k == 0, k == NK - 1)
                        last.then_inc(q_chunks, 1)

                    def project_kv(s, b, g):
                        if b == 0:
                            wait(pe, w_lo_done[2], g + 1)
                        wait(pe, q_copied, s + 1)
                        for k in range(NK):
                            last = product3(pe, proj_ps[:, 0:2 * D], (xt_hi[:, b, k, :], xt_lo[:, b, k, :]),
                                            (w_hi[:, k, GQ:GW], w_lo[:, k, GQ:GW]), k == 0, k == NK - 1)
                        last.then_inc(kv_projected, 1)

                    def turn_cached_k(s, b):
                        wait(pe, p_lo_done[3], s - 1)
                        wait(pe, k_in[b % 2], (s // 2 + 1) * (NC * 16))
                        for c in range(NC):
                            last = pe.transpose(turn_ps[0][:, c * P:(c + 1) * P], kg[:, b % 2, c, :], ident)
                        last.then_inc(kc_turned, 1)

                    def turn_q(s, b):
                        wait(pe, p_lo_done[4], s - 1)
                        wait(pe, ropeq_done, s + 1)
                        for h in range(REP):
                            last = pe.transpose(turn_ps[1][:, h * P:(h + 1) * P], rot_q[:, b % 2, h, :], ident)
                        last.then_inc(q_turned, 1)

                    def turn_new_k(s):
                        wait(pe, kc_lo_done, s + 1)
                        wait(pe, ropek_done, s + 1)
                        pe.transpose(turn_ps[0][:, 0:P], rot_k[:, :], ident).then_inc(kn_turned, 1)

                    def scores(s, heads):
                        if heads[0] == 0:
                            wait(pe, q_lo_done, s + 1)
                            wait(pe, kn_lo_done, s + 1)
                        for h in heads:
                            wait(pe, max_done[(h + 2) % REP], s if h < 2 else s + 1)
                            for a in range(2):
                                last = product3(pe, score_ps[h % 2][:, 512 * a:512 * a + HALF],
                                                (qt_hi[:, h * P:(h + 1) * P], qt_lo[:, h * P:(h + 1) * P]),
                                                (kt_hi[:, a * HALF:(a + 1) * HALF], kt_lo[:, a * HALF:(a + 1) * HALF]),
                                                True, True)
                            last.then_inc(scored[h], 1)

                    def turn_probs(s, b, j):
                        if j == 0:
                            wait(pe, probs_done, s + 1)
                            wait(pe, q_lo_done, at_most(s + 2))
                        elif j == 1:
                            wait(pe, kn_lo_done, at_most(s + 2))
                        else:
                            wait(pe, p_lo_done[j - 2], s + 1)
                        for h in range(REP):
                            last = pe.transpose(turn_ps[1 - j % 2][:, h * P:(h + 1) * P],
                                                probs[:, b % 2, h, j * P:(j + 1) * P], ident)
                        last.then_inc(p_turned[j], 1)

                    def values(s, b, j):
                        if j == 0:
                            wait(pe, v_lo_done, s + 1)
                        wait(pe, p_lo_done[j], s + 1)
                        at = (b + j) % 2
                        last = product3(pe, value_ps[:, :], (v_hi[:, b % 2, j, :], v_lo[:, b % 2, j, :]),
                                        (pt_hi[:, at, :], pt_lo[:, at, :]), j == 0, j == NJ - 1)
                        if j == NJ - 1:
                            last.then_inc(valued, 1)

                    def project_o(s, b, g):
                        wait(pe, kv_copied, at_most(s + 4))
                        wait(pe, o_lo_done, s + 1)
                        for h in range(REP):
                            if b == 0 and h % 2 == 0:
                                wait(pe, wo_lo_done[h // 2], g + 1)
                            at = slice(h * P, (h + 1) * P)
                            last = product3(pe, proj_ps[:, :], (ot_hi[:, at], ot_lo[:, at]),
                                            (wo_hi[:, h, :], wo_lo[:, h, :]), h == 0, h == REP - 1)
                        last.then_inc(o_projected, 1)

                    def step(s, b, g):
                        b1, b2, b3 = (b + 1) % B, (b + 2) % B, (b + 3) % B
                        g3 = g + (b + 3) // B
                        if live(s):
                            turn_probs(s, b, 1)
                        if live(s + 3):
                            project_q(s + 3, b3, g3, (0, 1))
                        if live(s):
                            values(s, b, 0)
                            turn_probs(s, b, 2)
                            values(s, b, 1)
                            turn_probs(s, b, 3)
                        if live(s + 3):
                            project_q(s + 3, b3, g3, (2,))
                        if live(s):
                            values(s, b, 2)
                            turn_probs(s, b, 4)
                            values(s, b, 3)
                        if live(s + 3):
                            project_q(s + 3, b3, g3, (3,))
                        if live(s + 2):
                            turn_cached_k(s + 2, b2)
                        if live(s):
                            values(s, b, 4)
                        if live(s + 3):
                            project_kv(s + 3, b3, g3)
                        if live(s + 2):
                            turn_q(s + 2, b2)
                            turn_new_k(s + 2)
                        if live(s):
                            project_o(s, b, g)
                        if live(s + 2):
                            scores(s + 2, (0, 1))
                        if live(s + 1):
                            turn_probs(s + 1, b1, 0)
                        if live(s + 2):
                            scores(s + 2, (2, 3))

                    pe.wait_ge(const_in, 2 * 16)
                    for s in range(-3, 0):
                        step(s, s % B, -1)
                    pe.wait_ge(xt_lo_done, FIRST)
                    with pe.Fori(0, STEPS - B, B) as s0:
                        g = pe.snap(s0 // B)
                        for b in range(B):
                            step(s0 + b, b, g)
                    for b in range(B):
                        step(STEPS - B + b, b, HK - 1)

                @block.scalar
                def _(act):
                    def split_w(g, n):
                        ks, cols = W_PIECES[n]
                        if isinstance(g, int) and g == 0:
                            act.wait_ge(w0_in[n], 16)
                        else:
                            wait(act, w_in, g * 16)
                        if n < 2:
                            wait(act, q_chunks, g * (B * Q_CALLS) - (0 if n else Q_CALLS - 1))
                        else:
                            wait(act, kv_projected, g * B)
                        act.activation(w_hi[:, ks, cols], w_raw[:, ks, cols], ACT.Copy).then_inc(w_hi_done[n], 1)

                    def split_wo(g):
                        wait(act, wo_in, (g + 1) * 16)
                        wait(act, o_projected, g * B)
                        act.activation(wo_hi[:, :, :], wo_raw[:, :, :], ACT.Copy).then_inc(wo_hi_done, 1)

                    def copy_q(s):
                        wait(act, q_chunks, (s + 1) * Q_CALLS)
                        wait(act, ropeq_done, s)
                        wait(act, squares_done, s)
                        act.activation(qk[:, 0:REP, :].rearrange("p h d -> p (h d)"), proj_ps[:, :], ACT.Copy)\
                            .then_inc(q_copied, 1)

                    def copy_kv(s, b):
                        wait(act, kv_projected, s + 1)
                        wait(act, ropek_done, s)
                        act.activation(qk[:, REP, :], proj_ps[:, 0:D], ACT.Copy)
                        act.activation(vn[:, b % 4, :], proj_ps[:, D:2 * D], ACT.Copy).then_inc(kv_copied, 1)

                    def split_v(s, b):
                        wait(act, v_in[b % 2], (s // 2 + 1) * (NC * 16))
                        wait(act, kv_copied, s + 1)
                        act.activation(v_hi[:, b % 2, 0:NC, :], vg[:, b % 2, :, :], ACT.Copy)
                        act.activation(v_hi[:, b % 2, NC, :], vn[:, b % 4, :], ACT.Copy).then_inc(v_hi_done, 1)

                    def squares(s):
                        wait(act, eps_added, s)
                        wait(act, q_copied, s + 1)
                        wait(act, kv_copied, s + 1)
                        for h in range(REP + 1):
                            last = act.activation(squared[:, h, :], qk[:, h, :], ACT.Square, accum_out=ss[:, h:h + 1])
                        last.then_inc(squares_done, 1)

                    def split_cached_k(s):
                        wait(act, kc_turned, s + 1)
                        act.activation(kt_hi[:, 0:L], turn_ps[0][:, :], ACT.Copy).then_inc(kc_hi_done, 1)

                    def split_q(s):
                        wait(act, q_turned, s + 1)
                        act.activation(qt_hi[:, :], turn_ps[1][:, :], ACT.Copy).then_inc(q_hi_done, 1)

                    def split_new_k(s):
                        wait(act, kn_turned, s + 1)
                        act.activation(kt_hi[:, L:KEYS], turn_ps[0][:, 0:P], ACT.Copy).then_inc(kn_hi_done, 1)

                    def exps(s, b, heads):
                        if heads[0] == 0:
                            wait(act, recip_done, s)
                        for h in heads:
                            wait(act, shift_done[h], s + 1)
                            row = probs[:, b % 2, h, :]
                            act.activation(row, row, ACT.Exp, bias=shift[:, h:h + 1],
                                           scale=rstd[:, b % 2, h:h + 1], accum_out=sums[:, h:h + 1])\
                                .then_inc(exp_done[h], 1)

                    def split_probs(s, b, j):
                        wait(act, p_turned[j], s + 1)
                        act.activation(pt_hi[:, (b + j) % 2, :], turn_ps[1 - j % 2][:, :], ACT.Copy)\
                            .then_inc(p_hi_done[j], 1)

                    def split_o(s):
                        wait(act, valued, s + 1)
                        act.activation(ot_hi[:, :], value_ps[:, :], ACT.Copy).then_inc(o_hi_done, 1)

                    def step(s, b, g):
                        b1, b2, b3 = (b + 1) % B, (b + 2) % B, (b + 3) % B
                        next_w = b == B - 4 and live(s + 4)
                        if live(s):
                            split_probs(s, b, 1)
                        if live(s + 1):
                            exps(s + 1, b1, (1, 2))
                        if live(s):
                            split_probs(s, b, 2)
                        if live(s + 1):
                            exps(s + 1, b1, (3,))
                        if live(s):
                            split_probs(s, b, 3)
                        if next_w:
                            split_w(g + 1, 0)
                        if live(s):
                            split_probs(s, b, 4)
                        if live(s + 3):
                            copy_q(s + 3)
                        if live(s + 2):
                            split_cached_k(s + 2)
                        if live(s):
                            split_o(s)
                        if live(s + 3):
                            copy_kv(s + 3, b3)
                        if live(s + 2):
                            split_q(s + 2)
                            split_new_k(s + 2)
                        if live(s + 3):
                            squares(s + 3)
                        if next_w:
                            split_w(g + 1, 1)
                        if live(s + 1):
                            split_v(s + 1, b1)
                        if next_w:
                            split_w(g + 1, 2)
                        if b == B - 1 and live(s + 1):
                            split_wo(g + 1)
                        if live(s + 1):
                            split_probs(s + 1, b1, 0)
                        if live(s + 2):
                            exps(s + 2, b2, (0,))

                    def split_wg(s):
                        for k in WG_AT.get(s, ()):
                            act.wait_ge(wg_in, 16)
                            act.activation(wg_hi[:, k, :], wg_raw[:, k, :], ACT.Copy).then_inc(wg_hi_done, 1)

                    def split_x(bs):
                        act.activation(xt_hi[:, bs, :, :], x_raw[:, bs, :, :], ACT.Copy).then_inc(xt_hi_done, 1)

                    act.wait_ge(x0_in, 16)
                    split_x(0)
                    for n in range(len(W_PIECES)):
                        split_w(0, n)
                    act.wait_ge(setup_dve, SINES_READY)
                    act.activation(trig, trig, ACT.Sin).then_inc(sines_done, 1)
                    act.wait_ge(xt_in, 16)
                    for b in range(1, FIRST):
                        split_x(b)
                    for s in range(-3, 0):
                        step(s, s % B, -1)
                        if s == -3:
                            split_x(slice(FIRST, B))
                    with act.Fori(0, STEPS - B, B) as s0:
                        g = act.snap(s0 // B)
                        for b in range(B):
                            step(s0 + b, b, g)
                    for b in range(B):
                        step(STEPS - B + b, b, HK - 1)
                        split_wg(STEPS - B + b)

                @block.vector
                def _(dve):
                    links = [0]

                    def link(instruction):
                        links[0] += 1
                        instruction.then_inc(setup_dve, 1)
                        dve.wait_ge(setup_dve, links[0])

                    def split_w(g, n):
                        ks, cols = W_PIECES[n]
                        wait(dve, w_hi_done[n], g + 1)
                        dve.tensor_tensor(w_lo[:, ks, cols], w_raw[:, ks, cols], w_hi[:, ks, cols].bitcast(F32),
                                          ALU.subtract).then_inc(w_lo_done[n], 1)

                    def split_wo(g, n):
                        hs = WO_HALVES[n]
                        wait(dve, wo_hi_done, g + 1)
                        dve.tensor_tensor(wo_lo[:, hs, :], wo_raw[:, hs, :], wo_hi[:, hs, :].bitcast(F32), ALU.subtract)\
                            .then_inc(wo_lo_done[n], 1)

                    def over_heads(table):
                        return table.unsqueeze(1).broadcast_to((P, REP, table.shape[-1]))

                    lo, hi = slice(0, D // 2), slice(D // 2, D)

                    def rotate_q(s, b):
                        wait(dve, q_copied, s + 1)
                        wait(dve, ropeq_done, s)
                        wait(dve, q_turned, s - 1)
                        q = qk[:, 0:REP, :]
                        dve.tensor_tensor(rot_q[:, b % 2, :, :], q, over_heads(qa[:, b, :]), ALU.mult)
                        dve.tensor_tensor(rot_b[:, 0:REP, lo], q[:, :, hi], over_heads(qb[:, b, lo]), ALU.mult)
                        dve.tensor_tensor(rot_b[:, 0:REP, hi], q[:, :, lo], over_heads(qb[:, b, hi]), ALU.mult)\
                            .then_inc(ropeq_parts, 1)

                    def add_q(s, b):
                        wait(dve, ropeq_parts, s + 1)
                        dve.tensor_tensor(rot_q[:, b % 2, :, :], rot_q[:, b % 2, :, :], rot_b[:, 0:REP, :], ALU.add)\
                            .then_inc(ropeq_done, 1)

                    def rotate_k(s, b):
                        wait(dve, kn_turned, s)
                        wait(dve, kv_copied, s + 1)
                        wait(dve, rstd_done, s + 1)
                        k, norm = qk[:, REP, :], rstd[:, b % 2, REP:REP + 1]
                        dve.scalar_tensor_tensor(rot_k[:, :], k, norm, ka[:, b, :], ALU.mult, ALU.mult)
                        dve.scalar_tensor_tensor(rot_b[:, REP, lo], k[:, hi], norm, kb[:, b, lo], ALU.mult, ALU.mult)
                        dve.scalar_tensor_tensor(rot_b[:, REP, hi], k[:, lo], norm, kb[:, b, hi], ALU.mult, ALU.mult)\
                            .then_inc(ropek_parts, 1)
                        wait(dve, ropek_parts, s + 1)
                        dve.tensor_tensor(rot_k[:, :], rot_k[:, :], rot_b[:, REP, :], ALU.add)\
                            .then_inc(ropek_done, 1)

                    def split_cached_k(s):
                        wait(dve, kc_hi_done, s + 1)
                        dve.tensor_tensor(kt_lo[:, 0:L], turn_ps[0][:, :], kt_hi[:, 0:L].bitcast(F32), ALU.subtract)\
                            .then_inc(kc_lo_done, 1)

                    def split_q(s):
                        wait(dve, q_hi_done, s + 1)
                        dve.tensor_tensor(qt_lo[:, :], turn_ps[1][:, :], qt_hi[:, :].bitcast(F32), ALU.subtract)\
                            .then_inc(q_lo_done, 1)

                    def split_new_k(s):
                        wait(dve, kn_hi_done, s + 1)
                        dve.tensor_tensor(kt_lo[:, L:KEYS], turn_ps[0][:, 0:P], kt_hi[:, L:KEYS].bitcast(F32),
                                          ALU.subtract).then_inc(kn_lo_done, 1)

                    def maxima(s, b, heads):
                        def bias(h):
                            wait(dve, max_done[h], s + 1)
                            dve.scalar_tensor_tensor(shift[:, h:h + 1], row_max[:, h:h + 1], -1.0,
                                                     rstd[:, b % 2, h:h + 1], ALU.mult, ALU.mult)\
                                .then_inc(shift_done[h], 1)

                        for h in heads:
                            dve.wait_ge(setup_dve, MASK_READY)
                            if h == 0:
                                wait(dve, p_turned[NJ - 1], s - 1)
                            wait(dve, scored[h], s + 1)
                            dve.tensor_tensor_reduce(
                                probs[:, b % 2, h, :].rearrange("p (a k) -> p a k", a=2),
                                score_ps[h % 2][:, :].rearrange("p (a k) -> p a k", a=2)[:, :, 0:HALF],
                                mask[:, b, :].rearrange("p (a k) -> p a k", a=2),
                                1.0, -3e38, ALU.add, ALU.max, row_max[:, h:h + 1]).then_inc(max_done[h], 1)
                            if h:
                                bias(h - 1)
                        if h == REP - 1:
                            bias(h)

                    def normalise(s, b, heads):
                        if heads[0] == 0:
                            wait(dve, exp_done[REP - 1], s + 1)
                            dve.reciprocal(recips[:, :], sums[:, :]).then_inc(recip_done, 1)
                            wait(dve, recip_done, s + 1)
                        for h in heads:
                            row = probs[:, b % 2, h, :]
                            last = dve.tensor_scalar(row, row, recips[:, h:h + 1], None, ALU.mult)
                        if h == REP - 1:
                            last.then_inc(probs_done, 1)

                    def split_probs(s, b, j):
                        wait(dve, p_hi_done[j], s + 1)
                        at = (b + j) % 2
                        dve.tensor_tensor(pt_lo[:, at, :], turn_ps[1 - j % 2][:, :], pt_hi[:, at, :].bitcast(F32),
                                          ALU.subtract).then_inc(p_lo_done[j], 1)

                    def split_o(s):
                        wait(dve, o_hi_done, s + 1)
                        dve.tensor_tensor(ot_lo[:, :], value_ps[:, :], ot_hi[:, :].bitcast(F32), ALU.subtract)\
                            .then_inc(o_lo_done, 1)

                    def add_up(s, b):
                        wait(dve, o_projected, s + 1)
                        dve.tensor_tensor(acc[:, b, :], acc[:, b, :], proj_ps[:, :], ALU.add).then_inc(acc_added, 1)

                    def step(s, b, g):
                        b1, b2 = (b + 1) % B, (b + 2) % B
                        next_w = b == B - 3 and live(s + 3) and not (isinstance(s, int) and s < 0)
                        if live(s):
                            split_probs(s, b, 1)
                        if next_w:
                            split_w(g + 1, 1)
                        if live(s + 2):
                            rotate_k(s + 2, b2)
                        if live(s):
                            split_probs(s, b, 2)
                            split_probs(s, b, 3)
                        if next_w:
                            split_w(g + 1, 2)
                        if live(s + 1):
                            normalise(s + 1, b1, (0, 1))
                        if live(s):
                            split_probs(s, b, 4)
                        if b == 0:
                            split_wo(g, 0)
                        if live(s + 1):
                            normalise(s + 1, b1, (2, 3))
                        if live(s + 2):
                            split_cached_k(s + 2)
                        if live(s):
                            split_o(s)
                        if b == 0:
                            split_wo(g, 1)
                        if live(s + 3):
                            rotate_q(s + 3, (b + 3) % B)
                        if b == B - 4 and live(s + 4):
                            split_w(g + 1, 0)
                        if live(s + 2):
                            split_q(s + 2)
                            split_new_k(s + 2)
                        if live(s + 3):
                            add_q(s + 3, (b + 3) % B)
                        if live(s):
                            add_up(s, b)
                        if live(s + 2):
                            maxima(s + 2, b2, (0, 1))
                        if live(s + 1):
                            split_probs(s + 1, b1, 0)
                        if live(s + 2):
                            maxima(s + 2, b2, (2, 3))

                    def split_wg(s):
                        for k in WG_AT.get(s, ()):
                            dve.wait_ge(wg_hi_done, k + 1)
                            dve.tensor_tensor(wg_lo[:, k, :], wg_raw[:, k, :], wg_hi[:, k, :].bitcast(F32),
                                              ALU.subtract).then_inc(wg_lo_done, 1)

                    dve.memset(mask[:, :, L:KEYS], 0.0)
                    dve.memset(acc[:, 0:B // 2, :], 0.0)
                    dve.wait_ge(const_in, 2 * 16)
                    link(dve.tensor_copy(lens_f[:, :], lens_i[:, :]))
                    link(dve.tensor_scalar(pos[:, :], lens_f[:, :], cst[:, C_PART:C_PART + 1], None, ALU.add))
                    shape = (P, B, D // 2)
                    link(dve.tensor_tensor(angle, pos[:, :].unsqueeze(2).broadcast_to(shape),
                                           cst[:, C_INV:C_INV + D // 2].unsqueeze(1).broadcast_to(shape), ALU.mult))
                    dve.tensor_scalar(turns[:, 0, :, :], angle, 1 / (2 * PI), None, ALU.mult)
                    link(dve.tensor_scalar(turns[:, 1, :, :], angle, 1 / (2 * PI), 0.25, ALU.mult, ALU.add))
                    link(dve.tensor_scalar(turns, turns, ROUND, ROUND, ALU.add, ALU.subtract))
                    for t in range(2):
                        last = dve.scalar_tensor_tensor(trig[:, t, :, :], turns[:, t, :, :], -TWO_PI[0], angle,
                                                        ALU.mult, ALU.add)
                    link(last)
                    link(dve.scalar_tensor_tensor(trig, turns, -TWO_PI[1], trig, ALU.mult, ALU.add))
                    link(dve.scalar_tensor_tensor(trig, turns, -TWO_PI[2], trig, ALU.mult, ALU.add))
                    link(dve.tensor_scalar(cosines, cosines, 0.5 * PI, None, ALU.add))
                    link(dve.tensor_scalar(trig, trig, PI_IN, -PI_IN, ALU.min, ALU.max))
                    dve.memset(acc[:, B // 2:B, :], 0.0).then_inc(acc_added, 1)
                    assert links[0] == SINES_READY
                    dve.wait_ge(table_in, 4 * 16)
                    dve.wait_ge(sines_done, 1)
                    for n, (ta, tb, factor) in enumerate(((qa, qb, 1.0), (ka, kb, float(D) ** 0.5))):
                        w_of = lambda half: qkw[:, n, half].unsqueeze(1).broadcast_to(shape)
                        dve.scalar_tensor_tensor(ta[:, :, lo], cosines, factor, w_of(lo), ALU.mult, ALU.mult)
                        dve.scalar_tensor_tensor(ta[:, :, hi], cosines, factor, w_of(hi), ALU.mult, ALU.mult)
                        dve.scalar_tensor_tensor(tb[:, :, lo], sines, -factor, w_of(hi), ALU.mult, ALU.mult)
                        last = dve.scalar_tensor_tensor(tb[:, :, hi], sines, factor, w_of(lo), ALU.mult, ALU.mult)
                    link(last)
                    assert links[0] == TABLES_READY

                    def split_x(bs, n):
                        dve.wait_ge(xt_hi_done, n + 1)
                        dve.tensor_tensor(xt_lo[:, bs, :, :], x_raw[:, bs, :, :], xt_hi[:, bs, :, :].bitcast(F32),
                                          ALU.subtract).then_inc(xt_lo_done, 1)

                    for b in range(1, FIRST):
                        split_x(b, b)
                    for b in range(B):
                        last = dve.tensor_scalar(mask[:, b, 0:L], key_no, lens_f[:, b:b + 1], NEG, ALU.is_ge,
                                                 ALU.mult)
                    link(last)
                    assert links[0] == MASK_READY
                    for s in range(-3, 0):
                        step(s, s % B, -1)
                        if s == -3:
                            split_x(slice(FIRST, B), FIRST)
                            dve.wait_ge(xt_lo_done, FIRST)
                            dve.wait_ge(x0_lo_done, 1)
                    with dve.Fori(0, STEPS - B, B) as s0:
                        g = dve.snap(s0 // B)
                        for b in range(B):
                            step(s0 + b, b, g)
                    for b in range(B):
                        step(STEPS - B + b, b, HK - 1)
                        split_wg(STEPS - B + b)

        small_in = semaphore("small_in")
        wu_in = semaphore("wu_in")
        wd_in = semaphore("wd_in")
        wa_in = semaphore("wa_in")
        xn_in = semaphore("xn_in")
        out_done = semaphore("out_done")
        wu_hi_done = semaphore("wu_hi_done")
        wu_lo_done = semaphore("wu_lo_done")
        unpacked = semaphore("unpacked")
        c_copied = semaphore("c_copied")
        c_turned = semaphore("c_turned")
        ct_copied = semaphore("ct_copied")
        ct_hi_done = semaphore("ct_hi_done")
        ct_lo_done = semaphore("ct_lo_done")
        gated = semaphore("gated")
        upped = semaphore("upped")
        silu_done = semaphore("silu_done")
        abs_done = semaphore("abs_done")
        search = [semaphore(f"search{j}") for j in range(2)]
        flags = semaphore("flags")
        held_dve = semaphore("held_dve")
        edges_done = semaphore("edges_done")
        sides_done = semaphore("sides_done")
        su_done = semaphore("su_done")
        h_done = semaphore("h_done")
        h_turned = [semaphore(f"h_turned{n}") for n in range(3)]
        h_copied = [semaphore(f"h_copied{n}") for n in range(3)]
        downed = semaphore("downed")
        down_copied = semaphore("down_copied")
        x1_done = semaphore("x1_done")
        x1_turned = semaphore("x1_turned")
        x1_copied = semaphore("x1_copied")
        wa_last_in = semaphore("wa_last_in")
        xn_last_in = semaphore("xn_last_in")
        adapted = semaphore("adapted")
        y_copied = semaphore("y_copied")
        y_turned = semaphore("y_turned")
        yt_copied = semaphore("yt_copied")
        yt_hi_done = semaphore("yt_hi_done")
        yt_lo_done = semaphore("yt_lo_done")
        int4_done = semaphore("int4_done")
        int4_scaled = semaphore("int4_scaled")
        x1b_done = semaphore("x1b_done")
        res_done = semaphore("res_done")

        with ExitStack() as phase2:
            sb = tensors(phase2)
            ps = lambda name, n: phase2.enter_context(nc.psum_tensor(name, [P, n], F32))
            gu_ps = [ps(f"gu_ps{j}", 1536) for j in range(2)]
            turn2_ps, out_ps = ps("turn2_ps", 512), ps("out_ps", 512)
            NF = len(FCH)
            sb("placed_by_hand", [P, 3, NK, FI])
            wu_lo = sb("wu_lo", [P, NK, FI], F32R)
            wu_raw = nc.alloc_sbuf_tensor_at("wu_raw", [P, NK, FI], F32, offset=aligned(nc.sbuf_base))
            wd_sb = sb("wd_sb", [P, NF, DM])
            wf = sb("wf", [P, 2, 2, DM], F32R)
            bias = sb("bias", [P, DM])
            scl = sb("scl", [P, 2])
            ids_sb = sb("ids_sb", [1, B], I32)
            wa_sb = sb("wa_sb", [P, NK, DM])
            pair = lambda name, shape, dt=F32: [sb(f"{name}{j}", shape, dt) for j in range(2)]
            s_sb = pair("s_sb", [P, FI])
            m_sb = pair("m_sb", [P, FI])
            key_junk = pair("key_junk", [P, 2, FI], U16)
            key, junk = ([t[:, n, :] for t in key_junk] for n in range(2))
            sorting = [t[:, :, :].rearrange("p n k -> p (n k)").bitcast(F32) for t in key_junk]
            key2 = [t[:, :] for t in pair("key2", [P, FI], U16)]
            ct_hi, ct_lo = (pair(n, [P, DM], F32R) for n in ("ct_hi", "ct_lo"))
            tried, count, taken, reach, high, low, room = (pair(n, [P, 1]) for n in
                                                    ("tried", "count", "taken", "reach", "high", "low", "room"))
            edge = pair("edge", [P, 2], U16)
            top = pair("top", [P, TOP])
            chosen = pair("chosen", [P, TOP])
            many, many_turned = sb("many", [P, 32]), sb("many_turned", [P, 32])
            any_many = sb("any_many", [P, 1], I32)
            c_sb = sb("c_sb", [P, DM])
            ht = sb("ht", [P, NF, S])
            xn_sb = sb("xn_sb", [P, DM])
            x1 = sb("x1", [P, DM])
            y = sb("y", [P, DM])
            yt_hi, yt_lo = sb("yt_hi", [P, DM], F32R), sb("yt_lo", [P, DM], F32R)
            HT_JOBS = [FCH[0:4], FCH[4:8], FCH[8:]]
            ALL_JOBS = range(len(HT_JOBS))
            last_at = [early]

            def with_last(t, name, shape, dt=F32):
                own = nc.alloc_sbuf_tensor_at(name + "_last", [P, *shape], dt, offset=last_at[0])
                last_at[0] = aligned(last_at[0] + math.prod(shape) * 4)
                return [t, own]

            hts = with_last(ht, "ht", [NF, S])
            xns, x1s, ys = (with_last(t, n, [DM]) for t, n in ((xn_sb, "xn"), (x1, "x1"), (y, "y")))
            yt_his, yt_los = (with_last(t, n, [DM], F32R) for t, n in ((yt_hi, "yt_hi"), (yt_lo, "yt_lo")))
            was = with_last(wa_sb, "wa", [NK, DM])
            assert last_at[0] <= early + 2 * NK * FI * 4
            turn_pss = [turn2_ps[:, :], gu_ps[0][:, 0:512]]
            out_pss = [out_ps[:, :], gu_ps[0][:, 512:1024]]

            def h_ps(n, j, t):
                return (out_pss if j == 1 and t == 0 and n != 1 else turn_pss)[t]

            pw_sb = ht[:, 0:2 * NK, :].rearrange("p (a k) t -> p a (k t)", a=2).bitcast(I32)
            nibble = m_sb[1][:, 0:2 * DM].rearrange("p (a n) -> p a n", a=2).bitcast(I32)
            first_lows = [ht[:, :, :].rearrange("p c t -> p (c t)").bitcast(U16)[:, j * FI:(j + 1) * FI]
                          for j in range(2)]
            bias_i = x1[:, :].rearrange("p (n t) -> p n t", t=2).bitcast(I32)
            pb_sb = y[:, 0:DM // 2].bitcast(I32)

            first_ps = [turn2_ps, out_ps]
            first_ct = [c_sb[:, :], s_sb[1][:, 0:DM]]
            warm = sb("warm", [P, 1])

            def split_up(eng, k):
                eng.wait_ge(wu_hi_done, k + 1)
                eng.tensor_tensor(wu_lo[:, k, :], wu_raw[:, k, :], wu_hi[:, k, :].bitcast(F32), ALU.subtract)\
                    .then_inc(wu_lo_done, 1)

            with nc.Block() as block:
                @block.sync
                def _(sp):
                    sp.dma_start(pw_sb[:, :, :], pw).then_inc(small_in, 16)
                    sp.dma_start(pb_sb[:, :], pb).then_inc(small_in, 16)
                    sp.dma_start(scl[:, :], scales).then_inc(small_in, 16)
                    sp.dma_start(ids_sb[:, :], ids).then_inc(small_in, 16)
                    sp.dma_start(wu_raw[:, :, :], wu).then_inc(wu_in, 16)
                    sp.wait_ge(small_in, 4 * 16)
                    for b in range(B):
                        adapter = sp.value_load(ids_sb[0:1, b:b + 1], min_val=0, max_val=wa.shape[0] - 1)
                        t = int(b == B - 1)
                        if t:
                            sp.wait_ge(gated, B)
                        else:
                            wait(sp, adapted, b)
                        sp.dma_start(was[t][:, :, :], wa[bass.ds(adapter, 1)].rearrange("o p k n -> p (o k) n"))\
                            .then_inc(wa_last_in if t else wa_in, 16)
                        if not t:
                            wait(sp, res_done, b)
                        sp.dma_start(xns[t][:, :], xn[b * S:(b + 1) * S, :]).then_inc(xn_last_in if t else xn_in, 16)
                        if b == 0:
                            last = FCH[-1][1]
                            sp.wait_ge(wu_lo_done, NK)
                            sp.dma_start(wd_sb[:, 0:NF - 1, :],
                                         wd[0:(NF - 1) * P, :].rearrange("(c p) n -> p c n", p=P)).then_inc(wd_in, 16)
                            sp.dma_start(wd_sb[0:last, NF - 1, :], wd[(NF - 1) * P:FI, :]).then_inc(wd_in, 16)
                        else:
                            sp.wait_ge(res_done, b)
                            sp.dma_start(out[(b - 1) * S:b * S, :], acc[:, b - 1, :]).then_inc(out_done, 16)
                    sp.wait_ge(res_done, B)
                    sp.dma_start(out[(B - 1) * S:B * S, :], acc[:, B - 1, :]).then_inc(out_done, 16)
                    sp.wait_ge(out_done, B * 16)

                @block.tensor
                def _(pe):
                    def front(i):
                        wait(pe, c_copied, i - 1)
                        for k in range(NK):
                            last = pe.transpose(turn2_ps[:, k * P:(k + 1) * P], c_sb[:, k * P:(k + 1) * P], ident)
                        last.then_inc(c_turned, 1)

                    def products(j, w, bank):
                        at, n = BANKS3[bank]
                        for k in range(NK):
                            turn = slice(k * P, (k + 1) * P)
                            last = product3(pe, gu_ps[j][:, at:at + n], (ct_hi[j][:, turn], ct_lo[j][:, turn]),
                                            (w[0][:, k, at:at + n], w[1][:, k, at:at + n]), k == 0, k == NK - 1)
                        return last

                    def gate(i, j, banks):
                        for bank in banks:
                            if bank == 0:
                                wait(pe, ct_lo_done, i + 1)
                                wait(pe, su_done, i - 1)
                            last = products(j, (wg_hi, wg_lo), bank)
                        if bank == LAST_BANK:
                            last.then_inc(gated, 1)

                    def up(i, j, banks):
                        for bank in banks:
                            if bank == 0:
                                wait(pe, silu_done, i + 1)
                            last = products(j, (wu_hi, wu_lo), bank)
                        if bank == LAST_BANK:
                            last.then_inc(upped, 1)

                    def turn_h(i, j, n, t=0):
                        if n == 0:
                            wait(pe, h_done, i + 1)
                            if not t and j == 0:
                                wait(pe, yt_copied, i)
                        elif t or j == 0:
                            wait(pe, h_copied[n - 1], i + 1)
                        elif n == 1:
                            wait(pe, yt_copied, i)
                        else:
                            wait(pe, h_copied[0], i + 1)
                        to = h_ps(n, j, t)
                        for m, (at, width) in enumerate(HT_JOBS[n]):
                            last = pe.transpose(to[0:width, m * P:(m + 1) * P], m_sb[j][:, at:at + width], ident)
                        last.then_inc(h_turned[n], 1)

                    def down(i, t=0, chunks=range(NF)):
                        if chunks[0] == 0:
                            wait(pe, h_copied[2], i + 1)
                            if not t:
                                wait(pe, int4_scaled, i)
                        for c in chunks:
                            width = FCH[c][1]
                            last = pe.matmul(out_pss[t], hts[t][0:width, c, :], wd_sb[0:width, c, :],
                                             start=(c == 0), stop=(c == NF - 1))
                        if chunks[-1] == NF - 1:
                            last.then_inc(downed, 1)

                    def turn_x1(i, t=0):
                        wait(pe, x1_done, i + 1)
                        for k in range(NK):
                            turn = slice(k * P, (k + 1) * P)
                            last = pe.transpose(turn_pss[t][:, turn], x1s[t][:, turn], ident)
                        last.then_inc(x1_turned, 1)

                    def adapter(i, t=0):
                        wait(pe, x1_copied, i + 1)
                        if t:
                            pe.wait_ge(wa_last_in, 16)
                        else:
                            wait(pe, wa_in, (i + 1) * 16)
                        for k in range(NK):
                            last = pe.matmul(out_pss[t], x1s[t][:, k * P:(k + 1) * P], was[t][:, k, :],
                                             start=(k == 0), stop=(k == NK - 1))
                        last.then_inc(adapted, 1)

                    def turn_y(i, t=0):
                        wait(pe, y_copied, i + 1)
                        split = ys[t][:, :].rearrange("p (a q r) -> p a r q", a=2, r=2)
                        for c in range(NK):
                            last = pe.transpose(turn_pss[t][:, c * P:(c + 1) * P], split[:, c // 2, c % 2, :], ident)
                        last.then_inc(y_turned, 1)

                    def int4(i, t=0):
                        wait(pe, yt_lo_done, i + 1)
                        for c in range(NK):
                            w, turn = wf[:, c // 2, c % 2, :], slice(c * P, (c + 1) * P)
                            pe.matmul(out_pss[t], yt_his[t][:, turn], w, start=(c == 0), stop=False)
                            last = pe.matmul(out_pss[t], yt_los[t][:, turn], w, start=False, stop=(c == NK - 1))
                        last.then_inc(int4_done, 1)

                    def body(i0, gates):
                        for n in ALL_JOBS:
                            turn_h(i0, 0, n)
                            up(i0 + 2, 0, (n,))
                        down(i0)
                        up(i0 + 3, 1, (0,))
                        turn_x1(i0)
                        up(i0 + 3, 1, (1,))
                        adapter(i0)
                        up(i0 + 3, 1, (2,))
                        turn_y(i0)
                        for n in ALL_JOBS:
                            turn_h(i0 + 1, 1, n)
                        wait(pe, h_copied[2], i0 + 2)
                        int4(i0)
                        if gates:
                            front(i0 + 4)
                        down(i0 + 1)
                        if gates:
                            wait(pe, ct_copied, i0 + 5)
                            front(i0 + 5)
                            gate(i0 + 4, 0, (0,))
                            wait(pe, ct_copied, i0 + 6)
                        turn_x1(i0 + 1)
                        if gates:
                            gate(i0 + 4, 0, (1,))
                        adapter(i0 + 1)
                        if gates:
                            gate(i0 + 4, 0, (2,))
                        turn_y(i0 + 1)
                        if gates:
                            gate(i0 + 5, 1, (0, 1))
                        int4(i0 + 1)
                        if gates:
                            gate(i0 + 5, 1, (2,))

                    def last_pair(a, b):
                        for n in ALL_JOBS:
                            turn_h(a, 0, n)
                            turn_h(b, 1, n, 1)
                        down(a)
                        down(b, 1, range(NF // 2))
                        turn_x1(a)
                        down(b, 1, range(NF // 2, NF))
                        adapter(a)
                        turn_x1(b, 1)
                        turn_y(a)
                        adapter(b, 1)
                        int4(a)
                        turn_y(b, 1)
                        int4(b, 1)

                    for j in range(2):
                        for k in range(NK):
                            last = pe.transpose(first_ps[j][:, k * P:(k + 1) * P], acc[:, j, k * P:(k + 1) * P], ident)
                        last.then_inc(c_turned, 1)
                    for j in range(2):
                        gate(j, j, ALL_BANKS)
                    pe.wait_ge(wu_lo_done, NK)
                    for j in range(2):
                        up(j, j, ALL_BANKS)
                    for j in range(2):
                        front(2 + j)
                        wait(pe, ct_copied, 2 + j + 1)
                        gate(2 + j, j, ALL_BANKS)
                    pe.wait_ge(unpacked, UNPACKED)
                    pe.wait_ge(wd_in, 2 * 16)
                    with pe.Fori(0, B // 2 - 2) as p:
                        body(pe.snap(p * 2), True)
                    body(B - 4, False)
                    last_pair(B - 2, B - 1)

                @block.scalar
                def _(act):
                    def row(i):
                        return acc[:, i, :] if isinstance(i, int) else \
                            acc[:, bass.ds(i, 1), :].rearrange("p o n -> p (o n)")

                    def copy_c(i):
                        wait(act, ct_lo_done, i)
                        act.activation(c_sb[:, :], row(i), ACT.Copy).then_inc(c_copied, 1)

                    def front(i, j):
                        wait(act, c_turned, i + 1)
                        act.activation(c_sb[:, :], turn2_ps[:, :], ACT.Copy).then_inc(ct_copied, 1)
                        wait(act, ct_copied, i + 1)
                        act.activation(ct_hi[j][:, :], c_sb[:, :], ACT.Copy).then_inc(ct_hi_done, 1)

                    def silu(i, j):
                        wait(act, gated, i + 1)
                        wait(act, h_done, i - 1)
                        act.activation(s_sb[j][:, :], gu_ps[j][:, 0:FI], ACT.Silu).then_inc(silu_done, 1)

                    def magnitudes(i, j):
                        wait(act, silu_done, i + 1)
                        act.activation(m_sb[j][:, :], s_sb[j][:, :], ACT.Abs).then_inc(abs_done, 1)

                    def sides(i, j):
                        wait(act, abs_done, i + 1)
                        wait(act, edges_done, i + 1)
                        act.activation(key[j].bitcast(BF16), m_sb[j][:, :], ACT.Sign,
                                       bias=edge[j][:, :].bitcast(F32), scale=-1.0).then_inc(sides_done, 1)

                    def copy_h(i, j, jobs, t=0):
                        for n in jobs:
                            job, c, to = HT_JOBS[n], 4 * n, h_ps(n, j, t)
                            wait(act, h_turned[n], i + 1)
                            full = sum(width == P for _, width in job)
                            last = act.activation(hts[t][:, c:c + full, :].rearrange("p c t -> p (c t)"),
                                                  to[:, 0:full * P], ACT.Copy)
                            for m in range(full, len(job)):
                                width = job[m][1]
                                last = act.activation(hts[t][0:width, c + m, :], to[0:width, m * P:(m + 1) * P], ACT.Copy)
                            last.then_inc(h_copied[n], 1)

                    def copy_down(i, t=0):
                        wait(act, downed, i + 1)
                        act.activation(x1s[t][:, :], out_pss[t], ACT.Copy).then_inc(down_copied, 1)

                    def copy_x1(i, t=0):
                        wait(act, x1_turned, i + 1)
                        wait(act, x1b_done, i + 1)
                        act.activation(x1s[t][:, :], turn_pss[t], ACT.Copy).then_inc(x1_copied, 1)

                    def copy_y(i, t=0):
                        wait(act, adapted, i + 1)
                        if not t:
                            wait(act, res_done, i)
                        act.activation(ys[t][:, :], out_pss[t], ACT.Copy).then_inc(y_copied, 1)

                    def split_y(i, t=0):
                        wait(act, y_turned, i + 1)
                        act.activation(ys[t][:, :], turn_pss[t], ACT.Copy).then_inc(yt_copied, 1)
                        wait(act, yt_copied, i + 1)
                        act.activation(yt_his[t][:, :], ys[t][:, :], ACT.Copy).then_inc(yt_hi_done, 1)

                    def scale_int4(i, t=0):
                        wait(act, int4_done, i + 1)
                        act.activation(ys[t][:, :], out_pss[t], ACT.Copy, scale=scl[:, 0:1]).then_inc(int4_scaled, 1)

                    def body(i0, gates):
                        copy_h(i0, 0, ALL_JOBS)
                        magnitudes(i0 + 2, 0)
                        copy_down(i0)
                        copy_x1(i0)
                        copy_y(i0)
                        split_y(i0)
                        if gates:
                            copy_c(i0 + 4)
                        copy_h(i0 + 1, 1, ALL_JOBS)
                        scale_int4(i0)
                        if gates:
                            front(i0 + 4, 0)
                        magnitudes(i0 + 3, 1)
                        if gates:
                            copy_c(i0 + 5)
                        copy_down(i0 + 1)
                        if gates:
                            front(i0 + 5, 1)
                        copy_x1(i0 + 1)
                        for j in range(2):
                            sides(i0 + 2 + j, j)
                        copy_y(i0 + 1)
                        split_y(i0 + 1)
                        if gates:
                            silu(i0 + 4, 0)
                        scale_int4(i0 + 1)
                        if gates:
                            silu(i0 + 5, 1)

                    def last_pair(a, b):
                        for n in ALL_JOBS:
                            copy_h(a, 0, (n,))
                            copy_h(b, 1, (n,), 1)
                        copy_down(a)
                        copy_x1(a)
                        copy_down(b, 1)
                        copy_y(a)
                        copy_x1(b, 1)
                        split_y(a)
                        copy_y(b, 1)
                        scale_int4(a)
                        split_y(b, 1)
                        scale_int4(b, 1)

                    act.activation(warm[:, :], cst[:, C_PART:C_PART + 1], ACT.Silu)
                    for j in range(2):
                        wait(act, c_turned, j + 1)
                        act.activation(first_ct[j], first_ps[j][:, :], ACT.Copy).then_inc(ct_copied, 1)
                        wait(act, ct_copied, j + 1)
                        act.activation(ct_hi[j][:, :], first_ct[j], ACT.Copy).then_inc(ct_hi_done, 1)
                    silu(0, 0)
                    magnitudes(0, 0)
                    act.wait_ge(wu_in, 16)
                    for k in range(NK):
                        act.activation(wu_hi[:, k, :], wu_raw[:, k, :], ACT.Copy).then_inc(wu_hi_done, 1)
                    silu(1, 1)
                    act.wait_ge(small_in, 4 * 16)
                    act.wait_ge(unpacked, UNPACKED)
                    magnitudes(1, 1)
                    for j in range(2):
                        copy_c(2 + j)
                        front(2 + j, j)
                    for j in range(2):
                        sides(j, j)
                    for j in range(2):
                        silu(2 + j, j)
                    with act.Fori(0, B // 2 - 2) as p:
                        body(act.snap(p * 2), True)
                    body(B - 4, False)
                    last_pair(B - 2, B - 1)

                @block.gpsimd
                def _(pool):
                    def front(i, j):
                        wait(pool, ct_hi_done, i + 1)
                        pool.tensor_tensor(ct_lo[j][:, :], c_sb[:, :], ct_hi[j][:, :].bitcast(F32), ALU.subtract)\
                            .then_inc(ct_lo_done, 1)

                    def add_x(i, t=0):
                        wait(pool, down_copied, i + 1)
                        if t:
                            pool.wait_ge(xn_last_in, 16)
                        else:
                            wait(pool, xn_in, (i + 1) * 16)
                        pool.tensor_tensor(x1s[t][:, :], x1s[t][:, :], xns[t][:, :], ALU.add).then_inc(x1_done, 1)

                    def add_bias(i, t=0):
                        wait(pool, x1_done, i + 1)
                        pool.tensor_tensor(xns[t][:, :], x1s[t][:, :], bias[:, :], ALU.add).then_inc(x1b_done, 1)

                    def y_lo(i, t=0):
                        wait(pool, yt_hi_done, i + 1)
                        pool.tensor_tensor(yt_los[t][:, :], ys[t][:, :], yt_his[t][:, :].bitcast(F32), ALU.subtract)\
                            .then_inc(yt_lo_done, 1)

                    def add_int4(i, t=0):
                        wait(pool, int4_scaled, i + 1)
                        wait(pool, x1b_done, i + 1)
                        to = acc[:, i, :] if isinstance(i, int) else \
                            acc[:, bass.ds(i, 1), :].rearrange("p o n -> p (o n)")
                        pool.tensor_tensor(to, ys[t][:, :], xns[t][:, :], ALU.add).then_inc(res_done, 1)

                    def last_pair(a, b):
                        add_x(a)
                        add_bias(a)
                        add_x(b, 1)
                        add_bias(b, 1)
                        y_lo(a)
                        add_int4(a)
                        y_lo(b, 1)
                        add_int4(b, 1)

                    def body(i0, gates):
                        for j in range(2):
                            add_x(i0 + j)
                            if gates and j == 1:
                                front(i0 + 5, 1)
                            add_bias(i0 + j)
                            y_lo(i0 + j)
                            add_int4(i0 + j)
                            if gates and j == 0:
                                front(i0 + 4, 0)

                    for j in range(2):
                        wait(pool, ct_hi_done, j + 1)
                        pool.tensor_tensor(ct_lo[j][:, :], first_ct[j], ct_hi[j][:, :].bitcast(F32), ALU.subtract)\
                            .then_inc(ct_lo_done, 1)
                    for k in range(NK):
                        if k not in WU_ON_DVE:
                            split_up(pool, k)
                    pool.wait_ge(unpacked, UNPACKED)
                    for j in range(2):
                        front(2 + j, j)
                    with pool.Fori(0, B // 2 - 2) as p:
                        body(pool.snap(p * 2), True)
                    body(B - 4, False)
                    last_pair(B - 2, B - 1)

                @block.vector
                def _(dve):
                    links = [0]

                    def link(instruction):
                        links[0] += 1
                        instruction.then_inc(unpacked, 1)
                        dve.wait_ge(unpacked, links[0])

                    def drop_lower_halves(i0, pair_no, early=False):
                        n = [0, 0]

                        def then(j, instruction):
                            n[j] += 1
                            instruction.then_inc(search[j], 1)

                        def after(j):
                            dve.wait_ge(search[j], pair_no * LINKS + (1 + n[j]))

                        def hold(j):
                            after(j)
                            dve.sem_inc(held_dve, 1)

                        def count_below(j, keys, threshold):
                            after(j)
                            then(j, dve.tensor_scalar(junk[j], keys[j], threshold[j][:, :], None, ALU.is_lt,
                                                      ALU.add, accum_out=count[j][:, :]))

                        def judge(j, below, bit):
                            after(j)
                            then(j, dve.tensor_scalar(taken[j][:, :], count[j][:, :], below[j], 2.0 ** bit,
                                                      ALU.is_lt, ALU.mult))

                        def try_next(j, bit, result):
                            after(j)
                            then(j, dve.scalar_tensor_tensor((tried if bit else result)[j][:, :], taken[j][:, :],
                                                             -(2.0 ** (bit - 1)) if bit else -1.0, tried[j][:, :],
                                                             ALU.add, ALU.add))

                        def descend(bits, keys, below, result, between={}):
                            for j in range(2):
                                after(j)
                                then(j, dve.memset(tried[j][:, :], 2.0 ** (bits - 1)))
                            for bit in range(bits - 1, -1, -1):
                                count_below(0, keys, tried)
                                if bit < bits - 1:
                                    try_next(1, bit + 1, result)
                                judge(0, below, bit)
                                if bit in between:
                                    between[bit]()
                                count_below(1, keys, tried)
                                try_next(0, bit, result)
                                judge(1, below, bit)
                            try_next(1, 0, result)

                        halves = [s[:, :].bitcast(U16).rearrange("p (n t) -> p n t", t=2) for s in s_sb]
                        for j in range(2):
                            if early and j == 1:
                                for k in WU_ON_DVE:
                                    split_up(dve, k)
                            dve.wait_ge(silu_done, i0 + (j + 1))
                            after(j)
                            if early:
                                dve.tensor_copy(first_lows[j], halves[j][:, :, 0])
                            then(j, dve.tensor_scalar(key[j], halves[j][:, :, 1], 0x7FFF, None, ALU.bitwise_and))
                        lows = first_lows if early else [h[:, :, 0] for h in halves]

                        def times_up(j):
                            after(j)
                            dve.wait_ge(abs_done, i0 + (j + 1))
                            dve.wait_ge(upped, i0 + (j + 1))
                            dve.tensor_tensor(s_sb[j][:, :], gu_ps[j][:, 0:FI], s_sb[j][:, :], ALU.mult)\
                                .then_inc(su_done, 1)

                        descend(15, key, [DROP - 0.5] * 2, high, {EARLY: lambda: [times_up(j) for j in range(2)]}
                                if early else {})
                        shares = [t.bitcast(BF16) for t in key2]
                        for j in range(2):
                            count_below(j, key, high)
                        for j in range(2):
                            after(j)
                            then(j, dve.tensor_scalar(shares[j], key[j], high[j][:, :], -1.0, ALU.is_equal, ALU.mult))
                        for j in range(2):
                            after(j)
                            then(j, dve.tensor_scalar(room[j][:, :], count[j][:, :], -1.0, DROP - 0.5,
                                                      ALU.mult, ALU.add))

                        def sort_keys(j):
                            after(j)
                            then(j, dve.scalar_tensor_tensor(sorting[j], lows[j], -65536.0, shares[j],
                                                             ALU.add, ALU.mult))

                        def set_edges():
                            for j in range(2):
                                after(j)
                                dve.tensor_copy(edge[j][:, 0:1], low[j][:, :])
                                dve.tensor_copy(edge[j][:, 1:2], high[j][:, :]).then_inc(edges_done, 1)

                        f = [0]

                        def flag(instruction):
                            f[0] += 1
                            instruction.then_inc(flags, 1)

                        def after_flag():
                            dve.wait_ge(flags, pair_no * FLAGS + (1 + f[0]))

                        def turn_flag():
                            after_flag()
                            flag(dve.transpose(many_turned[:, :], many[:, :]))

                        def gather_flag():
                            after_flag()
                            flag(dve.tensor_reduce(any_many[:, :], many_turned[:, :], mybir.AxisListType.X, ALU.max))

                        def flagged():
                            after_flag()
                            dve.sem_inc(held_dve, 1)
                            blocks = [dve.value_load(any_many[q:q + 1, 0:1], min_val=0, max_val=1)
                                      for q in range(0, P, 32)]
                            return blocks[0] + blocks[1] + blocks[2] + blocks[3]

                        after(0)
                        after(1)
                        after_flag()
                        flag(dve.tensor_scalar(many[:, 0:1], room[0][:, :], room[1][:, :], TOP - 1.0,
                                               ALU.max, ALU.is_gt))
                        sort_keys(0)
                        turn_flag()
                        sort_keys(1)
                        gather_flag()
                        if not early:
                            for j in range(2):
                                times_up(j)
                        start, f_start = list(n), f[0]
                        with dve.If(flagged() < 1):
                            for j in range(2):
                                hold(j)
                                then(j, dve.max(top[j][:, 0:8], sorting[j]))
                            for j in range(2):
                                hold(j)
                                then(j, dve.match_replace(sorting[j], top[j][:, 0:8], sorting[j], -1.0))
                            for j in range(2):
                                hold(j)
                                then(j, dve.max(top[j][:, 8:TOP], sorting[j]))
                            for j in range(2):
                                after(j)
                                then(j, dve.scalar_tensor_tensor(chosen[j][:, :], cst[:, C_RANK:C_KEY], room[j][:, :],
                                                                 top[j][:, :], ALU.is_equal, ALU.mult,
                                                                 accum_out=taken[j][:, :]))
                            for j in range(2):
                                after(j)
                                then(j, dve.tensor_scalar(low[j][:, :], taken[j][:, :], -1.0, 65536.0,
                                                          ALU.mult, ALU.add))
                            set_edges()
                            for result, compare in ((reach, ALU.is_ge), (count, ALU.is_gt)):
                                for j in range(2):
                                    after(j)
                                    then(j, dve.tensor_scalar(chosen[j][:, :], top[j][:, :], taken[j][:, :], None,
                                                              compare, ALU.add, accum_out=result[j][:, :]))
                            after(0)
                            flag(dve.tensor_tensor(tried[0][:, :], reach[0][:, :], room[0][:, :], ALU.subtract))
                            after(1)
                            after_flag()
                            flag(dve.scalar_tensor_tensor(tried[1][:, :], reach[1][:, :], room[1][:, :],
                                                          tried[0][:, :], ALU.subtract, ALU.max))
                            after_flag()
                            flag(dve.tensor_scalar(many[:, 0:1], tried[1][:, :], 1.0, None, ALU.is_gt))
                            for j in range(2):
                                assert n[j] == start[j] + SORT_LINKS
                                dve.sem_inc(search[j], DESCENT_LINKS - SORT_LINKS)
                        n[:], f[0] = start, f_start
                        with dve.Else():
                            for j in range(2):
                                after(j)
                                then(j, dve.tensor_scalar(sorting[j], sorting[j], 1.0, -1.0, ALU.max, ALU.mult))
                            for j in range(2):
                                after(j)
                                then(j, dve.tensor_scalar(key2[j], sorting[j], 65536.0, None, ALU.add))
                            descend(16, key2, [r[:, :] for r in room], low)
                            for j in range(2):
                                count_below(j, key2, low)
                            assert n == [m + DESCENT_LINKS for m in start]
                            set_edges()
                            flag(dve.memset(many[:, 0:1], 1.0))
                            f[0] += 2
                            dve.sem_inc(flags, 2)
                        for j in range(2):
                            after(j)
                            then(j, dve.scalar_tensor_tensor(room[j][:, :], count[j][:, :], -1.0, room[j][:, :],
                                                             ALU.mult, ALU.add))
                        turn_flag()
                        gather_flag()
                        assert f[0] == FLAGS
                        for j in range(2):
                            dve.wait_ge(sides_done, i0 + (j + 1))
                            dve.wait_ge(su_done, i0 + (j + 1))
                            after(j)
                            then(j, dve.scalar_tensor_tensor(m_sb[j][:, :], key[j].bitcast(BF16), 0.0, s_sb[j][:, :],
                                                             ALU.is_lt, ALU.mult))
                        start = list(n)
                        with dve.If(flagged() < 1):
                            for j in range(2):
                                after(j)
                                dve.sem_inc(h_done, 1)
                                dve.sem_inc(search[j], TIE_LINKS)
                        with dve.Else():
                            for j in range(2):
                                side, equal, rank, kept = (key[j].bitcast(BF16), junk[j].bitcast(BF16), key2[j],
                                                           junk[j].bitcast(BF16))
                                after(j)
                                then(j, dve.tensor_scalar(room[j][:, :], room[j][:, :], 1.0, None, ALU.add))
                                after(j)
                                then(j, dve.tensor_scalar(equal, side, 0.0, None, ALU.is_equal))
                                after(j)
                                then(j, dve.tensor_tensor_scan(rank, equal, equal, 0.0, ALU.add, ALU.bypass))
                                after(j)
                                then(j, dve.scalar_tensor_tensor(kept, rank, room[j][:, :], side,
                                                                 ALU.is_gt, ALU.subtract))
                                after(j)
                                dve.scalar_tensor_tensor(m_sb[j][:, :], kept, 0.0, s_sb[j][:, :], ALU.is_gt, ALU.mult)\
                                    .then_inc(h_done, 1)
                                assert n[j] == LINKS

                    dve.wait_ge(small_in, 4 * 16)
                    for parity in range(2):
                        shift4 = 0 if parity else 4
                        link(dve.tensor_scalar(nibble[:, :, :], pw_sb[:, :, :], shift4, 15, ALU.arith_shift_right,
                                               ALU.bitwise_and))
                        link(dve.tensor_scalar(wf[:, :, parity, :], nibble[:, :, :], -8.0, None, ALU.add))
                        link(dve.tensor_scalar(bias_i[:, :, parity], pb_sb[:, :], shift4, 15, ALU.arith_shift_right,
                                               ALU.bitwise_and))
                    link(dve.tensor_scalar(bias[:, :], bias_i[:, :, :].rearrange("p n t -> p (n t)"), -8.0,
                                           scl[:, 1:2], ALU.add, ALU.mult))
                    assert links[0] == UNPACKED
                    for j in range(2):
                        dve.memset(taken[j][:, :], 0.0).then_inc(search[j], 1)
                    dve.memset(many[:, :], 0.0).then_inc(flags, 1)
                    drop_lower_halves(0, 0, early=True)
                    with dve.Fori(0, B // 2 - 1) as p:
                        drop_lower_halves(dve.snap(p * 2 + 2), dve.snap(p + 1))


_INS = ["xt", "xn", "lens", "pages", "ids", "wqkv", "wo", "qw", "kw", "kc", "vc", "wg", "wu", "wd", "wa", "pw", "pb",
        "scales", "consts"]


def kernel(x, itok_Bx16_0_63, itok_B_207_1644, itok_B_1_14, L0_cond_Wq, L0_cond_Wk, L0_cond_Wv, L0_cond_Wo,
           L0_cond_q_norm_w, L0_cond_k_norm_w, L0_cond_k_cache, L0_cond_v_cache, L0_attn_w_gate, L0_attn_w_up,
           L0_attn_w_down, L0_cond2_weight, L0_ffn_packed_w, L0_ffn_packed_b, L0_ffn_scale_w, L0_ffn_scale_b):
    import numpy as np
    import concourse.bacc as bacc
    from concourse.bass_utils import run_bass_kernel_spmd

    x, pages, lens, ids = (np.asarray(a) for a in (x, itok_Bx16_0_63, itok_B_207_1644, itok_B_1_14))
    wq, wk, wv, wo = (np.asarray(a) for a in (L0_cond_Wq, L0_cond_Wk, L0_cond_Wv, L0_cond_Wo))
    by_head = [w.reshape(HK, -1, NK, P).transpose(0, 3, 2, 1) for w in (wq, wk, wv)]
    chunked = lambda w: np.asarray(w).T.reshape(NK, P, -1).transpose(1, 0, 2)
    consts = np.zeros((P, C_ALL), np.float32)
    consts[:, C_ID:C_ID + P] = np.eye(P)
    consts[:, C_INV:C_INV + D // 2] = 1.0 / 10000.0 ** (np.arange(0, D, 2) / D)
    consts[:, C_PART] = np.arange(P)
    consts[:, C_LANE] = np.arange(P) % PSIZE * HK
    consts[:, C_RANK:C_KEY] = np.arange(TOP) + 0.5
    consts[:, C_KEY:] = np.arange(L)
    arrays = dict(
        xt=x.reshape(B, S, NK, P).transpose(3, 0, 2, 1).reshape(P, -1),
        xn=x.reshape(B * S, DM),
        lens=np.broadcast_to(lens, (P, B)),
        pages=np.repeat(pages.reshape(B, NC, P // PSIZE).transpose(2, 0, 1).reshape(P // PSIZE, -1), PSIZE, axis=0),
        ids=ids.reshape(1, B),
        wqkv=np.concatenate(by_head, axis=3),
        wo=wo.reshape(DM, HK, REP, D).transpose(1, 3, 2, 0),
        qw=np.broadcast_to(np.asarray(L0_cond_q_norm_w), (P, D)),
        kw=np.broadcast_to(np.asarray(L0_cond_k_norm_w), (P, D)),
        kc=np.asarray(L0_cond_k_cache).reshape(-1, D),
        vc=np.asarray(L0_cond_v_cache).reshape(-1, D),
        wg=chunked(L0_attn_w_gate),
        wu=chunked(L0_attn_w_up),
        wd=np.asarray(L0_attn_w_down).T,
        wa=np.asarray(L0_cond2_weight).transpose(0, 2, 1).reshape(-1, NK, P, DM).transpose(0, 2, 1, 3),
        pw=np.asarray(L0_ffn_packed_w).reshape(DM, 2, P).transpose(2, 1, 0),
        pb=np.broadcast_to(np.asarray(L0_ffn_packed_b), (P, DM // 2)),
        scales=np.broadcast_to(np.stack([np.asarray(L0_ffn_scale_w), np.asarray(L0_ffn_scale_b)]), (P, 2)),
        consts=consts,
    )
    nc = bacc.Bacc("TRN2", target_bir_lowering=False, num_devices=1)
    arrays = {n: np.ascontiguousarray(arrays[n]) for n in _INS}
    args = [nc.dram_tensor(n, a.shape, mybir.dt.from_np(a.dtype), kind="ExternalInput").ap() for n, a in arrays.items()]
    out = nc.dram_tensor("out", (B * S, DM), F32, kind="ExternalOutput").ap()
    adaln_attn_ffn(nc, *args, out)
    r = run_bass_kernel_spmd(nc, [arrays], core_ids=[0])
    return r.results[0]["out"].reshape(B, S, DM)
```
